# Optimizing a Trainium2 kernel written in Bass

```python
import numpy as np
import jax
import jax.numpy as jnp

def _softmax(x, axis=-1):
    return jax.nn.softmax(x, axis=axis)

def _gelu(x):
    return jax.nn.gelu(x, approximate=True)

def _silu(x):
    return jax.nn.silu(x)

def _sigmoid(x):
    return jax.nn.sigmoid(x)

def _layernorm(x, axis=-1, eps=1e-05):
    m = jnp.mean(x, axis=axis, keepdims=True)
    v = jnp.var(x, axis=axis, keepdims=True)
    return (x - m) / jnp.sqrt(v + eps)

def _scatter_add(tgt, idx, src, axis=0):
    return tgt.at[idx].add(src)

def _segment_sum(src, seg, n):
    return jax.ops.segment_sum(src, seg, n)
kernel_name = 'mk_adaln_d2_jaxref_r8_f608cf'

def setup_inputs(seed: int=0):
    np.random.seed(seed)
    _w = jnp.asarray

    def _L0_attn_setup():
        import jax, jax.numpy as jnp
        import numpy as np
        B, N, D_MODEL, HEADS, DFF, M = (4, 512, 128, 16, 512, 32)
        DH = D_MODEL // HEADS
        EPS_K = 0.0001
        LN_EPS = 1e-05

        def softmax_kernel(x, proj, is_query):
            norm = x.shape[-1] ** (-0.25)
            ratio = proj.shape[0] ** (-0.5)
            xp = jnp.einsum('bhnd,md->bhnm', x * norm, proj)
            diag = jnp.sum(jnp.square(x), axis=-1, keepdims=True) * 0.5 * (norm * norm)
            if is_query:
                stab = jnp.max(xp, axis=-1, keepdims=True)
            else:
                stab = jnp.max(xp, axis=(-1, -2), keepdims=True)
            return ratio * (jnp.exp(xp - diag - stab) + EPS_K)

        def layer_norm(x, g, b):
            mu = jnp.mean(x, axis=-1, keepdims=True)
            var = jnp.mean(jnp.square(x - mu), axis=-1, keepdims=True)
            return (x - mu) * jax.lax.rsqrt(var + LN_EPS) * g + b
        key = jax.random.key(seed)
        ks = jax.random.split(key, 12)
        s = 0.02
        return {'video': jax.random.normal(ks[0], (B, N, D_MODEL), jnp.float32), 'Wq': jax.random.normal(ks[1], (D_MODEL, D_MODEL), jnp.float32) * s, 'bq': jnp.zeros((D_MODEL,), jnp.float32), 'Wk': jax.random.normal(ks[2], (D_MODEL, D_MODEL), jnp.float32) * s, 'bk': jnp.zeros((D_MODEL,), jnp.float32), 'Wv': jax.random.normal(ks[3], (D_MODEL, D_MODEL), jnp.float32) * s, 'bv': jnp.zeros((D_MODEL,), jnp.float32), 'Wo': jax.random.normal(ks[4], (D_MODEL, D_MODEL), jnp.float32) * s, 'bo': jnp.zeros((D_MODEL,), jnp.float32), 'proj': jax.random.normal(ks[5], (M, DH), jnp.float32), 'W1': jax.random.normal(ks[6], (DFF, D_MODEL), jnp.float32) * s, 'b1': jnp.zeros((DFF,), jnp.float32), 'W2': jax.random.normal(ks[7], (D_MODEL, DFF), jnp.float32) * s, 'b2': jnp.zeros((D_MODEL,), jnp.float32), 'g2': jnp.ones((D_MODEL,), jnp.float32), 'be2': jnp.zeros((D_MODEL,), jnp.float32), 'g3': jnp.ones((D_MODEL,), jnp.float32), 'be3': jnp.zeros((D_MODEL,), jnp.float32)}
    _L0_attn_in = _L0_attn_setup()

    def _L0_ffn_setup():
        import jax, jax.numpy as jnp
        import numpy as np
        B, S, D, F, E, R = (4, 256, 128, 512, 8, 4)
        key = jax.random.key(seed)
        ks = jax.random.split(key, 8)
        s_in = 1.0 / np.sqrt(D)
        s_ff = 1.0 / np.sqrt(F)
        return {'hidden_states': jax.random.normal(ks[0], (B, S, D), jnp.float32), 'gate_W': jax.random.normal(ks[1], (E, D), jnp.float32) * s_in, 'gate_b': jnp.zeros((E,), jnp.float32), 'wi_W': jax.random.normal(ks[2], (F, D), jnp.float32) * s_in, 'wi_b': jnp.zeros((F,), jnp.float32), 'wo_W': jax.random.normal(ks[3], (D, F), jnp.float32) * s_ff, 'wo_b': jnp.zeros((D,), jnp.float32), 'lora_A': jax.random.normal(ks[4], (E, R, D), jnp.float32) * s_in, 'lora_B': jax.random.normal(ks[5], (E, F, R), jnp.float32) * 0.02}
    _L0_ffn_in = _L0_ffn_setup()
    _L0_c = _w((lambda *s: np.random.randn(*s).astype(np.float32) * 0.05)(8, 128))
    _L0_wmod = _w((lambda *s: np.random.randn(*s).astype(np.float32) * 0.05)(128, 6 * 128) * 128 ** (-0.5))

    def _L1_attn_setup():
        import jax, jax.numpy as jnp
        import numpy as np
        B, L, DM, H, HD, K = (4, 256, 128, 16, 64, 64)
        BASE_LR = 1.0
        EPS = 1e-06

        def _ttt_forward(hidden_states, wq, wk, wv, wo, W1, b1, theta, theta_bias, alpha, gamma, beta):
            Bs, Ls, _ = hidden_states.shape
            n_chunks = Ls // K

            def proj(w):
                return (hidden_states @ w).reshape(Bs, Ls, H, HD).transpose(0, 2, 1, 3)
            xq, xk, xv = (proj(wq), proj(wk), proj(wv))

            def to_chunks(x):
                return x.reshape(Bs, H, n_chunks, K, HD).transpose(2, 0, 1, 3, 4)
            cq, ck, cv = (to_chunks(xq), to_chunks(xk), to_chunks(xv))
            token_eta = jnp.clip(1.0 / jnp.arange(1, K + 1, dtype=jnp.float32) + alpha, 0.0)[None, None, :, None]
            g = gamma[None]
            be = beta[None]
            tb = theta_bias.reshape(1, H, 1, 1)
            W0 = jnp.broadcast_to(W1[None], (Bs, H, HD, HD))
            b0 = jnp.broadcast_to(b1[None], (Bs, H, 1, HD))

            def step(carry, inp):
                W, bb = carry
                xq_c, xk_c, xv_c = inp
                lr = jax.nn.sigmoid(jnp.einsum('bhkc,hcd->bhkd', xk_c, theta) + tb)
                eta = token_eta * (BASE_LR * lr / HD)
                Z1 = xk_c @ W + bb
                mu = Z1.mean(-1, keepdims=True)
                std = jnp.sqrt(Z1.var(-1, keepdims=True) + EPS)
                x_hat = (Z1 - mu) / std
                y = g * x_hat + be
                grad_output = y - (xv_c - xk_c)
                gxh = grad_output * g
                grad_x = (HD * gxh - gxh.sum(-1, keepdims=True) - x_hat * (gxh * x_hat).sum(-1, keepdims=True)) / (HD * std)
                dW = jnp.einsum('bhkc,bhkd->bhcd', eta * xk_c, grad_x)
                db = (eta * grad_x).sum(-2, keepdims=True)
                Wn, bn = (W - dW, bb - db)
                Zq = xq_c @ Wn + bn
                mu2 = Zq.mean(-1, keepdims=True)
                std2 = jnp.sqrt(Zq.var(-1, keepdims=True) + EPS)
                out = xq_c + g * ((Zq - mu2) / std2) + be
                return ((Wn, bn), out)
            _, outs = jax.lax.scan(step, (W0, b0), (cq, ck, cv))
            out = outs.transpose(1, 2, 0, 3, 4).reshape(Bs, H, Ls, HD)
            out = out.transpose(0, 2, 1, 3).reshape(Bs, Ls, H * HD)
            return out @ wo
        key = jax.random.key(seed)
        ks = jax.random.split(key, 8)
        s = 0.02
        return {'hidden_states': jax.random.normal(ks[0], (B, L, DM), jnp.float32), 'wq': jax.random.normal(ks[1], (DM, H * HD), jnp.float32) * s, 'wk': jax.random.normal(ks[2], (DM, H * HD), jnp.float32) * s, 'wv': jax.random.normal(ks[3], (DM, H * HD), jnp.float32) * s, 'wo': jax.random.normal(ks[4], (H * HD, DM), jnp.float32) * s, 'W1': jax.random.normal(ks[5], (H, HD, HD), jnp.float32) * s, 'b1': jnp.zeros((H, 1, HD), jnp.float32), 'theta': jax.random.normal(ks[6], (H, HD, 1), jnp.float32) * s, 'theta_bias': jnp.zeros((H, 1, 1), jnp.float32), 'alpha': jnp.zeros((K,), jnp.float32), 'gamma': jnp.ones((H, 1, HD), jnp.float32), 'beta': jnp.zeros((H, 1, HD), jnp.float32)}
    _L1_attn_in = _L1_attn_setup()

    def _L1_ffn_setup():
        import jax, jax.numpy as jnp
        import numpy as np
        DIM = 128

        def _reference_tuple_inner(x, W_r, W_k, W_v, mu_r, mu_k):
            B, T, C = x.shape
            x_prev = jnp.concatenate([jnp.zeros((B, 1, C), x.dtype), x[:, :-1, :]], axis=1)
            xr = mu_r * x + (1.0 - mu_r) * x_prev
            xk = mu_k * x + (1.0 - mu_k) * x_prev
            r = jax.nn.sigmoid(jnp.einsum('btc,dc->btd', xr, W_r))
            k = jnp.einsum('btc,dc->btd', xk, W_k)
            k_act = jnp.square(jax.nn.relu(k))
            out = r * jnp.einsum('btc,dc->btd', k_act, W_v)
            new_state = x[:, -1, :]
            return (out, new_state)
        key = jax.random.key(seed)
        ks = jax.random.split(key, 6)
        B, T, C = (8, 256, DIM)
        x = jax.random.normal(ks[0], (B, T, C), dtype=jnp.float32)
        s = 1.0 / np.sqrt(C)
        W_r = jax.random.uniform(ks[1], (C, C), jnp.float32, -s, s)
        W_k = jax.random.uniform(ks[2], (C, C), jnp.float32, -s, s)
        W_v = jax.random.uniform(ks[3], (C, C), jnp.float32, -s, s)
        mu_r = jax.random.uniform(ks[4], (C,), jnp.float32)
        mu_k = jax.random.uniform(ks[5], (C,), jnp.float32)
        return {'x': x, 'W_r': W_r, 'W_k': W_k, 'W_v': W_v, 'mu_r': mu_r, 'mu_k': mu_k}
    _L1_ffn_in = _L1_ffn_setup()
    _L1_c = _w((lambda *s: np.random.randn(*s).astype(np.float32) * 0.05)(8, 128))
    _L1_wmod = _w((lambda *s: np.random.randn(*s).astype(np.float32) * 0.05)(128, 6 * 128) * 128 ** (-0.5))
    _d = {'L0_attn_video': _L0_attn_in['video'], 'L0_attn_Wq': _L0_attn_in['Wq'], 'L0_attn_bq': _L0_attn_in['bq'], 'L0_attn_Wk': _L0_attn_in['Wk'], 'L0_attn_bk': _L0_attn_in['bk'], 'L0_attn_Wv': _L0_attn_in['Wv'], 'L0_attn_bv': _L0_attn_in['bv'], 'L0_attn_Wo': _L0_attn_in['Wo'], 'L0_attn_bo': _L0_attn_in['bo'], 'L0_attn_proj': _L0_attn_in['proj'], 'L0_attn_W1': _L0_attn_in['W1'], 'L0_attn_b1': _L0_attn_in['b1'], 'L0_attn_W2': _L0_attn_in['W2'], 'L0_attn_b2': _L0_attn_in['b2'], 'L0_attn_g2': _L0_attn_in['g2'], 'L0_attn_be2': _L0_attn_in['be2'], 'L0_attn_g3': _L0_attn_in['g3'], 'L0_attn_be3': _L0_attn_in['be3'], 'L0_ffn_gate_W': _L0_ffn_in['gate_W'], 'L0_ffn_gate_b': _L0_ffn_in['gate_b'], 'L0_ffn_wi_W': _L0_ffn_in['wi_W'], 'L0_ffn_wi_b': _L0_ffn_in['wi_b'], 'L0_ffn_wo_W': _L0_ffn_in['wo_W'], 'L0_ffn_wo_b': _L0_ffn_in['wo_b'], 'L0_ffn_lora_A': _L0_ffn_in['lora_A'], 'L0_ffn_lora_B': _L0_ffn_in['lora_B'], 'L0_c': _L0_c, 'L0_wmod': _L0_wmod, 'L1_attn_wq': _L1_attn_in['wq'], 'L1_attn_wk': _L1_attn_in['wk'], 'L1_attn_wv': _L1_attn_in['wv'], 'L1_attn_wo': _L1_attn_in['wo'], 'L1_attn_W1': _L1_attn_in['W1'], 'L1_attn_b1': _L1_attn_in['b1'], 'L1_attn_theta': _L1_attn_in['theta'], 'L1_attn_theta_bias': _L1_attn_in['theta_bias'], 'L1_attn_alpha': _L1_attn_in['alpha'], 'L1_attn_gamma': _L1_attn_in['gamma'], 'L1_attn_beta': _L1_attn_in['beta'], 'L1_ffn_W_r': _L1_ffn_in['W_r'], 'L1_ffn_W_k': _L1_ffn_in['W_k'], 'L1_ffn_W_v': _L1_ffn_in['W_v'], 'L1_ffn_mu_r': _L1_ffn_in['mu_r'], 'L1_ffn_mu_k': _L1_ffn_in['mu_k'], 'L1_c': _L1_c, 'L1_wmod': _L1_wmod}
    _x0 = _d['L0_attn_video']
    _d['L0_attn_video'] = jax.random.normal(jax.random.fold_in(jax.random.key(seed), 1), (8, 512, 128), dtype=_x0.dtype)
    del _x0
    return _d

def reference(L0_attn_video, L0_attn_Wq, L0_attn_bq, L0_attn_Wk, L0_attn_bk, L0_attn_Wv, L0_attn_bv, L0_attn_Wo, L0_attn_bo, L0_attn_proj, L0_attn_W1, L0_attn_b1, L0_attn_W2, L0_attn_b2, L0_attn_g2, L0_attn_be2, L0_attn_g3, L0_attn_be3, L0_ffn_gate_W, L0_ffn_gate_b, L0_ffn_wi_W, L0_ffn_wi_b, L0_ffn_wo_W, L0_ffn_wo_b, L0_ffn_lora_A, L0_ffn_lora_B, L0_c, L0_wmod, L1_attn_wq, L1_attn_wk, L1_attn_wv, L1_attn_wo, L1_attn_W1, L1_attn_b1, L1_attn_theta, L1_attn_theta_bias, L1_attn_alpha, L1_attn_gamma, L1_attn_beta, L1_ffn_W_r, L1_ffn_W_k, L1_ffn_W_v, L1_ffn_mu_r, L1_ffn_mu_k, L1_c, L1_wmod):

    def _L0_attn_ref(video, Wq, bq, Wk, bk, Wv, bv, Wo, bo, proj, W1, b1, W2, b2, g2, be2, g3, be3):
        import jax, jax.numpy as jnp
        import numpy as np
        B, N, D_MODEL, HEADS, DFF, M = (4, 512, 128, 16, 512, 32)
        DH = D_MODEL // HEADS
        EPS_K = 0.0001
        LN_EPS = 1e-05

        def softmax_kernel(x, proj, is_query):
            norm = x.shape[-1] ** (-0.25)
            ratio = proj.shape[0] ** (-0.5)
            xp = jnp.einsum('bhnd,md->bhnm', x * norm, proj)
            diag = jnp.sum(jnp.square(x), axis=-1, keepdims=True) * 0.5 * (norm * norm)
            if is_query:
                stab = jnp.max(xp, axis=-1, keepdims=True)
            else:
                stab = jnp.max(xp, axis=(-1, -2), keepdims=True)
            return ratio * (jnp.exp(xp - diag - stab) + EPS_K)

        def layer_norm(x, g, b):
            mu = jnp.mean(x, axis=-1, keepdims=True)
            var = jnp.mean(jnp.square(x - mu), axis=-1, keepdims=True)
            return (x - mu) * jax.lax.rsqrt(var + LN_EPS) * g + b
        b, n, d = video.shape
        split = lambda t: t.reshape(b, n, HEADS, DH).transpose(0, 2, 1, 3)
        q = split(video @ Wq.T + bq)
        k = split(video @ Wk.T + bk)
        v = split(video @ Wv.T + bv)
        qp = softmax_kernel(q, proj, is_query=True)
        kp = softmax_kernel(k, proj, is_query=False)
        k_sum = jnp.sum(kp, axis=2)
        denom = jnp.einsum('bhnm,bhm->bhn', qp, k_sum)
        ctx = jnp.einsum('bhnm,bhnd->bhmd', kp, v)
        out = jnp.einsum('bhnm,bhmd->bhnd', qp, ctx) / denom[..., None]
        attn = out.transpose(0, 2, 1, 3).reshape(b, n, d) @ Wo.T + bo
        x = layer_norm(video + attn, g2, be2)
        ff = jax.nn.relu(x @ W1.T + b1) @ W2.T + b2
        return layer_norm(x + ff, g3, be3)

    def _L0_ffn_ref(hidden_states, gate_W, gate_b, wi_W, wi_b, wo_W, wo_b, lora_A, lora_B):
        import jax, jax.numpy as jnp
        import numpy as np
        B, S, D, F, E, R = (4, 256, 128, 512, 8, 4)
        x = hidden_states
        logits = jnp.einsum('bsd,ed->bse', x, gate_W) + gate_b
        top1 = jnp.argmax(jax.nn.softmax(logits, axis=-1), axis=-1)
        base = jnp.einsum('bsd,fd->bsf', x, wi_W) + wi_b
        out = jnp.zeros_like(x)
        for i in range(lora_A.shape[0]):
            lora = jnp.einsum('bsr,fr->bsf', jnp.einsum('bsd,rd->bsr', x, lora_A[i]), lora_B[i])
            inter = jax.nn.relu(base + lora)
            expert_out = jnp.einsum('bsf,df->bsd', inter, wo_W) + wo_b
            mask = (top1 == i).astype(x.dtype)[..., None]
            out = out + mask * expert_out
        return out

    def _L1_attn_ref(hidden_states, wq, wk, wv, wo, W1, b1, theta, theta_bias, alpha, gamma, beta):
        import jax, jax.numpy as jnp
        import numpy as np
        B, L, DM, H, HD, K = (4, 256, 128, 16, 64, 64)
        BASE_LR = 1.0
        EPS = 1e-06

        def _ttt_forward(hidden_states, wq, wk, wv, wo, W1, b1, theta, theta_bias, alpha, gamma, beta):
            Bs, Ls, _ = hidden_states.shape
            n_chunks = Ls // K

            def proj(w):
                return (hidden_states @ w).reshape(Bs, Ls, H, HD).transpose(0, 2, 1, 3)
            xq, xk, xv = (proj(wq), proj(wk), proj(wv))

            def to_chunks(x):
                return x.reshape(Bs, H, n_chunks, K, HD).transpose(2, 0, 1, 3, 4)
            cq, ck, cv = (to_chunks(xq), to_chunks(xk), to_chunks(xv))
            token_eta = jnp.clip(1.0 / jnp.arange(1, K + 1, dtype=jnp.float32) + alpha, 0.0)[None, None, :, None]
            g = gamma[None]
            be = beta[None]
            tb = theta_bias.reshape(1, H, 1, 1)
            W0 = jnp.broadcast_to(W1[None], (Bs, H, HD, HD))
            b0 = jnp.broadcast_to(b1[None], (Bs, H, 1, HD))

            def step(carry, inp):
                W, bb = carry
                xq_c, xk_c, xv_c = inp
                lr = jax.nn.sigmoid(jnp.einsum('bhkc,hcd->bhkd', xk_c, theta) + tb)
                eta = token_eta * (BASE_LR * lr / HD)
                Z1 = xk_c @ W + bb
                mu = Z1.mean(-1, keepdims=True)
                std = jnp.sqrt(Z1.var(-1, keepdims=True) + EPS)
                x_hat = (Z1 - mu) / std
                y = g * x_hat + be
                grad_output = y - (xv_c - xk_c)
                gxh = grad_output * g
                grad_x = (HD * gxh - gxh.sum(-1, keepdims=True) - x_hat * (gxh * x_hat).sum(-1, keepdims=True)) / (HD * std)
                dW = jnp.einsum('bhkc,bhkd->bhcd', eta * xk_c, grad_x)
                db = (eta * grad_x).sum(-2, keepdims=True)
                Wn, bn = (W - dW, bb - db)
                Zq = xq_c @ Wn + bn
                mu2 = Zq.mean(-1, keepdims=True)
                std2 = jnp.sqrt(Zq.var(-1, keepdims=True) + EPS)
                out = xq_c + g * ((Zq - mu2) / std2) + be
                return ((Wn, bn), out)
            _, outs = jax.lax.scan(step, (W0, b0), (cq, ck, cv))
            out = outs.transpose(1, 2, 0, 3, 4).reshape(Bs, H, Ls, HD)
            out = out.transpose(0, 2, 1, 3).reshape(Bs, Ls, H * HD)
            return out @ wo
        return _ttt_forward(hidden_states, wq, wk, wv, wo, W1, b1, theta, theta_bias, alpha, gamma, beta)

    def _L1_ffn_ref(x, W_r, W_k, W_v, mu_r, mu_k):
        import jax, jax.numpy as jnp
        import numpy as np
        DIM = 128

        def _reference_tuple_inner(x, W_r, W_k, W_v, mu_r, mu_k):
            B, T, C = x.shape
            x_prev = jnp.concatenate([jnp.zeros((B, 1, C), x.dtype), x[:, :-1, :]], axis=1)
            xr = mu_r * x + (1.0 - mu_r) * x_prev
            xk = mu_k * x + (1.0 - mu_k) * x_prev
            r = jax.nn.sigmoid(jnp.einsum('btc,dc->btd', xr, W_r))
            k = jnp.einsum('btc,dc->btd', xk, W_k)
            k_act = jnp.square(jax.nn.relu(k))
            out = r * jnp.einsum('btc,dc->btd', k_act, W_v)
            new_state = x[:, -1, :]
            return (out, new_state)
        return _reference_tuple_inner(x, W_r, W_k, W_v, mu_r, mu_k)[0]
    x = L0_attn_video
    mod = (_silu(L0_c) @ L0_wmod).reshape(L0_c.shape[0], 6, 1, -1)
    sa, ca, ga, sb, cb, gb = (mod[:, 0], mod[:, 1], mod[:, 2], mod[:, 3], mod[:, 4], mod[:, 5])
    ga = (2 * (ga >= 0) - 1) * jnp.maximum(jnp.abs(ga), 0.25)
    gb = (2 * (gb >= 0) - 1) * jnp.maximum(jnp.abs(gb), 0.25)
    h = _layernorm(x, axis=-1) * (1 + ca) + sa
    x = x + ga * _L0_attn_ref(h, L0_attn_Wq, L0_attn_bq, L0_attn_Wk, L0_attn_bk, L0_attn_Wv, L0_attn_bv, L0_attn_Wo, L0_attn_bo, L0_attn_proj, L0_attn_W1, L0_attn_b1, L0_attn_W2, L0_attn_b2, L0_attn_g2, L0_attn_be2, L0_attn_g3, L0_attn_be3)
    h = _layernorm(x, axis=-1) * (1 + cb) + sb
    x = x + gb * _L0_ffn_ref(h, L0_ffn_gate_W, L0_ffn_gate_b, L0_ffn_wi_W, L0_ffn_wi_b, L0_ffn_wo_W, L0_ffn_wo_b, L0_ffn_lora_A, L0_ffn_lora_B)
    mod = (_silu(L1_c) @ L1_wmod).reshape(L1_c.shape[0], 6, 1, -1)
    sa, ca, ga, sb, cb, gb = (mod[:, 0], mod[:, 1], mod[:, 2], mod[:, 3], mod[:, 4], mod[:, 5])
    ga = (2 * (ga >= 0) - 1) * jnp.maximum(jnp.abs(ga), 0.25)
    gb = (2 * (gb >= 0) - 1) * jnp.maximum(jnp.abs(gb), 0.25)
    h = _layernorm(x, axis=-1) * (1 + ca) + sa
    x = x + ga * _L1_attn_ref(h, L1_attn_wq, L1_attn_wk, L1_attn_wv, L1_attn_wo, L1_attn_W1, L1_attn_b1, L1_attn_theta, L1_attn_theta_bias, L1_attn_alpha, L1_attn_gamma, L1_attn_beta)
    h = _layernorm(x, axis=-1) * (1 + cb) + sb
    x = x + gb * _L1_ffn_ref(h, L1_ffn_W_r, L1_ffn_W_k, L1_ffn_W_v, L1_ffn_mu_r, L1_ffn_mu_k)
    return x

_drawn_inputs = setup_inputs


def setup_inputs(seed=0):
    import zlib

    import numpy as np

    out = dict(_drawn_inputs(seed))
    spreads = {'L0_attn_bq': (0.0, 2.0),
     'L0_attn_bk': (0.0, 2.0),
     'L0_attn_bv': (0.0, 0.8),
     'L0_attn_bo': (0.0, 0.327),
     'L0_attn_b1': (0.0, 0.8),
     'L0_attn_b2': (0.0, 0.307),
     'L0_attn_g2': (1.0, 0.2),
     'L0_attn_be2': (0.0, 0.335),
     'L0_attn_g3': (1.0, 0.2),
     'L0_attn_be3': (0.0, 0.343),
     'L0_ffn_gate_b': (0.0, 0.8),
     'L0_ffn_wi_b': (0.0, 0.494),
     'L0_ffn_wo_b': (0.0, 0.374),
     'L1_attn_b1': (0.0, 0.1),
     'L1_attn_theta_bias': (0.0, 2.0),
     'L1_attn_alpha': (0.0, 0.386),
     'L1_attn_gamma': (1.0, 0.2),
     'L1_attn_beta': (0.0, 0.315)}
    factors = {'L0_attn_Wq': 200.0,
     'L0_attn_Wk': 64.0,
     'L0_attn_Wv': 8.0,
     'L0_attn_Wo': 8.0,
     'L0_attn_proj': 200.0,
     'L0_attn_W1': 3.728,
     'L0_attn_W2': 2.831,
     'L0_ffn_gate_W': 8.0,
     'L0_ffn_lora_A': 8.0,
     'L0_ffn_lora_B': 8.0,
     'L1_attn_wv': 3.074,
     'L1_attn_theta': 64.0,
     'L1_ffn_W_r': 8.0,
     'L1_ffn_W_k': 3.102,
     'L1_ffn_W_v': 2.878,
     'L1_ffn_mu_r': 8.0,
     'L1_ffn_mu_k': 4.906}
    for name, (base, spread) in spreads.items():
        noise = np.random.default_rng([zlib.crc32(name.encode()), seed]).standard_normal(out[name].shape)
        drawn = base * np.exp(spread * noise) if base else spread * noise
        out[name] = jnp.asarray(drawn.astype(out[name].dtype))
    for name, factor in factors.items():
        out[name] = (out[name] * factor).astype(out[name].dtype)
    return out
```

```python
from contextlib import ExitStack

import numpy as np

import concourse.bass as bass
from concourse import mybir

F32 = mybir.dt.float32
ALU = mybir.AluOpType
ACT = mybir.ActivationFunctionType
AX = mybir.AxisListType.X

B, N, D = 8, 512, 128
PAIRS = B // 2
TRIPS = PAIRS
T = N // 128
H0, DH, M = 16, 8, 32
FEAT = H0 * M
G = FEAT // 128
HG = H0 // G
FF = 512
NF = FF // 128
E, R = 8, 4
H, HD, K = 16, 64, 64
NJ = N // K
HW = H * HD
HP = H // 2
HH = H // 2
HALF = HH * HD
C = HD + 1
EPS_K, LN_EPS, TTT_EPS = 1e-4, 1e-5, 1e-6
NORM = DH ** -0.25


def shape_constants():
    ident = np.eye(128, dtype=np.float32)
    head_of_dim = np.arange(D) // DH
    head_of_feat = np.arange(FEAT) // M
    same = (head_of_dim[:, None] == head_of_feat[None, :]).astype(np.float32)
    proj_mask = same * np.float32(NORM)
    ctx_mask = same.T.reshape(G, 128, D).transpose(1, 0, 2).reshape(128, G * D)
    head_sel = (head_of_feat[:, None] == np.arange(H0)[None, :]).astype(np.float32)
    head_sel = head_sel.reshape(G, 128, H0).transpose(1, 0, 2).reshape(128, G * H0)
    neg_sel = np.zeros((128, FEAT), np.float32)
    neg_sel[:H0] = -(np.arange(H0)[:, None] == head_of_feat[None, :]).astype(np.float32)
    half_square = (head_of_dim[:, None] == np.arange(H0)[None, :]).astype(np.float32) * np.float32(0.5 * NORM * NORM)
    first = np.tile(np.arange(E, 0, -1, dtype=np.float32)[None, :], (128, 1))
    token_rate = np.tile(1.0 / np.arange(1, K + 1, dtype=np.float32), 2)[:, None].astype(np.float32)
    return {
        "c_ident": ident, "c_proj_mask": proj_mask, "c_ctx_mask": ctx_mask, "c_head_sel": head_sel,
        "c_neg_sel": neg_sel, "c_half_square": half_square, "c_first": first, "c_token_rate": token_rate,
    }


PER_BATCH = [f"ln{n}_{what}" for n in range(1, 6) for what in ("var", "std", "hat")]
PER_BATCH += ["k_tile_max", "k_max_ready", "k_stab_ready", "k_shifted", "k_exp", "k_feat_ready", "q_feat_ready", "x_layer0", "x_loaded"]
PER_PAIR = [
    "x_moved", "out_stored", "mods_ready", "dve_step", "pool_step", "rate_logit", "rate_sig",
    "w_ready", "z_squared", "z_var", "z_std", "scale_ready", "g_hat", "grad_base", "grad_top", "grad_bot", "k_scaled", "dw_done",
    "zq_squared", "zq_var", "zq_std", "ln6_var", "ln6_std", "ln6_hat", "mix_ready", "key_ready", "x_final",
]


def build(nc, a, out):
    with ExitStack() as ctx:
        def sb(name, shape):
            return ctx.enter_context(nc.sbuf_tensor(name, shape, F32))

        def new_sem(name):
            return ctx.enter_context(nc.semaphore(name))

        ps = ctx.enter_context(nc.psum_tensor("ps", [128, 8, 512], F32))
        bank = [ps[:, i, :] for i in range(8)]

        ident = sb("ident", [128, 128])
        proj_bd = sb("proj_bd", [128, FEAT])
        ctx_mask = sb("ctx_mask", [128, G, D])
        head_sel = sb("head_sel", [128, G, H0])
        neg_sel = sb("neg_sel", [128, FEAT])
        half_square = sb("half_square", [128, H0])
        first = sb("first", [128, E])
        ones = sb("ones", [128, 128])
        w_q0, w_k0, w_v0, w_o0 = (sb(n, [128, D]) for n in ("w_q0", "w_k0", "w_v0", "w_o0"))
        b_q0, b_k0, g2, be2 = (sb(n, [128, 1]) for n in ("b_q0", "b_k0", "g2", "be2"))
        bc_v0, bc_o0, bc_b2, bc_g3, bc_be3, bc_wo = (sb(n, [128, D]) for n in ("bc_v0", "bc_o0", "bc_b2", "bc_g3", "bc_be3", "bc_wo"))
        w_1 = sb("w_1", [128, FF])
        b_1 = sb("b_1", [128, NF])
        w_2 = sb("w_2", [128, NF, D])
        w_ga = sb("w_ga", [128, E + E * R])
        bc_gate = sb("bc_gate", [128, E])
        w_i = sb("w_i", [128, FF])
        b_i = sb("b_i", [128, NF])
        w_of = sb("w_of", [128, NF, D])
        lora_b = sb("lora_b", [128, FF])
        w_q1 = sb("w_q1", [128, HW])
        w_k1 = sb("w_k1", [128, HW])
        w_t1 = sb("w_t1", [128, HW])
        g_wo = sb("g_wo", [128, HP, D])
        w_qo = sb("w_qo", [128, D])
        bc_out1 = sb("bc_out1", [128, D])
        w_theta = sb("w_theta", [128, H])
        bc_tb = sb("bc_tb", [128, H])
        rate = sb("rate", [128, 1])
        gamma2 = sb("gamma2", [128, HW])
        gam_bet = sb("gam_bet", [128, HW])
        w_init = sb("w_init", [C, H, 2, HD])
        w_r, w_kf, w_vf = (sb(n, [128, D]) for n in ("w_r", "w_kf", "w_vf"))
        mu_r, mu_k = sb("mu_r", [128, 1]), sb("mu_k", [128, 1])
        mod_all = sb("mod_all", [128, 8, B])
        gate0 = sb("gate0", [128, B, 2, D])
        gate1 = sb("gate1", [128, PAIRS, 2, D])
        mod = sb("mod", [128, 8, 2])
        g_ab0 = sb("g_ab0", [128, 2, 2, D])
        g_ab1 = sb("g_ab1", [128, 2, D])
        gg3 = sb("gg3", [128, 2, 2, D])

        x = sb("x", [128, 2, T, D])
        L = []
        for u in range(2):
            tiles = sb(f"tiles{u}", [128, 6, N])
            rows_ = sb(f"feats{u}", [128, 8, 512])
            L.append(dict(
                tiles=tiles, feats=rows_,
                stats=sb(f"stats{u}", [128, T, 6]), mv=sb(f"mv{u}", [128, T, 2]), std=sb(f"std{u}", [128, T]),
                inv=sb(f"inv{u}", [128, T]), hat=tiles[:, 0, :].rearrange("p (t d) -> p t d", t=T), hT=tiles[:, 1, :],
                qT=tiles[:, 2, :], q2=tiles[:, 3, :], kT=tiles[:, 4, :], k2=tiles[:, 5, :],
                v=sb(f"v{u}", [128, T, D + 1]), qmax=sb(f"qmax{u}", [128, T, H0]), qb=sb(f"qb{u}", [128, N]),
                big=rows_[:, 0:4, :], ek=rows_[:, 4:8, :], kmax=sb(f"kmax{u}", [128, T, H0]),
                kmx=sb(f"kmx{u}", [128, H0]), stab=sb(f"stab{u}", [H0, 1]), sd=sb(f"sd{u}", [H0, H0]),
                ctx=sb(f"ctx{u}", [128, G, D + H0]), rden=sb(f"rden{u}", [128, T, H0]), y=sb(f"y{u}", [128, T, D]),
                lg=sb(f"lg{u}", [128, T, E]), lm=sb(f"lm{u}", [128, T]), eq=sb(f"eq{u}", [128, T, E]),
                um=sb(f"um{u}", [128, T, E * R]), umT=sb(f"umT{u}", [128, N]),
            ))

        xc = sb("xc", [128, NJ, D])
        h3 = sb("h3", [128, NJ, 2, K])
        w_sb = sb("w_sb", [C, H, 2, HD])
        kT1 = sb("keys1", [C, H, 2 * K])
        qT1 = sb("queries1", [C, H, 2 * K])
        k_tok = L[0]["tiles"][:, 1:3, :].rearrange("p a b -> p (a b)")
        k_sc = sb("k_sc", [128, H, C])
        t_tok = L[0]["feats"][:, 0:4, :].rearrange("p (s a) b -> p s (a b)", s=2)
        eta = sb("eta", [128, NJ, H])
        sq = L[0]["feats"][:, 4:6, :].rearrange("p a b -> p (a b)")
        ssum, zstd, zinv, scl = (sb(n, [128, H]) for n in ("ssum", "zstd", "zinv", "scl"))
        zhat = L[0]["feats"][:, 6:8, :].rearrange("p a b -> p (a b)")
        gbase = L[1]["feats"][:, 4:6, :].rearrange("p a b -> p (a b)")
        tmp = L[1]["feats"][:, 6:8, :].rearrange("p a b -> p (a b)")
        c12 = sb("c12", [128, 2, 2, HH])
        grad = sb("grad", [128, H, 2, HD])
        qsum, qstd, qinv = (sb(n, [128, H]) for n in ("qsum", "qstd", "qinv"))
        zT = L[1]["tiles"][:, 1:3, :].rearrange("p a (g t) -> p (a g) t", t=128)
        att1 = sb("att1", [128, D])
        stats6, mv6 = sb("stats6", [128, NJ, 6]), sb("mv6", [128, NJ, 2])
        std6, inv6 = sb("std6", [128, NJ]), sb("inv6", [128, NJ])
        hat6 = sq[:, :].rearrange("p (j d) -> p j d", j=NJ)
        h4 = zhat[:, :].rearrange("p (j b t) -> p j b t", j=NJ, b=2)
        diff = gbase[:, :].rearrange("p (j b t) -> p j b t", j=NJ, b=2)
        mix_r, mix_k, kact = tmp[:, :], k_tok[:, :], t_tok[:, 0, :]
        r_sb = t_tok[:, 1, :]
        zq_hat = L[1]["feats"][:, 0:2, :].rearrange("p a b -> p (a b)")
        sqq = L[1]["feats"][:, 2:4, :].rearrange("p a b -> p (a b)")
        s_wv = L[0]["big"][:, 0:2, :].rearrange("p a b -> p (a b)")
        s_gam = L[0]["big"][:, 2:4, :].rearrange("p a b -> p (a b)")
        s_bet = L[1]["big"][:, 0:2, :].rearrange("p a b -> p (a b)")
        s_the = L[1]["big"][:, 2:4, :].rearrange("p a b -> p (a b)")
        s_wqT = L[0]["ek"][:, 0:2, :].rearrange("p a b -> p (a b)").rearrange("p (g d) -> p g d", g=HP)
        s_wo = L[0]["ek"][:, 2:4, :].rearrange("p a b -> p (a b)").rearrange("p (g d) -> p g d", g=HP)
        s_bb = L[1]["ek"][:, 0:2, :].rearrange("p a b -> p (a b)").rearrange("p (g d) -> p g d", g=HP)
        s_w0 = L[1]["ek"][0:C, 2:4, :].rearrange("p a b -> p (a b)").rearrange("p (h d) -> p h d", h=H)
        wmod = [L[u]["tiles"][:, 0:3, :].rearrange("p a b -> p (a b)")[:, 0:6 * D] for u in range(2)]
        s_cT = sb("s_cT", [128, 2, B])
        s_sig = sb("s_sig", [128, 2, B])
        s_cb = L[0]["tiles"][:, 3:6, :].rearrange("p a b -> p (a b)")
        s_small = sb("s_small", [128, 48])

        names = [f"{n}_{u}" for n in PER_BATCH for u in range(2)] + PER_PAIR
        names += [f"filled_{i}" for i in range(8)] + [f"drained_{i}" for i in range(8)] + ["engines_done"]
        S = {n: new_sem(n) for n in names}
        numbers = [s.num for s in S.values()]
        assert numbers == list(range(numbers[0], numbers[0] + len(numbers)))
        go = {e: new_sem(f"go_{e}") for e in ("pe", "act", "dve", "sp")}
        weights_loaded = new_sem("weights_loaded")
        pool_set, dve_set, act_set, pe_set = (new_sem(n) for n in ("pool_set", "dve_set", "act_set", "pe_set"))
        set_step = new_sem("set_step")

        loads = [
            (ident[:, :], a["c_ident"]), (proj_bd[:, :], a["proj_tiled"]), (s_cb[:, 0:FEAT], a["c_proj_mask"]),
            (ctx_mask[:, :, :].rearrange("p g d -> p (g d)"), a["c_ctx_mask"]),
            (head_sel[:, :, :].rearrange("p g d -> p (g d)"), a["c_head_sel"]),
            (neg_sel[:, :], a["c_neg_sel"]), (half_square[:, :], a["c_half_square"]), (first[:, :], a["c_first"]),
            (s_small[:, 0:1], a["c_token_rate"]), (s_small[:, 1:2], a["alpha2"]),
            (w_q0[:, :], a["WqT"]), (w_k0[:, :], a["WkT"]), (w_v0[:, :], a["WvT"]), (w_o0[:, :], a["WoT"]),
            (b_q0[:, :], a["bq"]), (b_k0[:, :], a["bk"]), (g2[:, :], a["g2"]), (be2[:, :], a["be2"]),
            (w_1[:, :], a["W1T"]), (b_1[:, :], a["b1"]), (w_2[:, :, :], a["W2T"].rearrange("(g p) d -> p g d", p=128)),
            (w_ga[:, :], a["gate_lora_a"]), (w_i[:, :], a["wiT"]), (b_i[:, :], a["wi_b"]),
            (w_of[:, :, :], a["woT"].rearrange("(g p) d -> p g d", p=128)), (lora_b[:, :], a["lora_b"]),
            (w_q1[:, :], a["wq1"]), (w_k1[:, :], a["wk1"]), (s_wv, a["wv1"]),
            (s_wqT, a["wq1T"].rearrange("(g p) d -> p g d", p=128)), (s_wo, a["wo1"].rearrange("(g p) d -> p g d", p=128)),
            (s_w0[0:HD, :, :], a["W1c"]), (s_w0[HD:C, :, :], a["b1c"]),
            (s_small[:, 2:2 + HP], a["betaT"]), (s_small[:, 16:16 + HP], a["gammaT"]),
            (w_r[:, :], a["W_rT"]), (w_kf[:, :], a["W_kT"]), (w_vf[:, :], a["W_vT"]), (mu_r[:, :], a["mu_r"]), (mu_k[:, :], a["mu_k"]),
            (s_cT[:, 0, :], a["c0T"]), (s_cT[:, 1, :], a["c1T"]), (wmod[0][:, :], a["wmod0"]), (wmod[1][:, :], a["wmod1"]),
        ]
        for dst, name in ((bc_v0, "bv"), (bc_o0, "bo"), (bc_b2, "b2"), (bc_g3, "g3"), (bc_be3, "be3"), (bc_wo, "wo_b"),
                          (bc_gate, "gate_b"), (bc_tb, "theta_bias")):
            loads.append((dst[:, :], a[name].partition_broadcast(128)))
        for dst, name in ((s_gam, "gamma"), (s_bet, "beta"), (s_the, "theta")):
            loads.append((dst, a[name].partition_broadcast(128)))
        N_LOADS = len(loads)
        N_SETS = 10

        GATE_COLS = [2 * D, 5 * D]
        MOD_BLOCKS = [0, 1, 3, 4]
        x_dram = a["x"].rearrange("b (t p) d -> b p t d", p=128)
        out_dram = out.rearrange("b (j t) d -> b t j d", t=K)

        jobs = {}

        block = ctx.enter_context(nc.Block())

        @block.tensor
        def _(pe):
            count = [0] * 8
            mm = nc.tensor.matmul

            def begin(name, b):
                if count[b]:
                    pe.wait_ge(S[f"drained_{b}"], count[b])
                count[b] += 1
                jobs[name] = (b, count[b])

            def end(ins, b):
                ins.then_inc(S[f"filled_{b}"], 1)

            def ready(name):
                b, n = jobs[name]
                pe.wait_ge(S[f"drained_{b}"], n)

            pe.wait_ge(weights_loaded, 16 * N_LOADS)
            pe.wait_ge(dve_set, 1)
            for g in range(HP):
                mm(bank[0][:, 0:D], s_wqT[:, g, :], s_wo[:, g, :], start=(g == 0), stop=(g == HP - 1))
            for g in range(HP):
                mm(bank[1][:, 0:D], s_bb[:, g, :], s_wo[:, g, :], start=(g == 0), stop=(g == HP - 1))
            for l in range(2):
                for n, blk in enumerate(MOD_BLOCKS):
                    mm(bank[2][:, (4 * l + n) * B:(4 * l + n + 1) * B], wmod[l][:, blk * D:(blk + 1) * D],
                       s_sig[:, l, :], start=True, stop=True)
            cb = s_cb[:, :].rearrange("p (n m) -> p n m", m=128)
            for n in range(B + PAIRS):
                l = 0 if n < B else 1
                for k, col in enumerate(GATE_COLS):
                    last = mm(bank[4 + n % 4][:, k * D:(k + 1) * D], cb[:, n, :], wmod[l][:, col:col + D],
                              start=True, stop=True)
                last.then_inc(pe_set, 1)
                if n % 4 == 3 and n < B + PAIRS - 1:
                    pe.wait_ge(dve_set, 1 + n + 1)

            pe.wait_ge(pool_set, N_SETS)
            pe.wait_ge(dve_set, 2 + B + PAIRS)

            with pe.Fori(0, TRIPS) as _i:
                for b in range(8):
                    count[b] = 0

                def transposes(name, b, src, u, ready):
                    begin(name, b)
                    pe.wait_ge(S[f"{ready}_{u}"], 1)
                    for t in range(T):
                        last = nc.tensor.transpose(bank[b][:, t * 128:(t + 1) * 128], src[:, t, :], ident[:, :])
                    end(last, b)

                for u in range(2):
                    transposes(f"hT{u}", 4 * u, L[u]["hat"], u, "ln1_hat")
                for u in range(2):
                    l = L[u]
                    ready(f"hT{u}")
                    for n, (w, name) in enumerate(((w_q0, "qT"), (w_k0, "kT"))):
                        b = 4 * u + 1 + n
                        begin(f"{name}{u}", b)
                        end(mm(bank[b], w[:, :], l["hT"][:, :], start=True, stop=True), b)
                    b = 4 * u + 3
                    begin(f"v{u}", b)
                    for t in range(T):
                        last = mm(bank[b][:, t * D:(t + 1) * D], l["hT"][:, t * 128:(t + 1) * 128], w_v0[:, :], start=True, stop=True)
                    end(last, b)
                for name, src, sem in (("xq", "qT", 1), ("xk", "kT", 2)):
                    for u in range(2):
                        l = L[u]
                        ready(f"{src}{u}")
                        for t in range(T):
                            b = 4 * u + t
                            begin(f"{name}{u}{t}", b)
                            end(mm(bank[b], l[src][:, t * 128:(t + 1) * 128], proj_bd[:, :], start=True, stop=True), b)
                for u in range(2):
                    l, b = L[u], 4 * u
                    begin(f"qb{u}", b)
                    ready(f"xq{u}{T - 1}")
                    mm(bank[b][0:H0, :], half_square[:, :], l["q2"][:, :], start=True, stop=False)
                    for t in range(T):
                        last = mm(bank[b][0:H0, t * 128:(t + 1) * 128], l["qmax"][:, t, :], ident[:, :], start=False, stop=(t == T - 1))
                    end(last, b)
                    b = 4 * u + 1
                    begin(f"kmT{u}", b)
                    pe.wait_ge(S[f"k_max_ready_{u}"], 1)
                    end(nc.tensor.transpose(bank[b][0:H0, 0:128], l["kmx"][:, :], ident[:, :]), b)
                for u in range(2):
                    l = L[u]
                    ready(f"qb{u}")
                    for g in range(G):
                        b = 4 * u + (2 + g) % 4
                        begin(f"fq{u}{g}", b)
                        mm(bank[b], proj_bd[:, g * 128:(g + 1) * 128], l["qT"][:, :], start=True, stop=False)
                        end(mm(bank[b], neg_sel[:, g * 128:(g + 1) * 128], l["qb"][:, :], start=False, stop=True), b)
                for u in range(2):
                    l, b = L[u], 4 * u + 2
                    begin(f"kb{u}", b)
                    pe.wait_ge(S[f"k_stab_ready_{u}"], 1)
                    for t in range(T):
                        o = bank[b][:, t * H0:(t + 1) * H0]
                        mm(o, l["k2"][:, t * 128:(t + 1) * 128], half_square[:, :], start=True, stop=False)
                        last = mm(o, ones[0:H0, :], l["sd"][:, :], start=False, stop=True)
                    end(last, b)
                for u in range(2):
                    l = L[u]
                    pe.wait_ge(S[f"k_feat_ready_{u}"], T)
                    ready(f"v{u}")
                    for half in range(2):
                        b = 4 * u + half
                        begin(f"ctx{u}{half}", b)
                        for g in (2 * half, 2 * half + 1):
                            for t in range(T):
                                last = mm(bank[b][:, (g % 2) * 256:(g % 2) * 256 + D + 1], l["ek"][:, t, g * 128:(g + 1) * 128],
                                          l["v"][:, t, :], start=(t == 0), stop=(t == T - 1))
                        end(last, b)
                for u in range(2):
                    l = L[u]
                    pe.wait_ge(S[f"q_feat_ready_{u}"], G)
                    ready(f"ctx{u}0")
                    ready(f"ctx{u}1")
                    for half in range(2):
                        b = 4 * u + 2 + half
                        begin(f"num{u}{half}", b)
                        for t in (2 * half, 2 * half + 1):
                            for g in range(G):
                                last = mm(bank[b][:, (t % 2) * 256:(t % 2) * 256 + D + H0], l["big"][:, g, t * 128:(t + 1) * 128],
                                          l["ctx"][:, g, :], start=(g == 0), stop=(g == G - 1))
                        end(last, b)
                for u in range(2):
                    l, b = L[u], 4 * u
                    begin(f"attnT{u}", b)
                    ready(f"num{u}0")
                    ready(f"num{u}1")
                    for t in range(T):
                        last = nc.tensor.transpose(bank[b][:, t * 128:(t + 1) * 128], l["y"][:, t, :], ident[:, :])
                    end(last, b)
                for u in range(2):
                    l, b = L[u], 4 * u + 1
                    begin(f"y1{u}", b)
                    ready(f"attnT{u}")
                    for t in range(T):
                        o = bank[b][:, t * D:(t + 1) * D]
                        mm(o, l["q2"][:, t * 128:(t + 1) * 128], w_o0[:, :], start=True, stop=False)
                        last = mm(o, l["hT"][:, t * 128:(t + 1) * 128], ident[:, :], start=False, stop=True)
                    end(last, b)
                for u in range(2):
                    transposes(f"x1T{u}", 4 * u, L[u]["hat"], u, "ln2_hat")
                for u in range(2):
                    l = L[u]
                    ready(f"x1T{u}")
                    for f in range(NF):
                        b = 4 * u + (2 + f) % 4
                        begin(f"f1{u}{f}", b)
                        end(mm(bank[b], w_1[:, f * 128:(f + 1) * 128], l["kT"][:, :], start=True, stop=True), b)
                for u in range(2):
                    l, b = L[u], 4 * u + 2
                    begin(f"y2{u}", b)
                    for f in range(NF):
                        ready(f"f1{u}{f}")
                    for t in range(T):
                        o = bank[b][:, t * D:(t + 1) * D]
                        for f in range(NF):
                            mm(o, l["big"][:, f, t * 128:(t + 1) * 128], w_2[:, f, :], start=(f == 0), stop=False)
                        last = mm(o, l["kT"][:, t * 128:(t + 1) * 128], ident[:, :], start=False, stop=True)
                    end(last, b)
                for u in range(2):
                    transposes(f"h2T{u}", 4 * u, L[u]["hat"], u, "ln4_hat")
                for u in range(2):
                    l, b = L[u], 4 * u + 1
                    ready(f"h2T{u}")
                    begin(f"gate{u}", b)
                    for t in range(T):
                        last = mm(bank[b][:, t * 40:(t + 1) * 40], l["hT"][:, t * 128:(t + 1) * 128], w_ga[:, :], start=True, stop=True)
                    end(last, b)
                for u in range(2):
                    l, b = L[u], 4 * u
                    begin(f"umT{u}", b)
                    ready(f"gate{u}")
                    for t in range(T):
                        last = nc.tensor.transpose(bank[b][0:E * R, t * 128:(t + 1) * 128], l["um"][:, t, :], ident[:, :])
                    end(last, b)
                for u in range(2):
                    l = L[u]
                    ready(f"umT{u}")
                    for f in range(NF):
                        b = 4 * u + (1 + f) % 4
                        begin(f"f2{u}{f}", b)
                        mm(bank[b], w_i[:, f * 128:(f + 1) * 128], l["hT"][:, :], start=True, stop=False)
                        end(mm(bank[b], lora_b[:, f * 128:(f + 1) * 128], l["umT"][:, :], start=False, stop=True), b)
                for u in range(2):
                    l, b = L[u], 4 * u + 1
                    begin(f"y3{u}", b)
                    for f in range(NF):
                        ready(f"f2{u}{f}")
                    for t in range(T):
                        for f in range(NF):
                            last = mm(bank[b][:, t * D:(t + 1) * D], l["big"][:, f, t * 128:(t + 1) * 128], w_of[:, f, :],
                                      start=(f == 0), stop=(f == NF - 1))
                    end(last, b)
                for u in range(2):
                    transposes(f"h3T{u}", 4 * u, L[u]["hat"], u, "ln5_hat")

                def chunk(j):
                    return h3[:, j, :, :].rearrange("p b t -> p (b t)")

                def headT(name, w, j):
                    for half in range(2):
                        b = 6 + half
                        begin(f"{name}{j}{half}", b)
                        for g in range(4):
                            gg = 4 * half + g
                            last = mm(bank[b][:, g * 128:(g + 1) * 128], w[:, gg * 128:(gg + 1) * 128], chunk(j), start=True, stop=True)
                        end(last, b)

                def rows(name, w, j):
                    for half in range(2):
                        b = 6 + half
                        begin(f"{name}{j}{half}", b)
                        end(mm(bank[b], chunk(j), w[:, half * HALF:(half + 1) * HALF], start=True, stop=True), b)

                def project(j):
                    headT("kT1_", w_k1, j)
                    rows("k1_", w_k1, j)
                    rows("t1_", w_t1, j)

                def predict(name, src, used, half):
                    b = 4 + half
                    for h in range(HH * half, HH * (half + 1)):
                        for c in range(2):
                            last = mm(bank[b][64 * c:64 * c + 64, (h % HH) * HD:(h % HH + 1) * HD],
                                      src[:, h, 64 * c:64 * c + 64], w_sb[:, h, c, :], start=True, stop=True)
                    end(last, b)

                for u in range(2):
                    ready(f"h3T{u}")
                for n in range(4):
                    begin(f"w{n}", n)
                    end(mm(bank[n][0:C, :], ident[0:C, 0:C],
                           w_init[:, 4 * n:4 * n + 4, :, :].rearrange("p h b d -> p (h b d)"), start=True, stop=True,
                           skip_group_check=True), n)
                begin("rate", 5)
                for j in range(NJ):
                    last = mm(bank[5][:, j * H:(j + 1) * H], chunk(j), w_theta[:, :], start=True, stop=True)
                end(last, 5)
                project(0)
                for j in range(NJ + 2):
                    if j < NJ:
                        for half in range(2):
                            begin(f"z{j}{half}", 4 + half)
                            pe.wait_ge(S["w_ready"], 2 * j + half + 1)
                            ready(f"kT1_{j}{half}")
                            predict("z", kT1, None, half)
                    if j + 1 < NJ:
                        project(j + 1)
                    if 1 <= j <= NJ:
                        for half in range(2):
                            begin(f"zq{j - 1}{half}", 4 + half)
                            pe.wait_ge(S["w_ready"], 2 * j + half + 1)
                            ready(f"qT1_{j - 1}{half}")
                            predict("zq", qT1, None, half)
                    if j < NJ:
                        headT("qT1_", w_q1, j)
                    if j >= 2:
                        for half in range(2):
                            b = 6 + half
                            begin(f"zT{j - 2}{half}", b)
                            ready(f"zq{j - 2}{half}")
                            for g in range(4):
                                last = nc.tensor.transpose(bank[b][:, g * 128:(g + 1) * 128],
                                                           zq_hat[:, (4 * half + g) * 128:(4 * half + g + 1) * 128], ident[:, :])
                            end(last, b)
                    if j < NJ:
                        for half in range(2):
                            pe.wait_ge(S["k_scaled"], 2 * j + half + 1)
                            pe.wait_ge(S["grad_top"], 2 * j + half + 1)
                            pe.wait_ge(S["grad_bot"], 2 * j + half + 1)
                            for h in range(HH * half, HH * (half + 1)):
                                last = mm(bank[h // 4][0:C, (h % 4) * 128:(h % 4 + 1) * 128], k_sc[:, h, :],
                                          grad[:, h, :, :].rearrange("p b d -> p (b d)"), start=False, stop=(h % 4 == 3),
                                          skip_group_check=True)
                            last.then_inc(S["dw_done"], 1)
                    if j >= 2:
                        begin(f"o{j - 2}", 6)
                        ready(f"zT{j - 2}0")
                        ready(f"zT{j - 2}1")
                        mm(bank[6][:, 0:D], chunk(j - 2), w_qo[:, :], start=True, stop=False)
                        for g in range(HP):
                            last = mm(bank[6][:, 0:D], zT[:, g, :], g_wo[:, g, :], start=False, stop=(g == HP - 1))
                        end(last, 6)

                for half in range(2):
                    b = half
                    begin(f"h4{half}", b + 4)
                    pe.wait_ge(S["ln6_hat"], 1)
                    for t in range(4):
                        last = nc.tensor.transpose(bank[b + 4][:, t * 128:(t + 1) * 128], hat6[:, 4 * half + t, :], ident[:, :])
                    end(last, b + 4)
                pe.wait_ge(S["mix_ready"], 2)
                for half in range(2):
                    b = 6 + half
                    begin(f"key{half}", b)
                    end(mm(bank[b], w_kf[:, :], mix_k[:, half * 512:(half + 1) * 512], start=True, stop=True), b)
                for half in range(2):
                    b = 4 + half
                    begin(f"r{half}", b)
                    for t in range(4):
                        j = 4 * half + t
                        last = mm(bank[b][:, t * D:(t + 1) * D], mix_r[:, j * 128:(j + 1) * 128], w_r[:, :], start=True, stop=True)
                    end(last, b)
                for half in range(2):
                    b = 6 + half
                    begin(f"val{half}", b)
                    pe.wait_ge(S["key_ready"], half + 1)
                    for t in range(4):
                        j = 4 * half + t
                        last = mm(bank[b][:, t * D:(t + 1) * D], kact[:, j * 128:(j + 1) * 128], w_vf[:, :], start=True, stop=True)
                    end(last, b)
                pe.drain().then_inc(S["engines_done"], 1)
                pe.wait_ge(go["pe"], 1)
                pe.sem_clear(go["pe"])

        def filled(eng, name):
            b, n = jobs[name]
            eng.wait_ge(S[f"filled_{b}"], n)
            return bank[b]

        def drained(name):
            return S[f"drained_{jobs[name][0]}"]

        def ready(eng, name):
            b, n = jobs[name]
            eng.wait_ge(S[f"drained_{b}"], n)

        @block.scalar
        def _(act):
            act.wait_ge(weights_loaded, 16 * N_LOADS)
            nc.scalar.activation(s_sig[:, :, :], s_cT[:, :, :], ACT.Sigmoid).then_inc(act_set, 1)
            act.wait_ge(dve_set, 2 + B + PAIRS)

            with act.Fori(0, TRIPS) as _i:
                def root(name, src, dst, u=None, scale=1.0, eps=LN_EPS):
                    key = name if u is None else f"{name}_{u}"
                    nc.scalar.activation(dst, src, ACT.Sqrt, bias=eps, scale=scale).then_inc(S[key], 1)

                def modulated(name, dst, shift, scl_):
                    src = filled(act, name)
                    nc.scalar.activation(dst, src, ACT.Identity, bias=shift, scale=scl_)\
                       .then_inc(drained(name), 1)

                act.wait_ge(S["mods_ready"], 1)
                for u in range(2):
                    act.wait_ge(S[f"ln1_var_{u}"], 1)
                    root("ln1_std", L[u]["mv"][:, :, 1], L[u]["std"][:, :], u)
                for u in range(2):
                    modulated(f"hT{u}", L[u]["hT"][:, :], mod[:, 0, u:u + 1], mod[:, 1, u:u + 1])
                for u in range(2):
                    l = L[u]
                    for name, dst, dst2, bias in (("qT", "qT", "q2", b_q0), ("kT", "kT", "k2", b_k0)):
                        src = filled(act, f"{name}{u}")
                        nc.scalar.activation(l[dst][:, :], src, ACT.Identity, bias=bias[:, :])
                        nc.scalar.activation(l[dst2][:, :], src, ACT.Square, bias=bias[:, :]).then_inc(drained(f"{name}{u}"), 1)
                for u in range(2):
                    for t in range(T):
                        src = filled(act, f"xk{u}{t}")
                        nc.scalar.copy(L[u]["ek"][:, t, :], src).then_inc(drained(f"xk{u}{t}"), 1)
                for u in range(2):
                    src = filled(act, f"qb{u}")
                    nc.scalar.copy(L[u]["qb"][0:H0, :], src[0:H0, :]).then_inc(drained(f"qb{u}"), 1)
                for u in range(2):
                    for g in range(G):
                        src = filled(act, f"fq{u}{g}")
                        nc.scalar.activation(L[u]["big"][:, g, :], src, ACT.Exp).then_inc(drained(f"fq{u}{g}"), 1)
                for u in range(2):
                    for t in range(T):
                        act.wait_ge(S[f"k_shifted_{u}"], t + 1)
                        nc.scalar.activation(L[u]["ek"][:, t, :], L[u]["ek"][:, t, :], ACT.Exp).then_inc(S[f"k_exp_{u}"], 1)
                for u in range(2):
                    src = filled(act, f"attnT{u}")
                    nc.scalar.copy(L[u]["q2"][:, :], src).then_inc(drained(f"attnT{u}"), 1)
                for u in range(2):
                    act.wait_ge(S[f"ln2_var_{u}"], 1)
                    root("ln2_std", L[u]["mv"][:, :, 1], L[u]["std"][:, :], u)
                for u in range(2):
                    modulated(f"x1T{u}", L[u]["kT"][:, :], be2[:, :], g2[:, :])
                for u in range(2):
                    for f in range(NF):
                        src = filled(act, f"f1{u}{f}")
                        nc.scalar.activation(L[u]["big"][:, f, :], src, ACT.Relu, bias=b_1[:, f:f + 1]).then_inc(drained(f"f1{u}{f}"), 1)
                for u in range(2):
                    act.wait_ge(S[f"ln3_var_{u}"], 1)
                    root("ln3_std", L[u]["mv"][:, :, 1], L[u]["std"][:, :], u)
                for u in range(2):
                    act.wait_ge(S[f"ln4_var_{u}"], 1)
                    root("ln4_std", L[u]["mv"][:, :, 1], L[u]["std"][:, :], u)
                for u in range(2):
                    modulated(f"h2T{u}", L[u]["hT"][:, :], mod[:, 2, u:u + 1], mod[:, 3, u:u + 1])
                for u in range(2):
                    src = filled(act, f"umT{u}")
                    nc.scalar.copy(L[u]["umT"][0:E * R, :], src[0:E * R, :]).then_inc(drained(f"umT{u}"), 1)
                for u in range(2):
                    for f in range(NF):
                        src = filled(act, f"f2{u}{f}")
                        nc.scalar.activation(L[u]["big"][:, f, :], src, ACT.Relu, bias=b_i[:, f:f + 1]).then_inc(drained(f"f2{u}{f}"), 1)
                for u in range(2):
                    act.wait_ge(S[f"ln5_var_{u}"], 1)
                    root("ln5_std", L[u]["mv"][:, :, 1], L[u]["std"][:, :], u)
                for u in range(2):
                    src = filled(act, f"h3T{u}")
                    nc.scalar.activation(h3[:, :, u, :], src.rearrange("p (j t) -> p j t", j=NJ), ACT.Identity,
                                         bias=mod[:, 4, u:u + 1], scale=mod[:, 5, u:u + 1]).then_inc(drained(f"h3T{u}"), 1)

                ready(act, "rate")
                nc.scalar.activation(eta[:, :, :], eta[:, :, :], ACT.Sigmoid).then_inc(S["rate_sig"], 1)

                def state(half):
                    nc.scalar.copy(w_sb[:, HH * half:HH * (half + 1), :, :].rearrange("p h b d -> p (h b d)"),
                                   ps[0:C, 2 * half:2 * half + 2, :].rearrange("p a c -> p (a c)")).then_inc(S["w_ready"], 1)

                for half in range(2):
                    for n in (2 * half, 2 * half + 1):
                        filled(act, f"w{n}")
                    state(half)

                def split_heads(name, dst, j):
                    for half in range(2):
                        key = f"{name}{j}{half}"
                        src = filled(act, key).rearrange("p (g t) -> p g t", g=4)
                        d = dst[0:HD, HH * half:HH * (half + 1), :].rearrange("p (g e) t -> p g e t", e=2)
                        nc.scalar.copy(d[:, :, 0, :], src[0:HD])
                        nc.scalar.copy(d[:, :, 1, :], src[HD:128]).then_inc(drained(key), 1)

                def key_rows(j):
                    for half in range(2):
                        src = filled(act, f"k1_{j}{half}")
                        if j:
                            act.wait_ge(S["k_scaled"], 2 * (j - 1) + half + 1)
                        nc.scalar.copy(k_tok[:, half * HALF:(half + 1) * HALF], src).then_inc(drained(f"k1_{j}{half}"), 1)

                split_heads("kT1_", kT1, 0)
                key_rows(0)
                for j in range(NJ + 2):
                    if j < NJ:
                        for half in range(2):
                            src = filled(act, f"z{j}{half}")
                            nc.scalar.activation(sq[:, half * HALF:(half + 1) * HALF], src, ACT.Square).then_inc(S["z_squared"], 1)
                        for half in range(2):
                            act.wait_ge(S["z_var"], 2 * j + half + 1)
                            nc.scalar.activation(zstd[:, HH * half:HH * (half + 1)], ssum[:, HH * half:HH * (half + 1)], ACT.Sqrt,
                                                 bias=TTT_EPS, scale=1.0 / HD).then_inc(S["z_std"], 1)
                    if j + 1 < NJ:
                        split_heads("kT1_", kT1, j + 1)
                        key_rows(j + 1)
                    if 1 <= j <= NJ:
                        for half in range(2):
                            src = filled(act, f"zq{j - 1}{half}")
                            nc.scalar.activation(sqq[:, half * HALF:(half + 1) * HALF], src, ACT.Square).then_inc(S["zq_squared"], 1)
                        for half in range(2):
                            act.wait_ge(S["zq_var"], 2 * (j - 1) + half + 1)
                            nc.scalar.activation(qstd[:, HH * half:HH * (half + 1)], qsum[:, HH * half:HH * (half + 1)], ACT.Sqrt,
                                                 bias=TTT_EPS, scale=1.0 / HD).then_inc(S["zq_std"], 1)
                    if j < NJ:
                        split_heads("qT1_", qT1, j)
                    if j >= 2:
                        if j >= 3:
                            filled(act, f"o{j - 3}")
                        for half in range(2):
                            src = filled(act, f"zT{j - 2}{half}")
                            nc.scalar.copy(zT[:, 4 * half:4 * half + 4, :].rearrange("p g t -> p (g t)"), src).then_inc(drained(f"zT{j - 2}{half}"), 1)
                    if j < NJ:
                        for half in range(2):
                            act.wait_ge(S["dw_done"], 2 * j + half + 1)
                            state(half)
                act.wait_ge(S["ln6_var"], 1)
                nc.scalar.activation(std6[:, :], mv6[:, :, 1], ACT.Sqrt, bias=LN_EPS).then_inc(S["ln6_std"], 1)
                for half in range(2):
                    src = filled(act, f"h4{half}").rearrange("p (j b t) -> p j b t", j=4, b=2)
                    nc.scalar.activation(h4[:, 4 * half:4 * half + 4, 0, :], src[:, :, 0, :], ACT.Identity,
                                         bias=mod[:, 6, 0:1], scale=mod[:, 7, 0:1])
                    nc.scalar.activation(h4[:, 4 * half:4 * half + 4, 1, :], src[:, :, 1, :], ACT.Identity,
                                         bias=mod[:, 6, 1:2], scale=mod[:, 7, 1:2]).then_inc(drained(f"h4{half}"), 1)
                for half in range(2):
                    src = filled(act, f"key{half}")
                    d = kact[:, half * 512:(half + 1) * 512]
                    nc.scalar.activation(d, src, ACT.Relu).then_inc(drained(f"key{half}"), 1)
                    act.wait_ge(drained(f"key{half}"), jobs[f"key{half}"][1])
                    nc.scalar.activation(d, d, ACT.Square).then_inc(S["key_ready"], 1)
                for half in range(2):
                    src = filled(act, f"r{half}")
                    nc.scalar.activation(r_sb[:, half * 512:(half + 1) * 512], src, ACT.Sigmoid).then_inc(drained(f"r{half}"), 1)
                act.drain().then_inc(S["engines_done"], 1)
                act.wait_ge(go["act"], 1)
                act.sem_clear(go["act"])

        @block.vector
        def _(dve):
            V = nc.vector
            steps = [0]

            def step(ins, sem):
                steps[0] += 1
                ins.then_inc(sem, 1)
                return steps[0]

            def link0(ins):
                dve.wait_ge(set_step, step(ins, set_step))

            dve.wait_ge(weights_loaded, 16 * N_LOADS)
            dve.wait_ge(act_set, 1)
            link0(V.tensor_tensor(proj_bd[:, :], proj_bd[:, :], s_cb[:, 0:FEAT], ALU.mult))
            link0(V.tensor_tensor(s_sig[:, :, :], s_cT[:, :, :], s_sig[:, :, :], ALU.mult))
            cb = s_cb[:, :].rearrange("p (n m) -> p n m", m=128)
            for n in range(B):
                V.tensor_copy(cb[:, n, :], s_sig[:, 0, n:n + 1].broadcast_to([128, 128]))
            for n in range(B):
                V.tensor_copy(cb[:, B + n // 2, 64 * (n % 2):64 * (n % 2) + 64], s_sig[:, 1, n:n + 1].broadcast_to([128, 64]))
            for g in range(HP):
                last = V.tensor_copy(s_bb[:, g, :], s_small[:, 2 + g:3 + g].broadcast_to([128, 128]))
            last.then_inc(dve_set, 1)
            for n in range(B + PAIRS):
                dst = gate0[:, n, :, :] if n < B else gate1[:, n - B, :, :]
                dve.wait_ge(pe_set, n + 1)
                V.tensor_copy(dst.rearrange("p k d -> p (k d)"), bank[4 + n % 4][:, 0:2 * D]).then_inc(dve_set, 1)
            dve.wait_ge(dve_set, 1 + B + PAIRS)
            for gate, n, s_g, m_g in ((gate0, B, L[0]["ek"], L[1]["ek"]), (gate1, PAIRS, L[0]["ek"], L[1]["ek"])):
                gv = gate[:, :, :, :].rearrange("p n k d -> p (n k d)")
                sg = s_g[:, :, :].rearrange("p a b -> p (a b)")[:, 0:n * 2 * D]
                mg = m_g[:, :, :].rearrange("p a b -> p (a b)")[:, 0:n * 2 * D]
                if gate is gate0:
                    link0(V.tensor_reduce(s_small[0:C, 32:48], s_w0, AX, ALU.add))
                    link0(V.tensor_scalar(s_small[0:C, 32:48], s_small[0:C, 32:48], 1.0 / HD, None, ALU.mult))
                    for b in range(2):
                        V.tensor_tensor(w_init[:, :, b, :], s_w0, s_small[0:C, 32:48].unsqueeze(2).broadcast_to([C, H, HD]), ALU.subtract)
                    for g in range(HP):
                        V.tensor_scalar(g_wo[:, g, :], s_wo[:, g, :], s_small[:, 16 + g:17 + g], None, ALU.mult)
                    link0(V.tensor_copy(w_qo[:, :], bank[0][:, 0:D]))
                link0(V.tensor_scalar(sg, gv, 0.0, 2.0, ALU.is_ge, ALU.mult))
                link0(V.tensor_scalar(mg, gv, -1.0, None, ALU.mult))
                link0(V.tensor_tensor(mg, mg, gv, ALU.max))
                link0(V.tensor_scalar(mg, mg, 0.25, None, ALU.max))
                link0(V.scalar_tensor_tensor(gv, sg, -1.0, mg, ALU.add, ALU.mult))
            V.tensor_copy(bc_out1[:, :], bank[1][:, 0:D])
            link0(V.tensor_copy(mod_all[:, :, :].rearrange("p k b -> p (k b)"), bank[2][:, 0:8 * B]))
            mp = mod_all[:, :, :].rearrange("p (k two) b -> p k two b", two=2)
            V.tensor_scalar(mp[:, :, 1, :], mp[:, :, 1, :], 1.0, None, ALU.add)
            link0(V.tensor_tensor(w_t1[:, :], w_k1[:, :], s_wv, ALU.subtract))
            V.tensor_tensor(w_t1[:, :], w_t1[:, :], s_gam, ALU.mult)
            V.tensor_tensor(gamma2[:, :], s_gam, s_gam, ALU.mult)
            V.tensor_tensor(gam_bet[:, :], s_gam, s_bet, ALU.mult)
            link0(V.tensor_tensor(tmp[:, :], w_k1[:, :], s_the, ALU.mult))
            V.tensor_reduce(w_theta[:, :], tmp[:, :].rearrange("p (h d) -> p h d", h=H), AX, ALU.add)
            link0(V.tensor_tensor(rate[:, :], s_small[:, 0:1], s_small[:, 1:2], ALU.add))
            link0(V.tensor_scalar(rate[:, :], rate[:, :], 0.0, -1.0 / HD, ALU.max, ALU.mult))
            V.tensor_scalar(mu_r[:, :], mu_r[:, :], -1.0, None, ALU.add)
            V.tensor_scalar(mu_k[:, :], mu_k[:, :], -1.0, None, ALU.add).then_inc(dve_set, 1)
            dve.wait_ge(dve_set, 2 + B + PAIRS)
            dve.wait_ge(pool_set, N_SETS)

            with dve.Fori(0, TRIPS) as i:
                steps[0] = 0

                def go_on(ins):
                    return step(ins, S["dve_step"])

                def settled(n):
                    dve.wait_ge(S["dve_step"], n)

                def link(ins):
                    settled(go_on(ins))

                def over(ap, n):
                    return ap.unsqueeze(1).broadcast_to([128, n, D])

                V.tensor_copy(g_ab0[:, :, :, :].rearrange("p b k d -> p (b k d)"),
                              gate0[:, bass.ds(2 * i, 2), :, :].rearrange("p b k d -> p (b k d)"))
                V.tensor_copy(g_ab1[:, :, :].rearrange("p k d -> p (k d)"),
                              gate1[:, bass.ds(i, 1), :, :].rearrange("p b k d -> p (b k d)"))
                V.tensor_copy(mod[:, :, :], mod_all[:, :, bass.ds(2 * i, 2)]).then_inc(S["mods_ready"], 1)
                dve.wait_ge(S["mods_ready"], 1)
                for u in range(2):
                    V.tensor_tensor(gg3[:, u, 0, :], g_ab0[:, u, 0, :], bc_g3[:, :], ALU.mult)
                    go_on(V.tensor_tensor(gg3[:, u, 1, :], g_ab0[:, u, 0, :], bc_be3[:, :], ALU.mult))

                def norm_stats(name, u, src):
                    l = L[u]
                    for t in range(T):
                        n = go_on(V.bn_stats(l["stats"][:, t, :], src[:, t, :]))
                    settled(n)
                    for t in range(T):
                        last = V.bn_aggr(l["mv"][:, t, :], l["stats"][:, t, :])
                    last.then_inc(S[f"{name}_var_{u}"], 1)

                def norm_apply(name, u, src):
                    l = L[u]
                    dve.wait_ge(S[f"{name}_std_{u}"], 1)
                    link(V.reciprocal(l["inv"][:, :], l["std"][:, :]))
                    for t in range(T):
                        last = V.tensor_scalar(l["hat"][:, t, :], src[:, t, :], l["mv"][:, t, 0:1], l["inv"][:, t:t + 1],
                                               ALU.subtract, ALU.mult)
                    last.then_inc(S[f"{name}_hat_{u}"], 1)

                for u in range(2):
                    dve.wait_ge(S[f"x_loaded_{u}"], 16)
                    norm_stats("ln1", u, x[:, u, :, :])
                for u in range(2):
                    norm_apply("ln1", u, x[:, u, :, :])
                for u in range(2):
                    src = filled(dve, f"v{u}").rearrange("p (t d) -> p t d", t=T)
                    V.tensor_tensor(L[u]["v"][:, :, 0:D], src, over(bc_v0[:, :], T), ALU.add).then_inc(drained(f"v{u}"), 1)
                for u in range(2):
                    for t in range(T):
                        src = filled(dve, f"xq{u}{t}").rearrange("p (h m) -> p h m", h=H0)
                        V.tensor_reduce(L[u]["qmax"][:, t, :], src, AX, ALU.max).then_inc(drained(f"xq{u}{t}"), 1)
                for u in range(2):
                    l = L[u]
                    for t in range(T):
                        ready(dve, f"xk{u}{t}")
                        n = go_on(V.tensor_reduce(l["kmax"][:, t, :], l["ek"][:, t, :].rearrange("p (h m) -> p h m", h=H0), AX, ALU.max))
                    settled(n)
                    V.tensor_reduce(l["kmx"][:, :], l["kmax"][:, :, :].rearrange("p t h -> p h t"), AX, ALU.max).then_inc(S[f"k_max_ready_{u}"], 1)
                for u in range(2):
                    l = L[u]
                    src = filled(dve, f"kmT{u}")
                    V.tensor_reduce(l["stab"][:, :], src[0:H0, 0:128], AX, ALU.max).then_inc(drained(f"kmT{u}"), 1)
                    ready(dve, f"kmT{u}")
                    V.tensor_scalar(l["sd"][:, :], ident[0:H0, 0:H0], l["stab"][:, :], None, ALU.mult).then_inc(S[f"k_stab_ready_{u}"], 1)
                for u in range(2):
                    l = L[u]
                    src = filled(dve, f"kb{u}")
                    V.tensor_copy(l["kmax"][:, :, :].rearrange("p t h -> p (t h)"), src[:, 0:T * H0]).then_inc(drained(f"kb{u}"), 1)
                    ready(dve, f"kb{u}")
                    for t in range(T):
                        e = l["ek"][:, t, :].rearrange("p (h m) -> p h m", h=H0)
                        V.tensor_tensor(e, e, l["kmax"][:, t, :].unsqueeze(2).broadcast_to([128, H0, M]), ALU.subtract)\
                         .then_inc(S[f"k_shifted_{u}"], 1)
                for u in range(2):
                    for g in range(G):
                        ready(dve, f"fq{u}{g}")
                        V.tensor_scalar(L[u]["big"][:, g, :], L[u]["big"][:, g, :], EPS_K, None, ALU.add).then_inc(S[f"q_feat_ready_{u}"], 1)
                for u in range(2):
                    for t in range(T):
                        dve.wait_ge(S[f"k_exp_{u}"], t + 1)
                        V.tensor_scalar(L[u]["ek"][:, t, :], L[u]["ek"][:, t, :], EPS_K, None, ALU.add).then_inc(S[f"k_feat_ready_{u}"], 1)
                for u in range(2):
                    l = L[u]
                    for half in range(2):
                        src = filled(dve, f"ctx{u}{half}")
                        for g in (2 * half, 2 * half + 1):
                            o = (g % 2) * 256
                            V.tensor_tensor(l["ctx"][:, g, 0:D], src[:, o:o + D], ctx_mask[:, g, :], ALU.mult)
                            last = V.tensor_scalar(l["ctx"][:, g, D:D + H0], head_sel[:, g, :], src[:, o + D:o + D + 1], None, ALU.mult)
                        last.then_inc(drained(f"ctx{u}{half}"), 1)
                for u in range(2):
                    l = L[u]
                    for half in range(2):
                        src = filled(dve, f"num{u}{half}").rearrange("p (t c) -> p t c", t=2)
                        link(V.reciprocal(l["rden"][:, 2 * half:2 * half + 2, :], src[:, :, D:D + H0]))
                        for t in (2 * half, 2 * half + 1):
                            last = V.tensor_tensor(l["y"][:, t, :].rearrange("p (h d) -> p h d", h=H0),
                                                   src[:, t % 2, 0:D].rearrange("p (h d) -> p h d", h=H0),
                                                   l["rden"][:, t, :].unsqueeze(2).broadcast_to([128, H0, DH]), ALU.mult)
                        last.then_inc(drained(f"num{u}{half}"), 1)

                def add_row(name, u, row):
                    src = filled(dve, f"{name}{u}").rearrange("p (t d) -> p t d", t=T)
                    V.tensor_tensor(L[u]["y"][:, :, :], src, over(row[:, :], T), ALU.add).then_inc(drained(f"{name}{u}"), 1)
                    ready(dve, f"{name}{u}")

                for u in range(2):
                    add_row("y1", u, bc_o0)
                    norm_stats("ln2", u, L[u]["y"])
                for u in range(2):
                    norm_apply("ln2", u, L[u]["y"])
                for u in range(2):
                    add_row("y2", u, bc_b2)
                    norm_stats("ln3", u, L[u]["y"])
                for u in range(2):
                    l = L[u]
                    norm_apply("ln3", u, l["y"])
                    dve.wait_ge(S[f"ln3_hat_{u}"], 1)
                    link(V.tensor_tensor(l["y"][:, :, :], l["hat"][:, :, :], over(gg3[:, u, 0, :], T), ALU.mult))
                    link(V.tensor_tensor(x[:, u, :, :], x[:, u, :, :], l["y"][:, :, :], ALU.add))
                    link(V.tensor_tensor(x[:, u, :, :], x[:, u, :, :], over(gg3[:, u, 1, :], T), ALU.add))
                    norm_stats("ln4", u, x[:, u, :, :])
                for u in range(2):
                    norm_apply("ln4", u, x[:, u, :, :])
                for u in range(2):
                    l = L[u]
                    src = filled(dve, f"gate{u}")[:, 0:T * 40].rearrange("p (t c) -> p t c", t=T)
                    lg, eq, lm = l["lg"][:, :, :], l["eq"][:, :, :], l["lm"]
                    link(V.tensor_tensor(lg, src[:, :, 0:E], bc_gate[:, :].unsqueeze(1).broadcast_to([128, T, E]), ALU.add))
                    link(V.tensor_reduce(lm[:, :], lg, AX, ALU.max))
                    link(V.tensor_tensor(eq, lg, lm[:, :].unsqueeze(2).broadcast_to([128, T, E]), ALU.is_ge))
                    link(V.tensor_tensor(eq, eq, first[:, :].unsqueeze(1).broadcast_to([128, T, E]), ALU.mult))
                    link(V.tensor_reduce(lm[:, :], eq, AX, ALU.max))
                    link(V.tensor_tensor(eq, eq, lm[:, :].unsqueeze(2).broadcast_to([128, T, E]), ALU.is_equal))
                    V.tensor_tensor(l["um"][:, :, :].rearrange("p t (e r) -> p t e r", e=E),
                                    src[:, :, E:E + E * R].rearrange("p t (e r) -> p t e r", e=E),
                                    eq.unsqueeze(3).broadcast_to([128, T, E, R]), ALU.mult).then_inc(drained(f"gate{u}"), 1)
                for u in range(2):
                    l = L[u]
                    add_row("y3", u, bc_wo)
                    link(V.tensor_tensor(l["y"][:, :, :], l["y"][:, :, :], over(g_ab0[:, u, 1, :], T), ALU.mult))
                    V.tensor_tensor(x[:, u, :, :], x[:, u, :, :], l["y"][:, :, :], ALU.add).then_inc(S[f"x_layer0_{u}"], 1)
                    dve.wait_ge(S[f"x_layer0_{u}"], 1)
                    norm_stats("ln5", u, x[:, u, :, :])
                for u in range(2):
                    norm_apply("ln5", u, x[:, u, :, :])

                def heads(ap, half):
                    return ap[:, half * HALF:(half + 1) * HALF].rearrange("p (h d) -> p h d", h=HH)

                def per_head(ap):
                    return ap.unsqueeze(2).broadcast_to([ap.shape[0], HH, HD])

                def target_rows(j):
                    for half in range(2):
                        src = filled(dve, f"t1_{j}{half}")
                        V.tensor_tensor(t_tok[:, j % 2, half * HALF:(half + 1) * HALF], src, gam_bet[:, half * HALF:(half + 1) * HALF],
                                        ALU.add).then_inc(drained(f"t1_{j}{half}"), 1)

                src = filled(dve, "rate")[:, 0:NJ * H].rearrange("p (j h) -> p j h", j=NJ)
                V.tensor_tensor(eta[:, :, :], src, bc_tb[:, :].unsqueeze(1).broadcast_to([128, NJ, H]), ALU.add).then_inc(drained("rate"), 1)
                dve.wait_ge(S["rate_sig"], 1)
                link(V.tensor_scalar(eta[:, :, :], eta[:, :, :], rate[:, :], None, ALU.mult))
                target_rows(0)
                for j in range(NJ + 2):
                    halves = range(2)
                    if j < NJ:
                        for f in halves:
                            dve.wait_ge(S["z_squared"], 2 * j + f + 1)
                            V.tensor_reduce(ssum[:, HH * f:HH * (f + 1)], heads(sq, f), AX, ALU.add).then_inc(S["z_var"], 1)
                        for f in halves:
                            hs = slice(HH * f, HH * (f + 1))
                            dve.wait_ge(S["z_std"], 2 * j + f + 1)
                            link(V.reciprocal(zinv[:, hs], zstd[:, hs]))
                            V.tensor_tensor(heads(zhat, f), filled(dve, f"z{j}{f}").rearrange("p (h d) -> p h d", h=HH),
                                            per_head(zinv[:, hs]), ALU.mult).then_inc(drained(f"z{j}{f}"), 1)
                            V.tensor_tensor(scl[:, hs], zinv[:, hs], eta[:, j, hs], ALU.mult).then_inc(S["scale_ready"], 1)
                    if j + 1 < NJ:
                        target_rows(j + 1)
                    if 1 <= j <= NJ:
                        for f in halves:
                            dve.wait_ge(S["zq_squared"], 2 * (j - 1) + f + 1)
                            V.tensor_reduce(qsum[:, HH * f:HH * (f + 1)], heads(sqq, f), AX, ALU.add).then_inc(S["zq_var"], 1)
                    if j < NJ:
                        ready(dve, f"t1_{j}1")
                        base, prod = [0, 0], [0, 0]
                        for f in halves:
                            dve.wait_ge(S["g_hat"], 2 * j + f + 1)
                            base[f] = go_on(V.tensor_tensor(heads(gbase, f), heads(gbase, f), heads(t_tok[:, j % 2, :], f), ALU.add))
                        for f in halves:
                            settled(base[f])
                            ready(dve, f"z{j}{f}")
                            prod[f] = go_on(V.tensor_tensor(heads(tmp, f), heads(gbase, f), heads(zhat, f), ALU.mult))
                            V.tensor_reduce(c12[:, f, 0, :], heads(gbase, f), AX, ALU.add)
                        for f in halves:
                            settled(prod[f])
                            link(V.tensor_reduce(c12[:, f, 1, :], heads(tmp, f), AX, ALU.add))
                            link(V.tensor_scalar(c12[:, f, :, :], c12[:, f, :, :], 1.0 / HD, None, ALU.mult))
                            link(V.tensor_tensor(heads(tmp, f), heads(zhat, f), per_head(c12[:, f, 1, :]), ALU.mult))
                            V.tensor_tensor(heads(gbase, f), heads(gbase, f), heads(tmp, f), ALU.subtract).then_inc(S["grad_base"], 1)
                            dve.wait_ge(S["grad_base"], 2 * j + f + 1)
                            V.tensor_tensor(grad[0:K, HH * f:HH * (f + 1), 0, :], heads(gbase, f)[0:K], per_head(c12[0:K, f, 0, :]),
                                            ALU.subtract).then_inc(S["grad_top"], 1)
                    if 1 <= j <= NJ:
                        for f in halves:
                            hs = slice(HH * f, HH * (f + 1))
                            dve.wait_ge(S["zq_std"], 2 * (j - 1) + f + 1)
                            link(V.reciprocal(qinv[:, hs], qstd[:, hs]))
                            if j >= 2:
                                filled(dve, f"zT{j - 2}{f}")
                            V.tensor_tensor(heads(zq_hat, f), filled(dve, f"zq{j - 1}{f}").rearrange("p (h d) -> p h d", h=HH),
                                            per_head(qinv[:, hs]), ALU.mult).then_inc(drained(f"zq{j - 1}{f}"), 1)
                    if j >= 2:
                        src = filled(dve, f"o{j - 2}")
                        V.tensor_tensor(att1[:, :], src[:, 0:D], bc_out1[:, :], ALU.add).then_inc(drained(f"o{j - 2}"), 1)
                        ready(dve, f"o{j - 2}")
                        link(V.tensor_tensor(att1[:, :], att1[:, :], g_ab1[:, 0, :], ALU.mult))
                        dve.wait_ge(S["x_moved"], 64)
                        link(V.tensor_tensor(xc[:, j - 2, :], xc[:, j - 2, :], att1[:, :], ALU.add))

                settled(steps[0])
                for j in range(NJ):
                    n = go_on(V.bn_stats(stats6[:, j, :], xc[:, j, :]))
                settled(n)
                for j in range(NJ):
                    last = V.bn_aggr(mv6[:, j, :], stats6[:, j, :])
                last.then_inc(S["ln6_var"], 1)
                dve.wait_ge(S["ln6_std"], 1)
                link(V.reciprocal(inv6[:, :], std6[:, :]))
                for j in range(NJ):
                    last = V.tensor_scalar(hat6[:, j, :], xc[:, j, :], mv6[:, j, 0:1], inv6[:, j:j + 1], ALU.subtract, ALU.mult)
                last.then_inc(S["ln6_hat"], 1)
                for half in range(2):
                    ready(dve, f"h4{half}")
                V.tensor_tensor(diff[:, :, :, 1:K], h4[:, :, :, 1:K], h4[:, :, :, 0:K - 1], ALU.subtract)
                V.tensor_tensor(diff[:, 1:NJ, :, 0], h4[:, 1:NJ, :, 0], h4[:, 0:NJ - 1, :, K - 1], ALU.subtract)
                link(V.tensor_copy(diff[:, 0, :, 0], h4[:, 0, :, 0]))
                V.scalar_tensor_tensor(mix_k, gbase[:, :], mu_k[:, :], zhat[:, :], ALU.mult, ALU.add).then_inc(S["mix_ready"], 1)
                V.scalar_tensor_tensor(mix_r, gbase[:, :], mu_r[:, :], zhat[:, :], ALU.mult, ALU.add).then_inc(S["mix_ready"], 1)
                for half in range(2):
                    ready(dve, f"r{half}")
                    o = gbase[:, half * 512:(half + 1) * 512]
                    V.tensor_tensor(o, filled(dve, f"val{half}"), r_sb[:, half * 512:(half + 1) * 512], ALU.mult).then_inc(drained(f"val{half}"), 1)
                    ready(dve, f"val{half}")
                    o3 = o.rearrange("p (j d) -> p j d", j=4)
                    link(V.tensor_tensor(o3, o3, over(g_ab1[:, 1, :], 4), ALU.mult))
                    V.tensor_tensor(xc[:, 4 * half:4 * half + 4, :], xc[:, 4 * half:4 * half + 4, :], o3, ALU.add).then_inc(S["x_final"], 1)
                dve.drain().then_inc(S["engines_done"], 1)
                dve.wait_ge(go["dve"], 1)
                dve.sem_clear(go["dve"])

        @block.sync
        def _(sp):
            for dst, src in loads:
                sp.dma_start(dst, src).then_inc(weights_loaded, 16)
            with sp.Fori(0, TRIPS) as i:
                for u in range(2):
                    sp.dma_start(x[:, u, :, :], x_dram[bass.ds(2 * i + u, 1), :, :, :].rearrange("b p t d -> (b p) t d")).then_inc(S[f"x_loaded_{u}"], 16)
                for b in range(2):
                    sp.wait_ge(S[f"x_layer0_{b}"], 1)
                    for odd in range(2):
                        sp.dma_start(xc[64 * b:64 * b + 64, :, :].rearrange("p (t o) d -> p t o d", o=2)[:, :, odd, :],
                                     x[64 * odd:64 * odd + 64, b, :, :]).then_inc(S["x_moved"], 16)
                sp.wait_ge(S["x_final"], 2)
                for b in range(2):
                    sp.dma_start(out_dram[bass.ds(2 * i + b, 1), :, :, :].rearrange("b t j d -> (b t) j d"),
                                 xc[64 * b:64 * b + 64, :, :]).then_inc(S["out_stored"], 16)
                sp.wait_ge(S["x_moved"], 64)
                sp.wait_ge(S["out_stored"], 32)
                sp.drain().then_inc(S["engines_done"], 1)
                sp.wait_ge(go["sp"], 1)
                sp.sem_clear(go["sp"])

        @block.gpsimd
        def _(pool):
            P = nc.gpsimd
            done = 0
            for t in (ones[:, :], kT1[HD:C, :, :], qT1[HD:C, :, :], L[0]["v"][:, :, D:D + 1], L[1]["v"][:, :, D:D + 1]):
                done += 1
                P.memset(t, 1.0).then_inc(pool_set, 1)
                pool.wait_ge(pool_set, done)
            for t in (grad[:, :, :, :], L[0]["qb"][:, :], L[1]["qb"][:, :], L[0]["umT"][:, :], L[1]["umT"][:, :]):
                P.memset(t, 0.0).then_inc(pool_set, 1)
            pool.wait_ge(pool_set, N_SETS)
            pool.wait_ge(dve_set, 2 + B + PAIRS)
            with pool.Fori(0, TRIPS) as _i:
                def heads(ap, f):
                    return ap[:, f * HALF:(f + 1) * HALF].rearrange("p (h d) -> p h d", h=HH)

                for j in range(NJ):
                    if j:
                        pool.wait_ge(S["grad_bot"], 2 * j)
                    for f in range(2):
                        ready(pool, f"z{j}{f}")
                        P.tensor_tensor(heads(gbase, f), heads(zhat, f), heads(gamma2, f), ALU.mult).then_inc(S["g_hat"], 1)
                    for f in range(2):
                        hs = slice(HH * f, HH * (f + 1))
                        ready(pool, f"k1_{j}{f}")
                        pool.wait_ge(S["scale_ready"], 2 * j + f + 1)
                        P.tensor_tensor(k_sc[:, hs, 0:HD], heads(k_tok, f), scl[:, hs].unsqueeze(2).broadcast_to([128, HH, HD]), ALU.mult)
                        P.tensor_copy(k_sc[:, hs, HD:C], scl[:, hs].unsqueeze(2)).then_inc(S["k_scaled"], 1)
                    pool.wait_ge(S["k_scaled"], 2 * j + 2)
                    for f in range(2):
                        pool.wait_ge(S["grad_base"], 2 * j + f + 1)
                        P.tensor_tensor(grad[K:128, HH * f:HH * (f + 1), 1, :], heads(gbase, f)[K:128],
                                        c12[K:128, f, 0, :].unsqueeze(2).broadcast_to([K, HH, HD]), ALU.subtract).then_inc(S["grad_bot"], 1)
                pool.drain().then_inc(S["engines_done"], 1)
                pool.wait_ge(S["engines_done"], 5)
                pool.sem_clear(range(numbers[0], numbers[-1] + 1))
                for s in go.values():
                    pool.sem_inc(s, 1)


def laid_out(i):
    f = lambda v: np.ascontiguousarray(np.asarray(v))
    col = lambda v: f(np.asarray(v).reshape(-1, 128).T)
    row = lambda v: f(np.asarray(v).reshape(1, -1))
    lora_b = np.zeros((128, FF), np.float32)
    lora_b[:E * R] = np.asarray(i["L0_ffn_lora_B"]).transpose(0, 2, 1).reshape(E * R, FF)
    w1 = np.asarray(i["L1_attn_W1"]).transpose(1, 0, 2)
    return {
        "x": f(i["L0_attn_video"]), "proj_tiled": f(np.tile(np.asarray(i["L0_attn_proj"]).T, (H0, H0))),
        "WqT": f(i["L0_attn_Wq"].T), "WkT": f(i["L0_attn_Wk"].T), "WvT": f(i["L0_attn_Wv"].T), "WoT": f(i["L0_attn_Wo"].T),
        "bq": col(i["L0_attn_bq"]), "bk": col(i["L0_attn_bk"]), "g2": col(i["L0_attn_g2"]), "be2": col(i["L0_attn_be2"]),
        "bv": row(i["L0_attn_bv"]), "bo": row(i["L0_attn_bo"]), "b2": row(i["L0_attn_b2"]), "g3": row(i["L0_attn_g3"]),
        "be3": row(i["L0_attn_be3"]), "W1T": f(i["L0_attn_W1"].T), "b1": col(i["L0_attn_b1"]), "W2T": f(i["L0_attn_W2"].T),
        "gate_lora_a": f(np.concatenate([np.asarray(i["L0_ffn_gate_W"]), np.asarray(i["L0_ffn_lora_A"]).reshape(E * R, D)]).T),
        "gate_b": row(i["L0_ffn_gate_b"]), "wiT": f(i["L0_ffn_wi_W"].T), "wi_b": col(i["L0_ffn_wi_b"]), "woT": f(i["L0_ffn_wo_W"].T),
        "wo_b": row(i["L0_ffn_wo_b"]), "lora_b": lora_b, "c0T": f(i["L0_c"].T), "c1T": f(i["L1_c"].T),
        "wmod0": f(i["L0_wmod"]), "wmod1": f(i["L1_wmod"]),
        "wq1": f(i["L1_attn_wq"]), "wk1": f(i["L1_attn_wk"]), "wv1": f(i["L1_attn_wv"]), "wq1T": f(i["L1_attn_wq"].T),
        "wo1": f(i["L1_attn_wo"]), "W1c": f(w1), "b1c": f(np.asarray(i["L1_attn_b1"]).reshape(1, H, HD)),
        "theta": row(i["L1_attn_theta"]), "theta_bias": row(i["L1_attn_theta_bias"]),
        "alpha2": f(np.tile(np.asarray(i["L1_attn_alpha"]), 2)[:, None]), "gamma": row(i["L1_attn_gamma"]), "beta": row(i["L1_attn_beta"]),
        "gammaT": col(i["L1_attn_gamma"]), "betaT": col(i["L1_attn_beta"]),
        "W_rT": f(i["L1_ffn_W_r"].T), "W_kT": f(i["L1_ffn_W_k"].T), "W_vT": f(i["L1_ffn_W_v"].T),
        "mu_r": col(i["L1_ffn_mu_r"]), "mu_k": col(i["L1_ffn_mu_k"]),
        **shape_constants(),
    }


def kernel(**inputs):
    import concourse.bacc as bacc
    from concourse.bass_utils import run_bass_kernel_spmd

    arrays = laid_out(inputs)
    nc = bacc.Bacc("TRN2", target_bir_lowering=False, num_devices=1)
    aps = {n: nc.dram_tensor(f"in_{n}", v.shape, mybir.dt.from_np(v.dtype), kind="ExternalInput").ap() for n, v in arrays.items()}
    out = nc.dram_tensor("out_x", (B, N, D), F32, kind="ExternalOutput").ap()
    build(nc, aps, out)
    r = run_bass_kernel_spmd(nc, [{f"in_{n}": v for n, v in arrays.items()}], core_ids=[0])
    return r.results[0]["out_x"]
```

```python
from contextlib import ExitStack

import numpy as np

import concourse.bass as bass
from concourse import mybir

F32 = mybir.dt.float32
ALU = mybir.AluOpType
ACT = mybir.ActivationFunctionType
AX = mybir.AxisListType.X

B, N, D = 8, 512, 128
PAIRS = B // 2
TRIPS = PAIRS
T = N // 128
H0, DH, M = 16, 8, 32
FEAT = H0 * M
G = FEAT // 128
HG = H0 // G
FF = 512
NF = FF // 128
E, R = 8, 4
H, HD, K = 16, 64, 64
NJ = N // K
HW = H * HD
HP = H // 2
HH = H // 2
HALF = HH * HD
C = HD + 1
EPS_K, LN_EPS, TTT_EPS = 1e-4, 1e-5, 1e-6
NORM = DH ** -0.25


def shape_constants():
    ident = np.eye(128, dtype=np.float32)
    head_of_dim = np.arange(D) // DH
    head_of_feat = np.arange(FEAT) // M
    same = (head_of_dim[:, None] == head_of_feat[None, :]).astype(np.float32)
    proj_mask = same * np.float32(NORM)
    ctx_mask = same.T.reshape(G, 128, D).transpose(1, 0, 2).reshape(128, G * D)
    head_sel = (head_of_feat[:, None] == np.arange(H0)[None, :]).astype(np.float32)
    head_sel = head_sel.reshape(G, 128, H0).transpose(1, 0, 2).reshape(128, G * H0)
    neg_sel = np.zeros((128, FEAT), np.float32)
    neg_sel[:H0] = -(np.arange(H0)[:, None] == head_of_feat[None, :]).astype(np.float32)
    half_square = (head_of_dim[:, None] == np.arange(H0)[None, :]).astype(np.float32) * np.float32(0.5 * NORM * NORM)
    first = np.tile(np.arange(E, 0, -1, dtype=np.float32)[None, :], (128, 1))
    token_rate = np.tile(1.0 / np.arange(1, K + 1, dtype=np.float32), 2)[:, None].astype(np.float32)
    return {
        "c_ident": ident, "c_proj_mask": proj_mask, "c_ctx_mask": ctx_mask, "c_head_sel": head_sel,
        "c_neg_sel": neg_sel, "c_half_square": half_square, "c_first": first, "c_token_rate": token_rate,
    }


PER_BATCH = [f"ln{n}_{what}" for n in range(1, 6) for what in ("var", "std", "hat")]
PER_BATCH += ["k_tile_max", "k_max_ready", "k_stab_ready", "k_shifted", "k_exp", "k_feat_ready", "q_feat_ready", "x_layer0", "x_loaded"]
PER_PAIR = [
    "x_moved", "out_stored", "mods_ready", "dve_step", "pool_step", "rate_logit", "rate_sig",
    "w_ready", "z_squared", "z_var", "z_std", "scale_ready", "g_hat", "grad_base", "grad_top", "grad_bot", "k_scaled", "dw_done",
    "zq_squared", "base_ready", "att_step", "target_ready", "zq_var", "zq_std", "ln6_var", "ln6_std", "ln6_hat", "mix_ready", "key_ready", "x_ttt", "x_final",
]


def build(nc, a, out):
    with ExitStack() as ctx:
        def sb(name, shape):
            return ctx.enter_context(nc.sbuf_tensor(name, shape, F32))

        def new_sem(name):
            return ctx.enter_context(nc.semaphore(name))

        ps = ctx.enter_context(nc.psum_tensor("ps", [128, 8, 512], F32))
        bank = [ps[:, i, :] for i in range(8)]

        ident = sb("ident", [128, 128])
        proj_bd = sb("proj_bd", [128, FEAT])
        ctx_mask = sb("ctx_mask", [128, G, D])
        head_sel = sb("head_sel", [128, G, H0])
        neg_sel = sb("neg_sel", [128, FEAT])
        half_square = sb("half_square", [128, H0])
        first = sb("first", [128, E])
        ones = sb("ones", [128, 128])
        w_q0, w_k0, w_v0, w_o0 = (sb(n, [128, D]) for n in ("w_q0", "w_k0", "w_v0", "w_o0"))
        b_q0, b_k0, g2, be2 = (sb(n, [128, 1]) for n in ("b_q0", "b_k0", "g2", "be2"))
        bc_v0, bc_o0, bc_b2, bc_g3, bc_be3, bc_wo = (sb(n, [128, D]) for n in ("bc_v0", "bc_o0", "bc_b2", "bc_g3", "bc_be3", "bc_wo"))
        w_1 = sb("w_1", [128, FF])
        b_1 = sb("b_1", [128, NF])
        w_2 = sb("w_2", [128, NF, D])
        w_ga = sb("w_ga", [128, E + E * R])
        bc_gate = sb("bc_gate", [128, E])
        w_i = sb("w_i", [128, FF])
        b_i = sb("b_i", [128, NF])
        w_of = sb("w_of", [128, NF, D])
        lora_b = sb("lora_b", [128, FF])
        w_q1 = sb("w_q1", [128, HW])
        w_k1 = sb("w_k1", [128, HW])
        w_t1 = sb("w_t1", [128, HW])
        g_wo = sb("g_wo", [128, HP, D])
        w_qo = sb("w_qo", [128, D])
        bc_out1 = sb("bc_out1", [128, D])
        w_theta = sb("w_theta", [128, H])
        bc_tb = sb("bc_tb", [128, H])
        rate = sb("rate", [128, 1])
        gamma2 = sb("gamma2", [128, HW])
        gam_bet = sb("gam_bet", [128, HW])
        w_init = sb("w_init", [C, H, 2, HD])
        w_r, w_kf, w_vf = (sb(n, [128, D]) for n in ("w_r", "w_kf", "w_vf"))
        mu_r, mu_k = sb("mu_r", [128, 1]), sb("mu_k", [128, 1])
        mod_all = sb("mod_all", [128, 8, B])
        gate0 = sb("gate0", [128, B, 2, D])
        gate1 = sb("gate1", [128, PAIRS, 2, D])
        mod = sb("mod", [128, 8, 2])
        g_ab0 = sb("g_ab0", [128, 2, 2, D])
        g_ab1 = sb("g_ab1", [128, 2, D])
        gg3 = sb("gg3", [128, 2, 2, D])

        x = sb("x", [128, 2, T, D])
        L = []
        for u in range(2):
            tiles = sb(f"tiles{u}", [128, 6, N])
            rows_ = sb(f"feats{u}", [128, 8, 512])
            L.append(dict(
                tiles=tiles, feats=rows_,
                stats=sb(f"stats{u}", [128, T, 6]), mv=sb(f"mv{u}", [128, T, 2]), std=sb(f"std{u}", [128, T]),
                inv=sb(f"inv{u}", [128, T]), hat=tiles[:, 0, :].rearrange("p (t d) -> p t d", t=T), hT=tiles[:, 1, :],
                qT=tiles[:, 2, :], q2=tiles[:, 3, :], kT=tiles[:, 4, :], k2=tiles[:, 5, :],
                v=sb(f"v{u}", [128, T, D + 1]), qmax=sb(f"qmax{u}", [128, T, H0]), qb=sb(f"qb{u}", [128, N]),
                big=rows_[:, 0:4, :], ek=rows_[:, 4:8, :], kmax=sb(f"kmax{u}", [128, T, H0]),
                kmx=sb(f"kmx{u}", [128, H0]), stab=sb(f"stab{u}", [H0, 1]), sd=sb(f"sd{u}", [H0, H0]),
                ctx=sb(f"ctx{u}", [128, G, D + H0]), rden=sb(f"rden{u}", [128, T, H0]), y=sb(f"y{u}", [128, T, D]),
                lg=sb(f"lg{u}", [128, T, E]), lm=sb(f"lm{u}", [128, T]), eq=sb(f"eq{u}", [128, T, E]),
                um=sb(f"um{u}", [128, T, E * R]), umT=sb(f"umT{u}", [128, N]),
            ))

        xc = sb("xc", [128, NJ, D])
        h3 = sb("h3", [128, NJ, 2, K])
        w_sb = sb("w_sb", [C, H, 2, HD])
        kT1 = sb("keys1", [C, H, 2 * K])
        qT1 = sb("queries1", [C, H, 2 * K])
        k_tok = L[0]["tiles"][:, 1:5, :].rearrange("p (s a) b -> p s (a b)", s=2)
        k_sc = sb("k_sc", [128, H, C])
        t_tok = L[0]["feats"][:, 0:4, :].rearrange("p (s a) b -> p s (a b)", s=2)
        eta = sb("eta", [128, NJ, H])
        sq = L[0]["feats"][:, 4:6, :].rearrange("p a b -> p (a b)")
        ssum, zstd, zinv, scl = (sb(n, [128, H]) for n in ("ssum", "zstd", "zinv", "scl"))
        zhat = L[0]["feats"][:, 6:8, :].rearrange("p a b -> p (a b)")
        gbase = L[1]["feats"][:, 4:6, :].rearrange("p a b -> p (a b)")
        tmp = L[1]["feats"][:, 6:8, :].rearrange("p a b -> p (a b)")
        c12 = sb("c12", [128, 2, 2, HH])
        grad = sb("grad", [128, H, 2, HD])
        qsum, qstd, qinv = (sb(n, [128, H]) for n in ("qsum", "qstd", "qinv"))
        zT = L[1]["tiles"][:, 1:3, :].rearrange("p a (g t) -> p (a g) t", t=128)
        att1 = sb("att1", [128, 2, D])
        stats6, mv6 = sb("stats6", [128, NJ, 6]), sb("mv6", [128, NJ, 2])
        std6, inv6 = sb("std6", [128, NJ]), sb("inv6", [128, NJ])
        hat6 = sq[:, :].rearrange("p (j d) -> p j d", j=NJ)
        h4 = zhat[:, :].rearrange("p (j b t) -> p j b t", j=NJ, b=2)
        diff = gbase[:, :].rearrange("p (j b t) -> p j b t", j=NJ, b=2)
        mix_r, mix_k, kact = tmp[:, :], k_tok[:, 0, :], t_tok[:, 0, :]
        r_sb = t_tok[:, 1, :]
        zq_hat = L[1]["feats"][:, 0:2, :].rearrange("p a b -> p (a b)")
        sqq = L[1]["feats"][:, 2:4, :].rearrange("p a b -> p (a b)")
        s_wv = L[0]["big"][:, 0:2, :].rearrange("p a b -> p (a b)")
        s_gam = L[0]["big"][:, 2:4, :].rearrange("p a b -> p (a b)")
        s_bet = L[1]["big"][:, 0:2, :].rearrange("p a b -> p (a b)")
        s_the = L[1]["big"][:, 2:4, :].rearrange("p a b -> p (a b)")
        s_wqT = L[0]["ek"][:, 0:2, :].rearrange("p a b -> p (a b)").rearrange("p (g d) -> p g d", g=HP)
        s_wo = L[0]["ek"][:, 2:4, :].rearrange("p a b -> p (a b)").rearrange("p (g d) -> p g d", g=HP)
        s_bb = L[1]["ek"][:, 0:2, :].rearrange("p a b -> p (a b)").rearrange("p (g d) -> p g d", g=HP)
        s_w0 = L[1]["ek"][0:C, 2:4, :].rearrange("p a b -> p (a b)").rearrange("p (h d) -> p h d", h=H)
        wmod = [L[u]["tiles"][:, 0:3, :].rearrange("p a b -> p (a b)")[:, 0:6 * D] for u in range(2)]
        s_cT = sb("s_cT", [128, 2, B])
        s_sig = sb("s_sig", [128, 2, B])
        s_cb = L[0]["tiles"][:, 3:6, :].rearrange("p a b -> p (a b)")
        s_small = sb("s_small", [128, 48])

        names = [f"{n}_{u}" for n in PER_BATCH for u in range(2)] + PER_PAIR
        names += [f"filled_{i}" for i in range(8)] + [f"drained_{i}" for i in range(8)] + ["engines_done"]
        S = {n: new_sem(n) for n in names}
        numbers = [s.num for s in S.values()]
        assert numbers == list(range(numbers[0], numbers[0] + len(numbers)))
        go = {e: new_sem(f"go_{e}") for e in ("pe", "act", "dve", "sp")}
        weights_loaded = new_sem("weights_loaded")
        pool_set, dve_set, act_set, pe_set = (new_sem(n) for n in ("pool_set", "dve_set", "act_set", "pe_set"))
        set_step = new_sem("set_step")

        loads = [
            (ident[:, :], a["c_ident"]), (proj_bd[:, :], a["proj_tiled"]), (s_cb[:, 0:FEAT], a["c_proj_mask"]),
            (ctx_mask[:, :, :].rearrange("p g d -> p (g d)"), a["c_ctx_mask"]),
            (head_sel[:, :, :].rearrange("p g d -> p (g d)"), a["c_head_sel"]),
            (neg_sel[:, :], a["c_neg_sel"]), (half_square[:, :], a["c_half_square"]), (first[:, :], a["c_first"]),
            (s_small[:, 0:1], a["c_token_rate"]), (s_small[:, 1:2], a["alpha2"]),
            (w_q0[:, :], a["WqT"]), (w_k0[:, :], a["WkT"]), (w_v0[:, :], a["WvT"]), (w_o0[:, :], a["WoT"]),
            (b_q0[:, :], a["bq"]), (b_k0[:, :], a["bk"]), (g2[:, :], a["g2"]), (be2[:, :], a["be2"]),
            (w_1[:, :], a["W1T"]), (b_1[:, :], a["b1"]), (w_2[:, :, :], a["W2T"].rearrange("(g p) d -> p g d", p=128)),
            (w_ga[:, :], a["gate_lora_a"]), (w_i[:, :], a["wiT"]), (b_i[:, :], a["wi_b"]),
            (w_of[:, :, :], a["woT"].rearrange("(g p) d -> p g d", p=128)), (lora_b[:, :], a["lora_b"]),
            (w_q1[:, :], a["wq1"]), (w_k1[:, :], a["wk1"]), (s_wv, a["wv1"]),
            (s_wqT, a["wq1T"].rearrange("(g p) d -> p g d", p=128)), (s_wo, a["wo1"].rearrange("(g p) d -> p g d", p=128)),
            (s_w0[0:HD, :, :], a["W1c"]), (s_w0[HD:C, :, :], a["b1c"]),
            (s_small[:, 2:2 + HP], a["betaT"]), (s_small[:, 16:16 + HP], a["gammaT"]),
            (w_r[:, :], a["W_rT"]), (w_kf[:, :], a["W_kT"]), (w_vf[:, :], a["W_vT"]), (mu_r[:, :], a["mu_r"]), (mu_k[:, :], a["mu_k"]),
            (s_cT[:, 0, :], a["c0T"]), (s_cT[:, 1, :], a["c1T"]), (wmod[0][:, :], a["wmod0"]), (wmod[1][:, :], a["wmod1"]),
        ]
        for dst, name in ((bc_v0, "bv"), (bc_o0, "bo"), (bc_b2, "b2"), (bc_g3, "g3"), (bc_be3, "be3"), (bc_wo, "wo_b"),
                          (bc_gate, "gate_b"), (bc_tb, "theta_bias")):
            loads.append((dst[:, :], a[name].partition_broadcast(128)))
        for dst, name in ((s_gam, "gamma"), (s_bet, "beta"), (s_the, "theta")):
            loads.append((dst, a[name].partition_broadcast(128)))
        N_LOADS = len(loads)
        N_SETS = 10

        GATE_COLS = [2 * D, 5 * D]
        MOD_BLOCKS = [0, 1, 3, 4]
        x_dram = a["x"].rearrange("b (t p) d -> b p t d", p=128)
        out_dram = out.rearrange("b (j t) d -> b t j d", t=K)

        jobs = {}

        block = ctx.enter_context(nc.Block())

        @block.tensor
        def _(pe):
            count = [0] * 8
            mm = nc.tensor.matmul

            def begin(name, b):
                if count[b]:
                    pe.wait_ge(S[f"drained_{b}"], count[b])
                count[b] += 1
                jobs[name] = (b, count[b])

            def end(ins, b):
                ins.then_inc(S[f"filled_{b}"], 1)

            def ready(name):
                b, n = jobs[name]
                pe.wait_ge(S[f"drained_{b}"], n)

            pe.wait_ge(weights_loaded, 16 * N_LOADS)
            pe.wait_ge(dve_set, 1)
            for g in range(HP):
                mm(bank[0][:, 0:D], s_wqT[:, g, :], s_wo[:, g, :], start=(g == 0), stop=(g == HP - 1))
            for g in range(HP):
                mm(bank[1][:, 0:D], s_bb[:, g, :], s_wo[:, g, :], start=(g == 0), stop=(g == HP - 1))
            for l in range(2):
                for n, blk in enumerate(MOD_BLOCKS):
                    mm(bank[2][:, (4 * l + n) * B:(4 * l + n + 1) * B], wmod[l][:, blk * D:(blk + 1) * D],
                       s_sig[:, l, :], start=True, stop=True)
            cb = s_cb[:, :].rearrange("p (n m) -> p n m", m=128)
            for n in range(B + PAIRS):
                l = 0 if n < B else 1
                for k, col in enumerate(GATE_COLS):
                    last = mm(bank[4 + n % 4][:, k * D:(k + 1) * D], cb[:, n, :], wmod[l][:, col:col + D],
                              start=True, stop=True)
                last.then_inc(pe_set, 1)
                if n % 4 == 3 and n < B + PAIRS - 1:
                    pe.wait_ge(dve_set, 1 + n + 1)

            pe.wait_ge(pool_set, N_SETS)
            pe.wait_ge(dve_set, 2 + B + PAIRS)

            with pe.Fori(0, TRIPS) as _i:
                for b in range(8):
                    count[b] = 0

                def transposes(name, b, src, u, ready):
                    begin(name, b)
                    pe.wait_ge(S[f"{ready}_{u}"], 1)
                    for t in range(T):
                        last = nc.tensor.transpose(bank[b][:, t * 128:(t + 1) * 128], src[:, t, :], ident[:, :])
                    end(last, b)

                for u in range(2):
                    transposes(f"hT{u}", 4 * u, L[u]["hat"], u, "ln1_hat")
                for u in range(2):
                    l = L[u]
                    ready(f"hT{u}")
                    for n, (w, name) in enumerate(((w_q0, "qT"), (w_k0, "kT"))):
                        b = 4 * u + 1 + n
                        begin(f"{name}{u}", b)
                        end(mm(bank[b], w[:, :], l["hT"][:, :], start=True, stop=True), b)
                    b = 4 * u + 3
                    begin(f"v{u}", b)
                    for t in range(T):
                        last = mm(bank[b][:, t * D:(t + 1) * D], l["hT"][:, t * 128:(t + 1) * 128], w_v0[:, :], start=True, stop=True)
                    end(last, b)
                for name, src, sem in (("xq", "qT", 1), ("xk", "kT", 2)):
                    for u in range(2):
                        l = L[u]
                        ready(f"{src}{u}")
                        for t in range(T):
                            b = 4 * u + t
                            begin(f"{name}{u}{t}", b)
                            end(mm(bank[b], l[src][:, t * 128:(t + 1) * 128], proj_bd[:, :], start=True, stop=True), b)
                for u in range(2):
                    l, b = L[u], 4 * u
                    begin(f"qb{u}", b)
                    ready(f"xq{u}{T - 1}")
                    mm(bank[b][0:H0, :], half_square[:, :], l["q2"][:, :], start=True, stop=False)
                    for t in range(T):
                        last = mm(bank[b][0:H0, t * 128:(t + 1) * 128], l["qmax"][:, t, :], ident[:, :], start=False, stop=(t == T - 1))
                    end(last, b)
                    b = 4 * u + 1
                    begin(f"kmT{u}", b)
                    pe.wait_ge(S[f"k_max_ready_{u}"], 1)
                    end(nc.tensor.transpose(bank[b][0:H0, 0:128], l["kmx"][:, :], ident[:, :]), b)
                for u in range(2):
                    l = L[u]
                    ready(f"qb{u}")
                    for g in range(G):
                        b = 4 * u + (2 + g) % 4
                        begin(f"fq{u}{g}", b)
                        mm(bank[b], proj_bd[:, g * 128:(g + 1) * 128], l["qT"][:, :], start=True, stop=False)
                        end(mm(bank[b], neg_sel[:, g * 128:(g + 1) * 128], l["qb"][:, :], start=False, stop=True), b)
                for u in range(2):
                    l, b = L[u], 4 * u + 2
                    begin(f"kb{u}", b)
                    pe.wait_ge(S[f"k_stab_ready_{u}"], 1)
                    for t in range(T):
                        o = bank[b][:, t * H0:(t + 1) * H0]
                        mm(o, l["k2"][:, t * 128:(t + 1) * 128], half_square[:, :], start=True, stop=False)
                        last = mm(o, ones[0:H0, :], l["sd"][:, :], start=False, stop=True)
                    end(last, b)
                for u in range(2):
                    l = L[u]
                    pe.wait_ge(S[f"k_feat_ready_{u}"], T)
                    ready(f"v{u}")
                    for half in range(2):
                        b = 4 * u + half
                        begin(f"ctx{u}{half}", b)
                        for g in (2 * half, 2 * half + 1):
                            for t in range(T):
                                last = mm(bank[b][:, (g % 2) * 256:(g % 2) * 256 + D + 1], l["ek"][:, t, g * 128:(g + 1) * 128],
                                          l["v"][:, t, :], start=(t == 0), stop=(t == T - 1))
                        end(last, b)
                for u in range(2):
                    l = L[u]
                    pe.wait_ge(S[f"q_feat_ready_{u}"], G)
                    ready(f"ctx{u}0")
                    ready(f"ctx{u}1")
                    for half in range(2):
                        b = 4 * u + 2 + half
                        begin(f"num{u}{half}", b)
                        for t in (2 * half, 2 * half + 1):
                            for g in range(G):
                                last = mm(bank[b][:, (t % 2) * 256:(t % 2) * 256 + D + H0], l["big"][:, g, t * 128:(t + 1) * 128],
                                          l["ctx"][:, g, :], start=(g == 0), stop=(g == G - 1))
                        end(last, b)
                for u in range(2):
                    l, b = L[u], 4 * u
                    begin(f"attnT{u}", b)
                    ready(f"num{u}0")
                    ready(f"num{u}1")
                    for t in range(T):
                        last = nc.tensor.transpose(bank[b][:, t * 128:(t + 1) * 128], l["y"][:, t, :], ident[:, :])
                    end(last, b)
                for u in range(2):
                    l, b = L[u], 4 * u + 1
                    begin(f"y1{u}", b)
                    ready(f"attnT{u}")
                    for t in range(T):
                        o = bank[b][:, t * D:(t + 1) * D]
                        mm(o, l["q2"][:, t * 128:(t + 1) * 128], w_o0[:, :], start=True, stop=False)
                        last = mm(o, l["hT"][:, t * 128:(t + 1) * 128], ident[:, :], start=False, stop=True)
                    end(last, b)
                for u in range(2):
                    transposes(f"x1T{u}", 4 * u, L[u]["hat"], u, "ln2_hat")
                for u in range(2):
                    l = L[u]
                    ready(f"x1T{u}")
                    for f in range(NF):
                        b = 4 * u + (2 + f) % 4
                        begin(f"f1{u}{f}", b)
                        end(mm(bank[b], w_1[:, f * 128:(f + 1) * 128], l["kT"][:, :], start=True, stop=True), b)
                for u in range(2):
                    l, b = L[u], 4 * u + 2
                    begin(f"y2{u}", b)
                    for f in range(NF):
                        ready(f"f1{u}{f}")
                    for t in range(T):
                        o = bank[b][:, t * D:(t + 1) * D]
                        for f in range(NF):
                            mm(o, l["big"][:, f, t * 128:(t + 1) * 128], w_2[:, f, :], start=(f == 0), stop=False)
                        last = mm(o, l["kT"][:, t * 128:(t + 1) * 128], ident[:, :], start=False, stop=True)
                    end(last, b)
                for u in range(2):
                    transposes(f"h2T{u}", 4 * u, L[u]["hat"], u, "ln4_hat")
                for u in range(2):
                    l, b = L[u], 4 * u + 1
                    ready(f"h2T{u}")
                    begin(f"gate{u}", b)
                    for t in range(T):
                        last = mm(bank[b][:, t * 40:(t + 1) * 40], l["hT"][:, t * 128:(t + 1) * 128], w_ga[:, :], start=True, stop=True)
                    end(last, b)
                for u in range(2):
                    l, b = L[u], 4 * u
                    begin(f"umT{u}", b)
                    ready(f"gate{u}")
                    for t in range(T):
                        last = nc.tensor.transpose(bank[b][0:E * R, t * 128:(t + 1) * 128], l["um"][:, t, :], ident[:, :])
                    end(last, b)
                for u in range(2):
                    l = L[u]
                    ready(f"umT{u}")
                    for f in range(NF):
                        b = 4 * u + (1 + f) % 4
                        begin(f"f2{u}{f}", b)
                        mm(bank[b], w_i[:, f * 128:(f + 1) * 128], l["hT"][:, :], start=True, stop=False)
                        end(mm(bank[b], lora_b[:, f * 128:(f + 1) * 128], l["umT"][:, :], start=False, stop=True), b)
                for u in range(2):
                    l, b = L[u], 4 * u + 1
                    begin(f"y3{u}", b)
                    for f in range(NF):
                        ready(f"f2{u}{f}")
                    for t in range(T):
                        for f in range(NF):
                            last = mm(bank[b][:, t * D:(t + 1) * D], l["big"][:, f, t * 128:(t + 1) * 128], w_of[:, f, :],
                                      start=(f == 0), stop=(f == NF - 1))
                    end(last, b)
                for u in range(2):
                    transposes(f"h3T{u}", 4 * u, L[u]["hat"], u, "ln5_hat")

                def chunk(j):
                    return h3[:, j, :, :].rearrange("p b t -> p (b t)")

                ring = [0]

                def begin_ring(name):
                    b = 6 + ring[0] % 2
                    ring[0] += 1
                    begin(name, b)
                    return b

                def rows(name, w, j, f):
                    b = begin_ring(f"{name}{j}{f}")
                    end(mm(bank[b], chunk(j), w[:, f * HALF:(f + 1) * HALF], start=True, stop=True), b)

                def turned(name, src, f, wait):
                    b = begin_ring(name)
                    ready(wait)
                    for g in range(4 * f, 4 * f + 4):
                        last = nc.tensor.transpose(bank[b][:, (g % 4) * 128:(g % 4 + 1) * 128], src[:, g * 128:(g + 1) * 128], ident[:, :])
                    end(last, b)

                def predict(name, src, f):
                    b = 4 + f
                    for h in range(HH * f, HH * (f + 1)):
                        for c in range(2):
                            last = mm(bank[b][64 * c:64 * c + 64, (h % HH) * HD:(h % HH + 1) * HD],
                                      src[:, h, 64 * c:64 * c + 64], w_sb[:, h, c, :], start=True, stop=True)
                    end(last, b)

                for u in range(2):
                    ready(f"h3T{u}")
                for n in range(4):
                    begin(f"w{n}", n)
                    end(mm(bank[n][0:C, :], ident[0:C, 0:C],
                           w_init[:, 4 * n:4 * n + 4, :, :].rearrange("p h b d -> p (h b d)"), start=True, stop=True,
                           skip_group_check=True), n)
                begin("rate", 5)
                for j in range(NJ):
                    last = mm(bank[5][:, j * H:(j + 1) * H], chunk(j), w_theta[:, :], start=True, stop=True)
                end(last, 5)
                for f in range(2):
                    rows("k1_", w_k1, 0, f)
                    rows("t1_", w_t1, 0, f)
                    turned(f"kT1_0{f}", k_tok[:, 0, :], f, f"k1_0{f}")
                for s in range(2 * NJ + 4):
                    j, f = divmod(s, 2)
                    jq, fq = divmod(s - 1, 2)
                    jo, fo = divmod(s - 2, 2)
                    if j < NJ:
                        begin(f"z{j}{f}", 4 + f)
                        pe.wait_ge(S["w_ready"], s + 1)
                        ready(f"kT1_{j}{f}")
                        predict("z", kT1, f)
                    if 0 <= jq < NJ - 1:
                        turned(f"kT1_{jq + 1}{fq}", k_tok[:, (jq + 1) % 2, :], fq, f"k1_{jq + 1}{fq}")
                    if 1 <= jq <= NJ:
                        begin(f"zq{jq - 1}{fq}", 4 + fq)
                        pe.wait_ge(S["w_ready"], s)
                        ready(f"qT1_{jq - 1}{fq}")
                        predict("zq", qT1, fq)
                    if j + 1 < NJ:
                        rows("t1_", w_t1, j + 1, f)
                    if 0 <= jq < NJ:
                        b = begin_ring(f"qT1_{jq}{fq}")
                        for g in range(4 * fq, 4 * fq + 4):
                            last = mm(bank[b][:, (g % 4) * 128:(g % 4 + 1) * 128], w_q1[:, g * 128:(g + 1) * 128], chunk(jq), start=True, stop=True)
                        end(last, b)
                        pe.wait_ge(S["k_scaled"], s)
                        pe.wait_ge(S["grad_top"], s)
                        pe.wait_ge(S["grad_bot"], s)
                        for h in range(HH * fq, HH * (fq + 1)):
                            last = mm(bank[h // 4][0:C, (h % 4) * 128:(h % 4 + 1) * 128], k_sc[:, h, :],
                                      grad[:, h, :, :].rearrange("p b d -> p (b d)"), start=False, stop=(h % 4 == 3),
                                      skip_group_check=True)
                        last.then_inc(S["dw_done"], 1)
                    if 1 <= jo <= NJ:
                        turned(f"zT{jo - 1}{fo}", zq_hat, fo, f"zq{jo - 1}{fo}")
                    if j + 1 < NJ:
                        rows("k1_", w_k1, j + 1, f)
                    if 1 <= jo <= NJ and fo == 1:
                        b = begin_ring(f"o{jo - 1}")
                        ready(f"zT{jo - 1}0")
                        ready(f"zT{jo - 1}1")
                        mm(bank[b][:, 0:D], chunk(jo - 1), w_qo[:, :], start=True, stop=False)
                        for g in range(HP):
                            last = mm(bank[b][:, 0:D], zT[:, g, :], g_wo[:, g, :], start=False, stop=(g == HP - 1))
                        end(last, b)

                for half in range(2):
                    b = half
                    begin(f"h4{half}", b + 4)
                    pe.wait_ge(S["ln6_hat"], 1)
                    for t in range(4):
                        last = nc.tensor.transpose(bank[b + 4][:, t * 128:(t + 1) * 128], hat6[:, 4 * half + t, :], ident[:, :])
                    end(last, b + 4)
                pe.wait_ge(S["mix_ready"], 2)
                for half in range(2):
                    b = 6 + half
                    begin(f"key{half}", b)
                    end(mm(bank[b], w_kf[:, :], mix_k[:, half * 512:(half + 1) * 512], start=True, stop=True), b)
                for half in range(2):
                    b = 4 + half
                    begin(f"r{half}", b)
                    for t in range(4):
                        j = 4 * half + t
                        last = mm(bank[b][:, t * D:(t + 1) * D], mix_r[:, j * 128:(j + 1) * 128], w_r[:, :], start=True, stop=True)
                    end(last, b)
                for half in range(2):
                    b = 6 + half
                    begin(f"val{half}", b)
                    pe.wait_ge(S["key_ready"], half + 1)
                    for t in range(4):
                        j = 4 * half + t
                        last = mm(bank[b][:, t * D:(t + 1) * D], kact[:, j * 128:(j + 1) * 128], w_vf[:, :], start=True, stop=True)
                    end(last, b)
                pe.drain().then_inc(S["engines_done"], 1)
                pe.wait_ge(go["pe"], 1)
                pe.sem_clear(go["pe"])

        def filled(eng, name):
            b, n = jobs[name]
            eng.wait_ge(S[f"filled_{b}"], n)
            return bank[b]

        def drained(name):
            return S[f"drained_{jobs[name][0]}"]

        def ready(eng, name):
            b, n = jobs[name]
            eng.wait_ge(S[f"drained_{b}"], n)

        @block.scalar
        def _(act):
            act.wait_ge(weights_loaded, 16 * N_LOADS)
            nc.scalar.activation(s_sig[:, :, :], s_cT[:, :, :], ACT.Sigmoid).then_inc(act_set, 1)
            act.wait_ge(dve_set, 2 + B + PAIRS)

            with act.Fori(0, TRIPS) as _i:
                def root(name, src, dst, u=None, scale=1.0, eps=LN_EPS):
                    key = name if u is None else f"{name}_{u}"
                    nc.scalar.activation(dst, src, ACT.Sqrt, bias=eps, scale=scale).then_inc(S[key], 1)

                def modulated(name, dst, shift, scl_):
                    src = filled(act, name)
                    nc.scalar.activation(dst, src, ACT.Identity, bias=shift, scale=scl_)\
                       .then_inc(drained(name), 1)

                act.wait_ge(S["mods_ready"], 1)
                for u in range(2):
                    act.wait_ge(S[f"ln1_var_{u}"], 1)
                    root("ln1_std", L[u]["mv"][:, :, 1], L[u]["std"][:, :], u)
                for u in range(2):
                    modulated(f"hT{u}", L[u]["hT"][:, :], mod[:, 0, u:u + 1], mod[:, 1, u:u + 1])
                for u in range(2):
                    l = L[u]
                    for name, dst, dst2, bias in (("qT", "qT", "q2", b_q0), ("kT", "kT", "k2", b_k0)):
                        src = filled(act, f"{name}{u}")
                        nc.scalar.activation(l[dst][:, :], src, ACT.Identity, bias=bias[:, :])
                        nc.scalar.activation(l[dst2][:, :], src, ACT.Square, bias=bias[:, :]).then_inc(drained(f"{name}{u}"), 1)
                for u in range(2):
                    for t in range(T):
                        src = filled(act, f"xk{u}{t}")
                        nc.scalar.copy(L[u]["ek"][:, t, :], src).then_inc(drained(f"xk{u}{t}"), 1)
                for u in range(2):
                    src = filled(act, f"qb{u}")
                    nc.scalar.copy(L[u]["qb"][0:H0, :], src[0:H0, :]).then_inc(drained(f"qb{u}"), 1)
                for u in range(2):
                    for g in range(G):
                        src = filled(act, f"fq{u}{g}")
                        nc.scalar.activation(L[u]["big"][:, g, :], src, ACT.Exp).then_inc(drained(f"fq{u}{g}"), 1)
                for u in range(2):
                    for t in range(T):
                        act.wait_ge(S[f"k_shifted_{u}"], t + 1)
                        nc.scalar.activation(L[u]["ek"][:, t, :], L[u]["ek"][:, t, :], ACT.Exp).then_inc(S[f"k_exp_{u}"], 1)
                for u in range(2):
                    src = filled(act, f"attnT{u}")
                    nc.scalar.copy(L[u]["q2"][:, :], src).then_inc(drained(f"attnT{u}"), 1)
                for u in range(2):
                    act.wait_ge(S[f"ln2_var_{u}"], 1)
                    root("ln2_std", L[u]["mv"][:, :, 1], L[u]["std"][:, :], u)
                for u in range(2):
                    modulated(f"x1T{u}", L[u]["kT"][:, :], be2[:, :], g2[:, :])
                for u in range(2):
                    for f in range(NF):
                        src = filled(act, f"f1{u}{f}")
                        nc.scalar.activation(L[u]["big"][:, f, :], src, ACT.Relu, bias=b_1[:, f:f + 1]).then_inc(drained(f"f1{u}{f}"), 1)
                for u in range(2):
                    act.wait_ge(S[f"ln3_var_{u}"], 1)
                    root("ln3_std", L[u]["mv"][:, :, 1], L[u]["std"][:, :], u)
                for u in range(2):
                    act.wait_ge(S[f"ln4_var_{u}"], 1)
                    root("ln4_std", L[u]["mv"][:, :, 1], L[u]["std"][:, :], u)
                for u in range(2):
                    modulated(f"h2T{u}", L[u]["hT"][:, :], mod[:, 2, u:u + 1], mod[:, 3, u:u + 1])
                for u in range(2):
                    src = filled(act, f"umT{u}")
                    nc.scalar.copy(L[u]["umT"][0:E * R, :], src[0:E * R, :]).then_inc(drained(f"umT{u}"), 1)
                for u in range(2):
                    for f in range(NF):
                        src = filled(act, f"f2{u}{f}")
                        nc.scalar.activation(L[u]["big"][:, f, :], src, ACT.Relu, bias=b_i[:, f:f + 1]).then_inc(drained(f"f2{u}{f}"), 1)
                for u in range(2):
                    act.wait_ge(S[f"ln5_var_{u}"], 1)
                    root("ln5_std", L[u]["mv"][:, :, 1], L[u]["std"][:, :], u)
                for u in range(2):
                    src = filled(act, f"h3T{u}")
                    nc.scalar.activation(h3[:, :, u, :], src.rearrange("p (j t) -> p j t", j=NJ), ACT.Identity,
                                         bias=mod[:, 4, u:u + 1], scale=mod[:, 5, u:u + 1]).then_inc(drained(f"h3T{u}"), 1)

                ready(act, "rate")
                nc.scalar.activation(eta[:, :, :], eta[:, :, :], ACT.Sigmoid).then_inc(S["rate_sig"], 1)

                def state(half):
                    nc.scalar.copy(w_sb[:, HH * half:HH * (half + 1), :, :].rearrange("p h b d -> p (h b d)"),
                                   ps[0:C, 2 * half:2 * half + 2, :].rearrange("p a c -> p (a c)")).then_inc(S["w_ready"], 1)

                for half in range(2):
                    for n in (2 * half, 2 * half + 1):
                        filled(act, f"w{n}")
                    state(half)

                def split_heads(key, dst, f):
                    src = filled(act, key).rearrange("p (g t) -> p g t", g=4)
                    d = dst[0:HD, HH * f:HH * (f + 1), :].rearrange("p (g e) t -> p g e t", e=2)
                    nc.scalar.copy(d[:, :, 0, :], src[0:HD])
                    nc.scalar.copy(d[:, :, 1, :], src[HD:128]).then_inc(drained(key), 1)

                def key_rows(j, f):
                    src = filled(act, f"k1_{j}{f}")
                    if j >= 2:
                        act.wait_ge(S["k_scaled"], 2 * (j - 2) + f + 1)
                    nc.scalar.copy(k_tok[:, j % 2, f * HALF:(f + 1) * HALF], src).then_inc(drained(f"k1_{j}{f}"), 1)

                def target_rows(j, f):
                    src = filled(act, f"t1_{j}{f}")
                    if j >= 2:
                        act.wait_ge(S["grad_base"], 2 * (j - 2) + f + 1)
                    nc.scalar.copy(t_tok[:, j % 2, f * HALF:(f + 1) * HALF], src).then_inc(drained(f"t1_{j}{f}"), 1)

                def spread(sem_in, n, dst, src, sem_out):
                    act.wait_ge(S[sem_in], n)
                    nc.scalar.activation(dst, src, ACT.Sqrt, bias=TTT_EPS, scale=1.0 / HD).then_inc(S[sem_out], 1)

                for f in range(2):
                    key_rows(0, f)
                    target_rows(0, f)
                    split_heads(f"kT1_0{f}", kT1, f)
                for s in range(2 * NJ + 4):
                    j, f = divmod(s, 2)
                    jq, fq = divmod(s - 1, 2)
                    jo, fo = divmod(s - 2, 2)
                    if j < NJ:
                        src = filled(act, f"z{j}{f}")
                        nc.scalar.activation(sq[:, f * HALF:(f + 1) * HALF], src, ACT.Square).then_inc(S["z_squared"], 1)
                        spread("z_var", s + 1, zstd[:, HH * f:HH * (f + 1)], ssum[:, HH * f:HH * (f + 1)], "z_std")
                    if 0 <= jq < NJ - 1:
                        split_heads(f"kT1_{jq + 1}{fq}", kT1, fq)
                    if 1 <= jq <= NJ:
                        src = filled(act, f"zq{jq - 1}{fq}")
                        nc.scalar.activation(sqq[:, fq * HALF:(fq + 1) * HALF], src, ACT.Square).then_inc(S["zq_squared"], 1)
                    if 1 <= jq <= NJ:
                        spread("zq_var", s - 2, qstd[:, HH * fq:HH * (fq + 1)], qsum[:, HH * fq:HH * (fq + 1)], "zq_std")
                    if j + 1 < NJ:
                        target_rows(j + 1, f)
                    if 0 <= jq < NJ:
                        split_heads(f"qT1_{jq}{fq}", qT1, fq)
                        act.wait_ge(S["dw_done"], s)
                        state(fq)
                    if 1 <= jo <= NJ:
                        if jo >= 2:
                            filled(act, f"o{jo - 2}")
                        src = filled(act, f"zT{jo - 1}{fo}")
                        nc.scalar.copy(zT[:, 4 * fo:4 * fo + 4, :].rearrange("p g t -> p (g t)"), src).then_inc(drained(f"zT{jo - 1}{fo}"), 1)
                    if j + 1 < NJ:
                        key_rows(j + 1, f)
                    if 1 <= jo <= NJ and fo == 1:
                        src = filled(act, f"o{jo - 1}")
                        if jo >= 3:
                            act.wait_ge(S["x_ttt"], jo - 2)
                        nc.scalar.copy(att1[:, jo % 2, :], src[:, 0:D]).then_inc(drained(f"o{jo - 1}"), 1)
                act.wait_ge(S["ln6_var"], 1)
                nc.scalar.activation(std6[:, :], mv6[:, :, 1], ACT.Sqrt, bias=LN_EPS).then_inc(S["ln6_std"], 1)
                for half in range(2):
                    src = filled(act, f"h4{half}").rearrange("p (j b t) -> p j b t", j=4, b=2)
                    nc.scalar.activation(h4[:, 4 * half:4 * half + 4, 0, :], src[:, :, 0, :], ACT.Identity,
                                         bias=mod[:, 6, 0:1], scale=mod[:, 7, 0:1])
                    nc.scalar.activation(h4[:, 4 * half:4 * half + 4, 1, :], src[:, :, 1, :], ACT.Identity,
                                         bias=mod[:, 6, 1:2], scale=mod[:, 7, 1:2]).then_inc(drained(f"h4{half}"), 1)
                for half in range(2):
                    src = filled(act, f"key{half}")
                    d = kact[:, half * 512:(half + 1) * 512]
                    nc.scalar.activation(d, src, ACT.Relu).then_inc(drained(f"key{half}"), 1)
                    act.wait_ge(drained(f"key{half}"), jobs[f"key{half}"][1])
                    nc.scalar.activation(d, d, ACT.Square).then_inc(S["key_ready"], 1)
                for half in range(2):
                    src = filled(act, f"r{half}")
                    nc.scalar.activation(r_sb[:, half * 512:(half + 1) * 512], src, ACT.Sigmoid).then_inc(drained(f"r{half}"), 1)
                act.drain().then_inc(S["engines_done"], 1)
                act.wait_ge(go["act"], 1)
                act.sem_clear(go["act"])

        @block.vector
        def _(dve):
            V = nc.vector
            steps = [0]

            def step(ins, sem):
                steps[0] += 1
                ins.then_inc(sem, 1)
                return steps[0]

            def link0(ins):
                dve.wait_ge(set_step, step(ins, set_step))

            dve.wait_ge(weights_loaded, 16 * N_LOADS)
            dve.wait_ge(act_set, 1)
            link0(V.tensor_tensor(proj_bd[:, :], proj_bd[:, :], s_cb[:, 0:FEAT], ALU.mult))
            link0(V.tensor_tensor(s_sig[:, :, :], s_cT[:, :, :], s_sig[:, :, :], ALU.mult))
            cb = s_cb[:, :].rearrange("p (n m) -> p n m", m=128)
            for n in range(B):
                V.tensor_copy(cb[:, n, :], s_sig[:, 0, n:n + 1].broadcast_to([128, 128]))
            for n in range(B):
                V.tensor_copy(cb[:, B + n // 2, 64 * (n % 2):64 * (n % 2) + 64], s_sig[:, 1, n:n + 1].broadcast_to([128, 64]))
            for g in range(HP):
                last = V.tensor_copy(s_bb[:, g, :], s_small[:, 2 + g:3 + g].broadcast_to([128, 128]))
            last.then_inc(dve_set, 1)
            for n in range(B + PAIRS):
                dst = gate0[:, n, :, :] if n < B else gate1[:, n - B, :, :]
                dve.wait_ge(pe_set, n + 1)
                V.tensor_copy(dst.rearrange("p k d -> p (k d)"), bank[4 + n % 4][:, 0:2 * D]).then_inc(dve_set, 1)
            dve.wait_ge(dve_set, 1 + B + PAIRS)
            for gate, n, s_g, m_g in ((gate0, B, L[0]["ek"], L[1]["ek"]), (gate1, PAIRS, L[0]["ek"], L[1]["ek"])):
                gv = gate[:, :, :, :].rearrange("p n k d -> p (n k d)")
                sg = s_g[:, :, :].rearrange("p a b -> p (a b)")[:, 0:n * 2 * D]
                mg = m_g[:, :, :].rearrange("p a b -> p (a b)")[:, 0:n * 2 * D]
                if gate is gate0:
                    link0(V.tensor_reduce(s_small[0:C, 32:48], s_w0, AX, ALU.add))
                    link0(V.tensor_scalar(s_small[0:C, 32:48], s_small[0:C, 32:48], 1.0 / HD, None, ALU.mult))
                    for b in range(2):
                        V.tensor_tensor(w_init[:, :, b, :], s_w0, s_small[0:C, 32:48].unsqueeze(2).broadcast_to([C, H, HD]), ALU.subtract)
                    for g in range(HP):
                        V.tensor_scalar(g_wo[:, g, :], s_wo[:, g, :], s_small[:, 16 + g:17 + g], None, ALU.mult)
                    link0(V.tensor_copy(w_qo[:, :], bank[0][:, 0:D]))
                link0(V.tensor_scalar(sg, gv, 0.0, 2.0, ALU.is_ge, ALU.mult))
                link0(V.tensor_scalar(mg, gv, -1.0, None, ALU.mult))
                link0(V.tensor_tensor(mg, mg, gv, ALU.max))
                link0(V.tensor_scalar(mg, mg, 0.25, None, ALU.max))
                link0(V.scalar_tensor_tensor(gv, sg, -1.0, mg, ALU.add, ALU.mult))
            V.tensor_copy(bc_out1[:, :], bank[1][:, 0:D])
            link0(V.tensor_copy(mod_all[:, :, :].rearrange("p k b -> p (k b)"), bank[2][:, 0:8 * B]))
            mp = mod_all[:, :, :].rearrange("p (k two) b -> p k two b", two=2)
            V.tensor_scalar(mp[:, :, 1, :], mp[:, :, 1, :], 1.0, None, ALU.add)
            link0(V.tensor_tensor(w_t1[:, :], w_k1[:, :], s_wv, ALU.subtract))
            V.tensor_tensor(w_t1[:, :], w_t1[:, :], s_gam, ALU.mult)
            V.tensor_tensor(gamma2[:, :], s_gam, s_gam, ALU.mult)
            V.tensor_tensor(gam_bet[:, :], s_gam, s_bet, ALU.mult)
            link0(V.tensor_tensor(tmp[:, :], w_k1[:, :], s_the, ALU.mult))
            V.tensor_reduce(w_theta[:, :], tmp[:, :].rearrange("p (h d) -> p h d", h=H), AX, ALU.add)
            link0(V.tensor_tensor(rate[:, :], s_small[:, 0:1], s_small[:, 1:2], ALU.add))
            link0(V.tensor_scalar(rate[:, :], rate[:, :], 0.0, -1.0 / HD, ALU.max, ALU.mult))
            V.tensor_scalar(mu_r[:, :], mu_r[:, :], -1.0, None, ALU.add)
            V.tensor_scalar(mu_k[:, :], mu_k[:, :], -1.0, None, ALU.add).then_inc(dve_set, 1)
            dve.wait_ge(dve_set, 2 + B + PAIRS)
            dve.wait_ge(pool_set, N_SETS)

            with dve.Fori(0, TRIPS) as i:
                steps[0] = 0

                def go_on(ins):
                    return step(ins, S["dve_step"])

                def settled(n):
                    dve.wait_ge(S["dve_step"], n)

                def link(ins):
                    settled(go_on(ins))

                def over(ap, n):
                    return ap.unsqueeze(1).broadcast_to([128, n, D])

                V.tensor_copy(g_ab0[:, :, :, :].rearrange("p b k d -> p (b k d)"),
                              gate0[:, bass.ds(2 * i, 2), :, :].rearrange("p b k d -> p (b k d)"))
                V.tensor_copy(g_ab1[:, :, :].rearrange("p k d -> p (k d)"),
                              gate1[:, bass.ds(i, 1), :, :].rearrange("p b k d -> p (b k d)"))
                V.tensor_copy(mod[:, :, :], mod_all[:, :, bass.ds(2 * i, 2)]).then_inc(S["mods_ready"], 1)
                dve.wait_ge(S["mods_ready"], 1)
                for u in range(2):
                    V.tensor_tensor(gg3[:, u, 0, :], g_ab0[:, u, 0, :], bc_g3[:, :], ALU.mult)
                    go_on(V.tensor_tensor(gg3[:, u, 1, :], g_ab0[:, u, 0, :], bc_be3[:, :], ALU.mult))

                def norm_stats(name, u, src):
                    l = L[u]
                    for t in range(T):
                        n = go_on(V.bn_stats(l["stats"][:, t, :], src[:, t, :]))
                    settled(n)
                    for t in range(T):
                        last = V.bn_aggr(l["mv"][:, t, :], l["stats"][:, t, :])
                    last.then_inc(S[f"{name}_var_{u}"], 1)

                def norm_apply(name, u, src):
                    l = L[u]
                    dve.wait_ge(S[f"{name}_std_{u}"], 1)
                    link(V.reciprocal(l["inv"][:, :], l["std"][:, :]))
                    for t in range(T):
                        last = V.tensor_scalar(l["hat"][:, t, :], src[:, t, :], l["mv"][:, t, 0:1], l["inv"][:, t:t + 1],
                                               ALU.subtract, ALU.mult)
                    last.then_inc(S[f"{name}_hat_{u}"], 1)

                for u in range(2):
                    dve.wait_ge(S[f"x_loaded_{u}"], 16)
                    norm_stats("ln1", u, x[:, u, :, :])
                for u in range(2):
                    norm_apply("ln1", u, x[:, u, :, :])
                for u in range(2):
                    src = filled(dve, f"v{u}").rearrange("p (t d) -> p t d", t=T)
                    V.tensor_tensor(L[u]["v"][:, :, 0:D], src, over(bc_v0[:, :], T), ALU.add).then_inc(drained(f"v{u}"), 1)
                for u in range(2):
                    for t in range(T):
                        src = filled(dve, f"xq{u}{t}").rearrange("p (h m) -> p h m", h=H0)
                        V.tensor_reduce(L[u]["qmax"][:, t, :], src, AX, ALU.max).then_inc(drained(f"xq{u}{t}"), 1)
                for u in range(2):
                    l = L[u]
                    for t in range(T):
                        ready(dve, f"xk{u}{t}")
                        n = go_on(V.tensor_reduce(l["kmax"][:, t, :], l["ek"][:, t, :].rearrange("p (h m) -> p h m", h=H0), AX, ALU.max))
                    settled(n)
                    V.tensor_reduce(l["kmx"][:, :], l["kmax"][:, :, :].rearrange("p t h -> p h t"), AX, ALU.max).then_inc(S[f"k_max_ready_{u}"], 1)
                for u in range(2):
                    l = L[u]
                    src = filled(dve, f"kmT{u}")
                    V.tensor_reduce(l["stab"][:, :], src[0:H0, 0:128], AX, ALU.max).then_inc(drained(f"kmT{u}"), 1)
                    ready(dve, f"kmT{u}")
                    V.tensor_scalar(l["sd"][:, :], ident[0:H0, 0:H0], l["stab"][:, :], None, ALU.mult).then_inc(S[f"k_stab_ready_{u}"], 1)
                for u in range(2):
                    l = L[u]
                    src = filled(dve, f"kb{u}")
                    V.tensor_copy(l["kmax"][:, :, :].rearrange("p t h -> p (t h)"), src[:, 0:T * H0]).then_inc(drained(f"kb{u}"), 1)
                    ready(dve, f"kb{u}")
                    for t in range(T):
                        e = l["ek"][:, t, :].rearrange("p (h m) -> p h m", h=H0)
                        V.tensor_tensor(e, e, l["kmax"][:, t, :].unsqueeze(2).broadcast_to([128, H0, M]), ALU.subtract)\
                         .then_inc(S[f"k_shifted_{u}"], 1)
                for u in range(2):
                    for g in range(G):
                        ready(dve, f"fq{u}{g}")
                        V.tensor_scalar(L[u]["big"][:, g, :], L[u]["big"][:, g, :], EPS_K, None, ALU.add).then_inc(S[f"q_feat_ready_{u}"], 1)
                for u in range(2):
                    for t in range(T):
                        dve.wait_ge(S[f"k_exp_{u}"], t + 1)
                        V.tensor_scalar(L[u]["ek"][:, t, :], L[u]["ek"][:, t, :], EPS_K, None, ALU.add).then_inc(S[f"k_feat_ready_{u}"], 1)
                for u in range(2):
                    l = L[u]
                    for half in range(2):
                        src = filled(dve, f"ctx{u}{half}")
                        for g in (2 * half, 2 * half + 1):
                            o = (g % 2) * 256
                            V.tensor_tensor(l["ctx"][:, g, 0:D], src[:, o:o + D], ctx_mask[:, g, :], ALU.mult)
                            last = V.tensor_scalar(l["ctx"][:, g, D:D + H0], head_sel[:, g, :], src[:, o + D:o + D + 1], None, ALU.mult)
                        last.then_inc(drained(f"ctx{u}{half}"), 1)
                for u in range(2):
                    l = L[u]
                    for half in range(2):
                        src = filled(dve, f"num{u}{half}").rearrange("p (t c) -> p t c", t=2)
                        link(V.reciprocal(l["rden"][:, 2 * half:2 * half + 2, :], src[:, :, D:D + H0]))
                        for t in (2 * half, 2 * half + 1):
                            last = V.tensor_tensor(l["y"][:, t, :].rearrange("p (h d) -> p h d", h=H0),
                                                   src[:, t % 2, 0:D].rearrange("p (h d) -> p h d", h=H0),
                                                   l["rden"][:, t, :].unsqueeze(2).broadcast_to([128, H0, DH]), ALU.mult)
                        last.then_inc(drained(f"num{u}{half}"), 1)

                def add_row(name, u, row):
                    src = filled(dve, f"{name}{u}").rearrange("p (t d) -> p t d", t=T)
                    V.tensor_tensor(L[u]["y"][:, :, :], src, over(row[:, :], T), ALU.add).then_inc(drained(f"{name}{u}"), 1)
                    ready(dve, f"{name}{u}")

                for u in range(2):
                    add_row("y1", u, bc_o0)
                    norm_stats("ln2", u, L[u]["y"])
                for u in range(2):
                    norm_apply("ln2", u, L[u]["y"])
                for u in range(2):
                    add_row("y2", u, bc_b2)
                    norm_stats("ln3", u, L[u]["y"])
                for u in range(2):
                    l = L[u]
                    norm_apply("ln3", u, l["y"])
                    dve.wait_ge(S[f"ln3_hat_{u}"], 1)
                    link(V.tensor_tensor(l["y"][:, :, :], l["hat"][:, :, :], over(gg3[:, u, 0, :], T), ALU.mult))
                    link(V.tensor_tensor(x[:, u, :, :], x[:, u, :, :], l["y"][:, :, :], ALU.add))
                    link(V.tensor_tensor(x[:, u, :, :], x[:, u, :, :], over(gg3[:, u, 1, :], T), ALU.add))
                    norm_stats("ln4", u, x[:, u, :, :])
                for u in range(2):
                    norm_apply("ln4", u, x[:, u, :, :])
                for u in range(2):
                    l = L[u]
                    src = filled(dve, f"gate{u}")[:, 0:T * 40].rearrange("p (t c) -> p t c", t=T)
                    lg, eq, lm = l["lg"][:, :, :], l["eq"][:, :, :], l["lm"]
                    link(V.tensor_tensor(lg, src[:, :, 0:E], bc_gate[:, :].unsqueeze(1).broadcast_to([128, T, E]), ALU.add))
                    link(V.tensor_reduce(lm[:, :], lg, AX, ALU.max))
                    link(V.tensor_tensor(eq, lg, lm[:, :].unsqueeze(2).broadcast_to([128, T, E]), ALU.is_ge))
                    link(V.tensor_tensor(eq, eq, first[:, :].unsqueeze(1).broadcast_to([128, T, E]), ALU.mult))
                    link(V.tensor_reduce(lm[:, :], eq, AX, ALU.max))
                    link(V.tensor_tensor(eq, eq, lm[:, :].unsqueeze(2).broadcast_to([128, T, E]), ALU.is_equal))
                    V.tensor_tensor(l["um"][:, :, :].rearrange("p t (e r) -> p t e r", e=E),
                                    src[:, :, E:E + E * R].rearrange("p t (e r) -> p t e r", e=E),
                                    eq.unsqueeze(3).broadcast_to([128, T, E, R]), ALU.mult).then_inc(drained(f"gate{u}"), 1)
                for u in range(2):
                    l = L[u]
                    add_row("y3", u, bc_wo)
                    link(V.tensor_tensor(l["y"][:, :, :], l["y"][:, :, :], over(g_ab0[:, u, 1, :], T), ALU.mult))
                    V.tensor_tensor(x[:, u, :, :], x[:, u, :, :], l["y"][:, :, :], ALU.add).then_inc(S[f"x_layer0_{u}"], 1)
                    dve.wait_ge(S[f"x_layer0_{u}"], 1)
                    norm_stats("ln5", u, x[:, u, :, :])
                for u in range(2):
                    norm_apply("ln5", u, x[:, u, :, :])

                def heads(ap, half):
                    return ap[:, half * HALF:(half + 1) * HALF].rearrange("p (h d) -> p h d", h=HH)

                def per_head(ap):
                    return ap.unsqueeze(2).broadcast_to([ap.shape[0], HH, HD])

                src = filled(dve, "rate")[:, 0:NJ * H].rearrange("p (j h) -> p j h", j=NJ)
                V.tensor_tensor(eta[:, :, :], src, bc_tb[:, :].unsqueeze(1).broadcast_to([128, NJ, H]), ALU.add).then_inc(drained("rate"), 1)
                dve.wait_ge(S["rate_sig"], 1)
                link(V.tensor_scalar(eta[:, :, :], eta[:, :, :], rate[:, :], None, ALU.mult))
                for s in range(2 * NJ + 3):
                    j, f = divmod(s, 2)
                    jq, fq = divmod(s - 1, 2)
                    hs = slice(HH * f, HH * (f + 1))
                    hq = slice(HH * fq, HH * (fq + 1))
                    if j < NJ:
                        dve.wait_ge(S["z_squared"], s + 1)
                        V.tensor_reduce(ssum[:, hs], heads(sq, f), AX, ALU.add).then_inc(S["z_var"], 1)
                    if j < NJ:
                        dve.wait_ge(S["z_std"], s + 1)
                        link(V.reciprocal(zinv[:, hs], zstd[:, hs]))
                        V.tensor_tensor(heads(zhat, f), filled(dve, f"z{j}{f}").rearrange("p (h d) -> p h d", h=HH),
                                        per_head(zinv[:, hs]), ALU.mult).then_inc(drained(f"z{j}{f}"), 1)
                        V.tensor_tensor(scl[:, hs], zinv[:, hs], eta[:, j, hs], ALU.mult).then_inc(S["scale_ready"], 1)
                    if 1 <= jq <= NJ:
                        dve.wait_ge(S["zq_squared"], s - 2)
                        V.tensor_reduce(qsum[:, hq], heads(sqq, fq), AX, ALU.add).then_inc(S["zq_var"], 1)
                    if 1 <= jq <= NJ:
                        dve.wait_ge(S["zq_std"], s - 2)
                        link(V.reciprocal(qinv[:, hq], qstd[:, hq]))
                        if jq >= 2:
                            filled(dve, f"zT{jq - 2}{fq}")
                        V.tensor_tensor(heads(zq_hat, fq), filled(dve, f"zq{jq - 1}{fq}").rearrange("p (h d) -> p h d", h=HH),
                                        per_head(qinv[:, hq]), ALU.mult).then_inc(drained(f"zq{jq - 1}{fq}"), 1)
                    if j < NJ:
                        ready(dve, f"z{j}{f}")
                        dve.wait_ge(S["base_ready"], s + 1)
                        prod = go_on(V.tensor_tensor(heads(tmp, f), heads(gbase, f), heads(zhat, f), ALU.mult))
                        link(V.tensor_reduce(c12[:, f, 0, :], heads(gbase, f), AX, ALU.add))
                        mean = go_on(V.tensor_scalar(c12[:, f, 0, :], c12[:, f, 0, :], 1.0 / HD, None, ALU.mult))
                        settled(prod)
                        link(V.tensor_reduce(c12[:, f, 1, :], heads(tmp, f), AX, ALU.add))
                        link(V.scalar_tensor_tensor(heads(tmp, f), heads(zhat, f), 1.0 / HD, per_head(c12[:, f, 1, :]), ALU.mult, ALU.mult))
                        V.tensor_tensor(heads(gbase, f), heads(gbase, f), heads(tmp, f), ALU.subtract).then_inc(S["grad_base"], 1)
                        settled(mean)
                        dve.wait_ge(S["grad_base"], s + 1)
                        V.tensor_tensor(grad[0:K, hs, 0, :], heads(gbase, f)[0:K], per_head(c12[0:K, f, 0, :]),
                                        ALU.subtract).then_inc(S["grad_top"], 1)

                dve.wait_ge(S["x_ttt"], NJ)
                for j in range(NJ):
                    n = go_on(V.bn_stats(stats6[:, j, :], xc[:, j, :]))
                settled(n)
                for j in range(NJ):
                    last = V.bn_aggr(mv6[:, j, :], stats6[:, j, :])
                last.then_inc(S["ln6_var"], 1)
                dve.wait_ge(S["ln6_std"], 1)
                link(V.reciprocal(inv6[:, :], std6[:, :]))
                for j in range(NJ):
                    last = V.tensor_scalar(hat6[:, j, :], xc[:, j, :], mv6[:, j, 0:1], inv6[:, j:j + 1], ALU.subtract, ALU.mult)
                last.then_inc(S["ln6_hat"], 1)
                for half in range(2):
                    ready(dve, f"h4{half}")
                V.tensor_tensor(diff[:, :, :, 1:K], h4[:, :, :, 1:K], h4[:, :, :, 0:K - 1], ALU.subtract)
                V.tensor_tensor(diff[:, 1:NJ, :, 0], h4[:, 1:NJ, :, 0], h4[:, 0:NJ - 1, :, K - 1], ALU.subtract)
                link(V.tensor_copy(diff[:, 0, :, 0], h4[:, 0, :, 0]))
                V.scalar_tensor_tensor(mix_k, gbase[:, :], mu_k[:, :], zhat[:, :], ALU.mult, ALU.add).then_inc(S["mix_ready"], 1)
                V.scalar_tensor_tensor(mix_r, gbase[:, :], mu_r[:, :], zhat[:, :], ALU.mult, ALU.add).then_inc(S["mix_ready"], 1)
                for half in range(2):
                    ready(dve, f"r{half}")
                    o = gbase[:, half * 512:(half + 1) * 512]
                    V.tensor_tensor(o, filled(dve, f"val{half}"), r_sb[:, half * 512:(half + 1) * 512], ALU.mult).then_inc(drained(f"val{half}"), 1)
                    ready(dve, f"val{half}")
                    o3 = o.rearrange("p (j d) -> p j d", j=4)
                    link(V.tensor_tensor(o3, o3, over(g_ab1[:, 1, :], 4), ALU.mult))
                    V.tensor_tensor(xc[:, 4 * half:4 * half + 4, :], xc[:, 4 * half:4 * half + 4, :], o3, ALU.add).then_inc(S["x_final"], 1)
                dve.drain().then_inc(S["engines_done"], 1)
                dve.wait_ge(go["dve"], 1)
                dve.sem_clear(go["dve"])

        @block.sync
        def _(sp):
            for dst, src in loads:
                sp.dma_start(dst, src).then_inc(weights_loaded, 16)
            with sp.Fori(0, TRIPS) as i:
                for u in range(2):
                    sp.dma_start(x[:, u, :, :], x_dram[bass.ds(2 * i + u, 1), :, :, :].rearrange("b p t d -> (b p) t d")).then_inc(S[f"x_loaded_{u}"], 16)
                for b in range(2):
                    sp.wait_ge(S[f"x_layer0_{b}"], 1)
                    for odd in range(2):
                        sp.dma_start(xc[64 * b:64 * b + 64, :, :].rearrange("p (t o) d -> p t o d", o=2)[:, :, odd, :],
                                     x[64 * odd:64 * odd + 64, b, :, :]).then_inc(S["x_moved"], 16)
                sp.wait_ge(S["x_final"], 2)
                for b in range(2):
                    sp.dma_start(out_dram[bass.ds(2 * i + b, 1), :, :, :].rearrange("b t j d -> (b t) j d"),
                                 xc[64 * b:64 * b + 64, :, :]).then_inc(S["out_stored"], 16)
                sp.wait_ge(S["x_moved"], 64)
                sp.wait_ge(S["out_stored"], 32)
                sp.drain().then_inc(S["engines_done"], 1)
                sp.wait_ge(go["sp"], 1)
                sp.sem_clear(go["sp"])

        @block.gpsimd
        def _(pool):
            P = nc.gpsimd
            done = 0
            for t in (ones[:, :], kT1[HD:C, :, :], qT1[HD:C, :, :], L[0]["v"][:, :, D:D + 1], L[1]["v"][:, :, D:D + 1]):
                done += 1
                P.memset(t, 1.0).then_inc(pool_set, 1)
                pool.wait_ge(pool_set, done)
            for t in (grad[:, :, :, :], L[0]["qb"][:, :], L[1]["qb"][:, :], L[0]["umT"][:, :], L[1]["umT"][:, :]):
                P.memset(t, 0.0).then_inc(pool_set, 1)
            pool.wait_ge(pool_set, N_SETS)
            pool.wait_ge(dve_set, 2 + B + PAIRS)
            with pool.Fori(0, TRIPS) as _i:
                def heads(ap, f):
                    return ap[:, f * HALF:(f + 1) * HALF].rearrange("p (h d) -> p h d", h=HH)

                def target(j, f):
                    ready(pool, f"t1_{j}{f}")
                    t = t_tok[:, j % 2, f * HALF:(f + 1) * HALF]
                    P.tensor_tensor(t, t, gam_bet[:, f * HALF:(f + 1) * HALF], ALU.add).then_inc(S["target_ready"], 1)

                for f in range(2):
                    target(0, f)
                for s in range(2 * NJ + 5):
                    j, f = divmod(s, 2)
                    jx, fx = divmod(s - 3, 2)
                    hs = slice(HH * f, HH * (f + 1))
                    if j < NJ:
                        if s:
                            pool.wait_ge(S["grad_bot"], s)
                        ready(pool, f"z{j}{f}")
                        P.tensor_tensor(heads(gbase, f), heads(zhat, f), heads(gamma2, f), ALU.mult).then_inc(S["g_hat"], 1)
                        pool.wait_ge(S["g_hat"], s + 1)
                        pool.wait_ge(S["target_ready"], s + 1)
                        P.tensor_tensor(heads(gbase, f), heads(gbase, f), heads(t_tok[:, j % 2, :], f), ALU.add).then_inc(S["base_ready"], 1)
                        ready(pool, f"k1_{j}{f}")
                        pool.wait_ge(S["scale_ready"], s + 1)
                        P.tensor_tensor(k_sc[:, hs, 0:HD], heads(k_tok[:, j % 2, :], f), scl[:, hs].unsqueeze(2).broadcast_to([128, HH, HD]), ALU.mult)
                        P.tensor_copy(k_sc[:, hs, HD:C], scl[:, hs].unsqueeze(2)).then_inc(S["k_scaled"], 1)
                        pool.wait_ge(S["k_scaled"], s + 1)
                        if j + 1 < NJ:
                            target(j + 1, f)
                    if 1 <= jx <= NJ and fx == 1:
                        if s <= 2 * NJ:
                            pool.wait_ge(S["grad_bot"], s)
                        ready(pool, f"o{jx - 1}")
                        at = att1[:, jx % 2, :]
                        P.tensor_tensor(at, at, bc_out1[:, :], ALU.add).then_inc(S["att_step"], 1)
                        pool.wait_ge(S["att_step"], 2 * jx - 1)
                        P.tensor_tensor(at, at, g_ab1[:, 0, :], ALU.mult).then_inc(S["att_step"], 1)
                        pool.wait_ge(S["att_step"], 2 * jx)
                        if jx == 1:
                            pool.wait_ge(S["x_moved"], 64)
                        P.tensor_tensor(xc[:, jx - 1, :], xc[:, jx - 1, :], at, ALU.add).then_inc(S["x_ttt"], 1)
                        pool.wait_ge(S["x_ttt"], jx)
                    if j < NJ:
                        if j + 1 < NJ:
                            pool.wait_ge(S["target_ready"], s + 3)
                        pool.wait_ge(S["grad_base"], s + 1)
                        P.tensor_tensor(grad[K:128, hs, 1, :], heads(gbase, f)[K:128],
                                        c12[K:128, f, 0, :].unsqueeze(2).broadcast_to([K, HH, HD]), ALU.subtract).then_inc(S["grad_bot"], 1)
                pool.drain().then_inc(S["engines_done"], 1)
                pool.wait_ge(S["engines_done"], 5)
                pool.sem_clear(range(numbers[0], numbers[-1] + 1))
                for s in go.values():
                    pool.sem_inc(s, 1)


def laid_out(i):
    f = lambda v: np.ascontiguousarray(np.asarray(v))
    col = lambda v: f(np.asarray(v).reshape(-1, 128).T)
    row = lambda v: f(np.asarray(v).reshape(1, -1))
    lora_b = np.zeros((128, FF), np.float32)
    lora_b[:E * R] = np.asarray(i["L0_ffn_lora_B"]).transpose(0, 2, 1).reshape(E * R, FF)
    w1 = np.asarray(i["L1_attn_W1"]).transpose(1, 0, 2)
    return {
        "x": f(i["L0_attn_video"]), "proj_tiled": f(np.tile(np.asarray(i["L0_attn_proj"]).T, (H0, H0))),
        "WqT": f(i["L0_attn_Wq"].T), "WkT": f(i["L0_attn_Wk"].T), "WvT": f(i["L0_attn_Wv"].T), "WoT": f(i["L0_attn_Wo"].T),
        "bq": col(i["L0_attn_bq"]), "bk": col(i["L0_attn_bk"]), "g2": col(i["L0_attn_g2"]), "be2": col(i["L0_attn_be2"]),
        "bv": row(i["L0_attn_bv"]), "bo": row(i["L0_attn_bo"]), "b2": row(i["L0_attn_b2"]), "g3": row(i["L0_attn_g3"]),
        "be3": row(i["L0_attn_be3"]), "W1T": f(i["L0_attn_W1"].T), "b1": col(i["L0_attn_b1"]), "W2T": f(i["L0_attn_W2"].T),
        "gate_lora_a": f(np.concatenate([np.asarray(i["L0_ffn_gate_W"]), np.asarray(i["L0_ffn_lora_A"]).reshape(E * R, D)]).T),
        "gate_b": row(i["L0_ffn_gate_b"]), "wiT": f(i["L0_ffn_wi_W"].T), "wi_b": col(i["L0_ffn_wi_b"]), "woT": f(i["L0_ffn_wo_W"].T),
        "wo_b": row(i["L0_ffn_wo_b"]), "lora_b": lora_b, "c0T": f(i["L0_c"].T), "c1T": f(i["L1_c"].T),
        "wmod0": f(i["L0_wmod"]), "wmod1": f(i["L1_wmod"]),
        "wq1": f(i["L1_attn_wq"]), "wk1": f(i["L1_attn_wk"]), "wv1": f(i["L1_attn_wv"]), "wq1T": f(i["L1_attn_wq"].T),
        "wo1": f(i["L1_attn_wo"]), "W1c": f(w1), "b1c": f(np.asarray(i["L1_attn_b1"]).reshape(1, H, HD)),
        "theta": row(i["L1_attn_theta"]), "theta_bias": row(i["L1_attn_theta_bias"]),
        "alpha2": f(np.tile(np.asarray(i["L1_attn_alpha"]), 2)[:, None]), "gamma": row(i["L1_attn_gamma"]), "beta": row(i["L1_attn_beta"]),
        "gammaT": col(i["L1_attn_gamma"]), "betaT": col(i["L1_attn_beta"]),
        "W_rT": f(i["L1_ffn_W_r"].T), "W_kT": f(i["L1_ffn_W_k"].T), "W_vT": f(i["L1_ffn_W_v"].T),
        "mu_r": col(i["L1_ffn_mu_r"]), "mu_k": col(i["L1_ffn_mu_k"]),
        **shape_constants(),
    }


def kernel(**inputs):
    import concourse.bacc as bacc
    from concourse.bass_utils import run_bass_kernel_spmd

    arrays = laid_out(inputs)
    nc = bacc.Bacc("TRN2", target_bir_lowering=False, num_devices=1)
    aps = {n: nc.dram_tensor(f"in_{n}", v.shape, mybir.dt.from_np(v.dtype), kind="ExternalInput").ap() for n, v in arrays.items()}
    out = nc.dram_tensor("out_x", (B, N, D), F32, kind="ExternalOutput").ap()
    build(nc, aps, out)
    r = run_bass_kernel_spmd(nc, [{f"in_{n}": v for n, v in arrays.items()}], core_ids=[0])
    return r.results[0]["out_x"]
```

```python
from contextlib import ExitStack

import numpy as np

import concourse.bass as bass
from concourse import mybir

F32 = mybir.dt.float32
BF16 = mybir.dt.bfloat16
ALU = mybir.AluOpType
ACT = mybir.ActivationFunctionType
AX = mybir.AxisListType.X

B, N, D = 8, 512, 128
PAIRS = B // 2
T = N // 128
H0, DH, M = 16, 8, 32
FEAT = H0 * M
G = FEAT // 128
FF = 512
NF = FF // 128
E, R = 8, 4
GA = E + E * R
H, HD, K = 16, 64, 64
NJ = N // K
HW = H * HD
HP = H // 2
HH = H // 2
HALF = HH * HD
C = HD + 1
EPS_K, LN_EPS, TTT_EPS = 1e-4, 1e-5, 1e-6
NORM = DH ** -0.25


def views(spec):
    where, at = {}, 0
    for name, width in spec:
        where[name] = (at, width)
        at += width
    return where, at


PACKS = {
    "cols": [("c0", B), ("c1", B), ("bq", 1), ("bk", 1), ("g2", 1), ("be2", 1), ("mu_r", 1), ("mu_k", 1), ("alpha", 1),
             ("token_rate", 1), ("b1", NF), ("bi", NF), ("beta", HP), ("gamma", HP)],
    "wmod": [("wmod0", 6 * D), ("wmod1", 6 * D)],
    "compose": [("wqT", HP * D), ("wo", HP * D)],
    "attn": [("ident", 128), ("wq", D), ("wk", D), ("wv", D), ("half_square", H0), ("proj", FEAT)],
    "attn2": [("ctx_mask", G * D), ("head_sel", G * H0), ("wo0", D), ("w1", FF), ("w2", NF * D)],
    "expert": [("gate_a", GA), ("wi", FF), ("wof", NF * D), ("lora_b", FF), ("first", E)],
    "ttt": [("wk1", HW), ("wq1", HW), ("w_r", D), ("w_kf", D), ("w_vf", D)],
    "rows": [("bv", D), ("bo", D), ("b2", D), ("g3", D), ("be3", D), ("wo_b", D), ("gate_b", E), ("theta_bias", H)],
    "gam_bet_rows": [("gamma", HW), ("beta", HW)],
}


def shape_constants():
    head_of_dim = np.arange(D) // DH
    head_of_feat = np.arange(FEAT) // M
    same = (head_of_dim[:, None] == head_of_feat[None, :]).astype(np.float32)
    head_sel = (head_of_feat[:, None] == np.arange(H0)[None, :]).astype(np.float32)
    return {
        "ident": np.eye(128, dtype=np.float32),
        "proj_mask": same * np.float32(NORM),
        "ctx_mask": same.T.reshape(G, 128, D).transpose(1, 0, 2).reshape(128, G * D),
        "head_sel": head_sel.reshape(G, 128, H0).transpose(1, 0, 2).reshape(128, G * H0),
        "half_square": (head_of_dim[:, None] == np.arange(H0)[None, :]).astype(np.float32) * np.float32(0.5 * NORM * NORM),
        "first": np.tile(np.arange(E, 0, -1, dtype=np.float32)[None, :], (128, 1)),
        "token_rate": np.tile(1.0 / np.arange(1, K + 1, dtype=np.float32), 2)[:, None].astype(np.float32),
    }


(LN1_STATS, LN1, QKV, Q_SHIFT, K_MAX, STABLE, K_SHIFT, Q_FEATURES, K_FEATURES, CONTEXT, ATTEND, ATTN_T, PROJECT, LN2, FF1, FF2,
 LN3, LN4, GATE, LORA, EXPERT1, EXPERT2, LN5, N_STEPS) = range(24)
(MIX_STATS, MIX_NORM, MIX_SHIFT, MIX_IN, MIX_OUT, N_MIX) = range(6)
TAIL_SLOTS = 4
MAIN_SLOTS = 2 * NJ + 1
ORDER = "0130130133120020201221001101001011010110010101010101011"

WARM = {
    "h2T1": 14, "umT1": 6, "h3T0": 4, "h3T1": 20, "qT1_00": 6, "fq11": 12, "o6": 8, "o7": 8,
}


def turns(who):
    taken = [0, 0, 0, 0]
    for u in map(int, ORDER):
        if u in who:
            yield u, taken[u]
        taken[u] += 1


PER_BATCH = [f"ln{n}_{what}" for n in range(1, 6) for what in ("var", "std", "hat")]
PER_BATCH += ["k_max_ready", "k_stab_ready", "k_shifted", "k_exp", "k_feat_ready", "q_exp", "x_layer0"]
PER_PAIR = [
    "x_moved", "mods_ready", "dve_step", "rate_sig",
    "w_ready", "z_squared", "z_var", "z_std", "scale_ready", "g_hat", "grad_base", "grad_top", "grad_bot", "k_scaled", "dw_done",
    "zq_squared", "zq_inv", "zq_ready", "att_step", "target_ready", "zq_var", "zq_std", "ln6_var", "ln6_std", "ln6_hat", "mix_ready", "key_ready", "x_ttt", "x_final",
]


def build(nc, a, out):
    with ExitStack() as ctx:
        def sb(name, shape, dtype=F32):
            return ctx.enter_context(nc.sbuf_tensor(name, shape, dtype))

        def new_sem(name):
            return ctx.enter_context(nc.semaphore(name))

        ps = ctx.enter_context(nc.psum_tensor("ps", [128, 8, 512], F32))
        bank = [ps[:, i, :] for i in range(8)]

        tile = {n: sb(f"pack_{n}", [128, views(PACKS[n])[1]]) for n in ("cols", "attn", "attn2", "expert", "ttt", "rows")}

        def part(pack, name):
            at, width = views(PACKS[pack])[0][name]
            return tile[pack][:, at:at + width]

        cT = tile["cols"][:, 0:2 * B].rearrange("p (l b) -> p l b", l=2)
        b_q0, b_k0, g2, be2, mu_r, mu_k, alpha, token_rate, b_1, b_i, betaT, gammaT = (
            part("cols", n) for n in ("bq", "bk", "g2", "be2", "mu_r", "mu_k", "alpha", "token_rate", "b1", "bi", "beta", "gamma"))
        ident, w_q0, w_k0, w_v0, half_square, proj_bd = (part("attn", n) for n in ("ident", "wq", "wk", "wv", "half_square", "proj"))
        w_o0, w_1 = (part("attn2", n) for n in ("wo0", "w1"))
        ctx_mask = part("attn2", "ctx_mask").rearrange("p (g d) -> p g d", g=G)
        head_sel = part("attn2", "head_sel").rearrange("p (g h) -> p g h", g=G)
        w_2 = part("attn2", "w2").rearrange("p (f d) -> p f d", f=NF)
        w_ga, w_i, lora_b, first = (part("expert", n) for n in ("gate_a", "wi", "lora_b", "first"))
        w_of = part("expert", "wof").rearrange("p (f d) -> p f d", f=NF)
        w_k1, w_q1, w_r, w_kf, w_vf = (part("ttt", n) for n in ("wk1", "wq1", "w_r", "w_kf", "w_vf"))
        bc_v0, bc_o0, bc_b2, bc_g3, bc_be3, bc_wo, bc_gate, bc_tb = (
            part("rows", n) for n in ("bv", "bo", "b2", "g3", "be3", "wo_b", "gate_b", "theta_bias"))
        ones = sb("ones", [128, 128])
        w_t1 = sb("w_t1", [128, HW])
        g_wo = sb("g_wo", [128, HP, D])
        w_qo = sb("w_qo", [128, D])
        bc_out1 = sb("bc_out1", [128, D])
        w_theta = sb("w_theta", [128, H])
        rate = sb("rate", [128, 1])
        gamma2 = sb("gamma2", [128, HW])
        gam_bet = sb("gam_bet", [128, HW])
        w_parts = sb("w_parts", [C, 3, H, HD], BF16)
        ident_bf = sb("ident_bf", [128, 128], BF16)
        mod_all = sb("mod_all", [128, 12, B])
        mod = sb("mod", [128, 12, 2])
        g_ab0 = sb("g_ab0", [128, 2, 2, D])
        g_ab1 = sb("g_ab1", [128, 2, D])
        gg3 = sb("gg3", [128, 2, 2, D])

        x = sb("x", [128, 2, T, D])
        L = []
        for u in range(2):
            tiles = sb(f"tiles{u}", [128, 6, N])
            rows_ = sb(f"feats{u}", [128, 8, 512])
            L.append(dict(
                tiles=tiles, feats=rows_,
                stats=sb(f"stats{u}", [128, T, 6]), mv=sb(f"mv{u}", [128, T, 2]), std=sb(f"std{u}", [128, T]),
                inv=sb(f"inv{u}", [128, T]), hat=tiles[:, 0, :].rearrange("p (t d) -> p t d", t=T), hT=tiles[:, 1, :],
                qT=tiles[:, 2, :], q2=tiles[:, 3, :], kT=tiles[:, 4, :], k2=tiles[:, 5, :],
                v=sb(f"v{u}", [128, T, D + 1]), qmax=sb(f"qmax{u}", [128, T, H0]), qd=sb(f"qd{u}", [128, T, H0]), qf=tiles[:, 2:6, :],
                big=rows_[:, 0:4, :], ek=rows_[:, 4:8, :], kmax=sb(f"kmax{u}", [128, T, H0]),
                kmx=sb(f"kmx{u}", [128, H0]), stab=sb(f"stab{u}", [H0, 1]), sd=sb(f"sd{u}", [H0, H0]),
                ctx=sb(f"ctx{u}", [128, G, D + H0]), rden=sb(f"rden{u}", [128, T, H0]), y=sb(f"y{u}", [128, T, D]),
                lg=sb(f"lg{u}", [128, T, E]), lm=sb(f"lm{u}", [128, T]), eq=sb(f"eq{u}", [128, T, E]),
                um=sb(f"um{u}", [128, T, E * R]), umT=sb(f"umT{u}", [128, N]),
            ))

        xc = sb("xc", [128, NJ, D])
        h3 = sb("h3", [128, NJ, 2, K])
        w_sb_t = sb("w_sb", [128, H, 2, HD])
        w_sb = w_sb_t[0:C]
        kT1_t = sb("keys1", [128, H, 2 * K])
        kT1 = kT1_t[0:C]
        qT1_t = sb("queries1", [128, H, 2 * K])
        qT1 = qT1_t[0:C]
        k_tok = L[0]["tiles"][:, 1:5, :].rearrange("p (s a) b -> p s (a b)", s=2)
        k_sc = sb("k_sc", [128, H, C])
        t_tok = L[0]["feats"][:, 0:4, :].rearrange("p (s a) b -> p s (a b)", s=2)
        eta = sb("eta", [128, NJ, H])
        sq = L[0]["feats"][:, 4:6, :].rearrange("p a b -> p (a b)")
        ssum, zstd, zinv, scl = (sb(n, [128, H]) for n in ("ssum", "zstd", "zinv", "scl"))
        zhat = L[0]["feats"][:, 6:8, :].rearrange("p a b -> p (a b)")
        gbase = L[1]["feats"][:, 4:6, :].rearrange("p a b -> p (a b)")
        tmp = L[1]["feats"][:, 6:8, :].rearrange("p a b -> p (a b)")
        c12 = sb("c12", [128, 2, 2, HH])
        grad = sb("grad", [128, H, 2, HD])
        qsum, qstd, qinv = (sb(n, [128, H]) for n in ("qsum", "qstd", "qinv"))
        att1 = sb("att1", [128, 2, D])
        stats6, mv6 = sb("stats6", [128, NJ, 6]), sb("mv6", [128, NJ, 2])
        std6, inv6 = sb("std6", [128, NJ]), sb("inv6", [128, NJ])
        hat6 = sb("hat6", [128, NJ, D])
        h4, diff = sb("h4", [128, NJ, 2, K]), sb("diff", [128, NJ, 2, K])
        h4_flat, diff_flat = (t[:, :, :, :].rearrange("p j b t -> p (j b t)") for t in (h4, diff))
        mix_rk = w_sb_t[:, :, :, :].rearrange("p h b d -> p (h b d)")
        mix_r, mix_k = mix_rk[:, 0:HW], mix_rk[:, HW:2 * HW]
        kact = k_sc[:, :, :].rearrange("p h c -> p (h c)")[:, 0:HW]
        r_sb = h3[:, :, :, :].rearrange("p j b t -> p (j b t)")
        mod_mix = sb("mod_mix", [128, 2, 2])
        zq_hat, sqq = h4_flat, hat6[:, :, :].rearrange("p j d -> p (j d)")
        zT = diff_flat.rearrange("p (g t) -> p g t", g=HP)
        compose = w_sb_t[:, :, :, :].rearrange("p h b d -> p (h b d)")
        s_wqT = compose[:, 0:HW].rearrange("p (g d) -> p g d", g=HP)
        s_wo = compose[:, HW:2 * HW].rearrange("p (g d) -> p g d", g=HP)
        s_gam_bet = kT1_t[:, :, :].rearrange("p h t -> p (h t)")
        s_gam, s_bet = s_gam_bet[:, 0:HW], s_gam_bet[:, HW:2 * HW]
        s_q = qT1_t[:, :, :].rearrange("p h t -> p (h t)")
        s_the, s_wv = s_q[:, 0:HW], s_q[:, HW:2 * HW]
        s_w0 = k_sc[0:C, :, 0:HD]
        s_sum = h3[0:C, :, :, :].rearrange("p j b t -> p (j b t)")[:, 0:HW // 2].rearrange("p (h d) -> p h d", h=H)
        s_wmod = grad[:, :, :, :].rearrange("p h b d -> p (h b d)")[:, 0:12 * D]
        s_mask = xc[:, 0:FEAT // D, :].rearrange("p j d -> p (j d)")
        s_sig = sb("s_sig", [128, 2, B])
        s_gate = sb("s_gate", [128, 2, 4, B])
        s_mean = sb("s_mean", [C, H])

        names = [f"{n}_{u}" for n in PER_BATCH for u in range(2)] + PER_PAIR
        names += [f"filled_{i}" for i in range(8)] + [f"drained_{i}" for i in range(8)] + ["engines_done"]
        S = {n: new_sem(n) for n in names}
        numbers = [s.num for s in S.values()]
        assert numbers == list(range(numbers[0], numbers[0] + len(numbers)))
        go = {e: new_sem(f"go_{e}") for e in ("pe", "act", "dve", "sp")}
        x_loaded = [new_sem(f"x_loaded_{u}") for u in range(2)]
        out_stored = new_sem("out_stored")
        pool_set, dve_set, act_set, pe_set = (new_sem(n) for n in ("pool_set", "dve_set", "act_set", "pe_set"))
        set_step = new_sem("set_step")

        loads = {
            "mod": [(tile["cols"][:, :], a["cols"]), (s_wmod, a["wmod"])],
            "compose": [(compose, a["compose"])],
            "attn": [(tile["attn"][:, :], a["attn"]), (s_mask, a["c_proj_mask"]), (tile["rows"][:, :], a["rows"].partition_broadcast(128))],
            "attn2": [(tile["attn2"][:, :], a["attn2"])],
            "expert": [(tile["expert"][:, :], a["expert"])],
            "ttt": [(tile["ttt"][:, :], a["ttt"]), (s_wv, a["wv1"]), (s_gam_bet, a["gam_bet_rows"].partition_broadcast(128)),
                    (s_the, a["theta"].partition_broadcast(128)), (s_w0, a["w0"].rearrange("c (h d) -> c h d", h=H))],
        }
        loaded_sem = {n: new_sem(f"{n}_loaded") for n in loads}

        def loaded(eng, name):
            eng.wait_ge(loaded_sem[name], 16 * len(loads[name]))

        LEVELS = HD.bit_length() - 1
        N_LAYER0_SET = 6
        N_POOL_SET = N_LAYER0_SET + 4 + 1 + LEVELS + LEVELS + 1 + 1 + 5 + 1 + 3

        x_dram = a["x"].rearrange("b t p d -> b p t d")
        out_dram = out.rearrange("b (j t) d -> b t j d", t=K)

        FIRST, LOOP, LAST = range(3)
        rounds = [{}, {}, {}]
        now = [FIRST]

        block = ctx.enter_context(nc.Block())

        @block.tensor
        def _(pe):
            count = [0] * 8
            mm = nc.tensor.matmul

            def begin(name, b):
                if count[b]:
                    pe.wait_ge(S[f"drained_{b}"], count[b])
                count[b] += 1
                for _ in range(WARM.get(name, 0)):
                    mm(bank[b], ident_bf[:, :], ident_bf[:, :].unsqueeze(1).broadcast_to([128, 4, 128]), start=True, stop=True)
                rounds[now[0]][name] = (b, count[b])

            def end(ins, b):
                ins.then_inc(S[f"filled_{b}"], 1)

            def ready(name):
                b, n = rounds[now[0]][name]
                pe.wait_ge(S[f"drained_{b}"], n)

            loaded(pe, "mod")
            pe.wait_ge(dve_set, 1)
            for n in range(12):
                last = mm(bank[2][:, n * B:(n + 1) * B], s_wmod[:, n * D:(n + 1) * D], s_sig[:, n // 6, :], start=True, stop=True)
            last.then_inc(pe_set, 1)
            loaded(pe, "compose")
            for g in range(HP):
                mm(bank[0][:, 0:D], s_wqT[:, g, :], s_wo[:, g, :], start=(g == 0), stop=(g == HP - 1))
            for g in range(HP):
                last = mm(bank[1][:, 0:D], betaT[:, g:g + 1].broadcast_to([128, 128]), s_wo[:, g, :], start=(g == 0), stop=(g == HP - 1))
            last.then_inc(pe_set, 1)
            loaded(pe, "attn")
            pe.wait_ge(act_set, 2)
            pe.wait_ge(dve_set, 3)
            pe.wait_ge(pool_set, N_LAYER0_SET)

            def gate_rows():
                pe.wait_ge(S["mods_ready"], 1)
                begin("gates0", 7)
                for u in range(2):
                    for k in range(2):
                        last = mm(bank[7][:, (2 * u + k) * D:(2 * u + k + 1) * D], mod[:, 2 + 3 * k, u:u + 1].broadcast_to([128, 128]),
                                  ident, start=True, stop=True)
                end(last, 7)

            def transposed_hat(name, b, u, sem):
                begin(name, b)
                pe.wait_ge(S[f"{sem}_{u}"], 1)
                for t in range(T):
                    last = nc.tensor.transpose(bank[b][:, t * 128:(t + 1) * 128], L[u]["hat"][:, t, :], ident[:, :])
                end(last, b)

            def layer0(step, u):
                l, b0 = L[u], 4 * u
                if step == LN1:
                    transposed_hat(f"hT{u}", b0, u, "ln1_hat")
                elif step == QKV:
                    ready(f"hT{u}")
                    for n, (w, name) in enumerate(((w_q0, "qT"), (w_k0, "kT"))):
                        b = b0 + 1 + n
                        begin(f"{name}{u}", b)
                        end(mm(bank[b], w[:, :], l["hT"][:, :], start=True, stop=True), b)
                    b = b0 + 3
                    begin(f"v{u}", b)
                    for t in range(T):
                        last = mm(bank[b][:, t * D:(t + 1) * D], l["hT"][:, t * 128:(t + 1) * 128], w_v0[:, :], start=True, stop=True)
                    end(last, b)
                elif step in (Q_SHIFT, K_MAX):
                    name, src = ("xq", "qT") if step == Q_SHIFT else ("xk", "kT")
                    ready(f"{src}{u}")
                    if step == Q_SHIFT:
                        begin(f"dq{u}", b0)
                        for t in range(T):
                            last = mm(bank[b0][:, t * H0:(t + 1) * H0], l["q2"][:, t * 128:(t + 1) * 128], half_square[:, :], start=True, stop=True)
                        end(last, b0)
                    for t in range(T):
                        b = b0 + (t + 1) % 4
                        begin(f"{name}{u}{t}", b)
                        end(mm(bank[b], l[src][:, t * 128:(t + 1) * 128], proj_bd[:, :], start=True, stop=True), b)
                elif step == STABLE:
                    b = b0 + 1
                    begin(f"kmT{u}", b)
                    pe.wait_ge(S[f"k_max_ready_{u}"], 1)
                    end(nc.tensor.transpose(bank[b][0:H0, 0:128], l["kmx"][:, :], ident[:, :]), b)
                elif step == Q_FEATURES:
                    pe.wait_ge(S[f"q_exp_{u}"], T)
                    for g in range(G):
                        b = b0 + (3 + g) % 4
                        begin(f"fq{u}{g}", b)
                        for t in range(T):
                            last = nc.tensor.transpose(bank[b][:, t * 128:(t + 1) * 128], l["big"][:, t, g * 128:(g + 1) * 128], ident[:, :])
                        end(last, b)
                elif step == K_SHIFT:
                    b = b0 + 2
                    begin(f"kb{u}", b)
                    pe.wait_ge(S[f"k_stab_ready_{u}"], 1)
                    for t in range(T):
                        o = bank[b][:, t * H0:(t + 1) * H0]
                        mm(o, l["k2"][:, t * 128:(t + 1) * 128], half_square[:, :], start=True, stop=False)
                        last = mm(o, ones[0:H0, :], l["sd"][:, :], start=False, stop=True)
                    end(last, b)
                elif step == CONTEXT:
                    loaded(pe, "attn2")
                    pe.wait_ge(S[f"k_feat_ready_{u}"], T)
                    ready(f"v{u}")
                    for half in range(2):
                        b = b0 + half
                        begin(f"ctx{u}{half}", b)
                        for g in (2 * half, 2 * half + 1):
                            for t in range(T):
                                last = mm(bank[b][:, (g % 2) * 256:(g % 2) * 256 + D + 1], l["ek"][:, t, g * 128:(g + 1) * 128],
                                          l["v"][:, t, :], start=(t == 0), stop=(t == T - 1))
                        end(last, b)
                elif step == ATTEND:
                    for g in range(G):
                        ready(f"fq{u}{g}")
                    ready(f"ctx{u}0")
                    ready(f"ctx{u}1")
                    for half in range(2):
                        b = b0 + 2 + half
                        begin(f"num{u}{half}", b)
                        for t in (2 * half, 2 * half + 1):
                            for g in range(G):
                                last = mm(bank[b][:, (t % 2) * 256:(t % 2) * 256 + D + H0], l["qf"][:, g, t * 128:(t + 1) * 128],
                                          l["ctx"][:, g, :], start=(g == 0), stop=(g == G - 1))
                        end(last, b)
                elif step == ATTN_T:
                    b = b0
                    begin(f"attnT{u}", b)
                    ready(f"num{u}0")
                    ready(f"num{u}1")
                    for t in range(T):
                        last = nc.tensor.transpose(bank[b][:, t * 128:(t + 1) * 128], l["y"][:, t, :], ident[:, :])
                    end(last, b)
                elif step == PROJECT:
                    b = b0 + 1
                    begin(f"y1{u}", b)
                    ready(f"attnT{u}")
                    for t in range(T):
                        o = bank[b][:, t * D:(t + 1) * D]
                        mm(o, l["hT"][:, t * 128:(t + 1) * 128], ident[:, :], start=True, stop=False)
                        last = mm(o, l["q2"][:, t * 128:(t + 1) * 128], w_o0[:, :], start=False, stop=True)
                    end(last, b)
                elif step == LN2:
                    transposed_hat(f"x1T{u}", b0, u, "ln2_hat")
                elif step == FF1:
                    ready(f"x1T{u}")
                    for f in range(NF):
                        b = b0 + (2 + f) % 4
                        begin(f"f1{u}{f}", b)
                        end(mm(bank[b], w_1[:, f * 128:(f + 1) * 128], l["kT"][:, :], start=True, stop=True), b)
                elif step == FF2:
                    b = b0 + 2
                    begin(f"y2{u}", b)
                    for f in range(NF):
                        ready(f"f1{u}{f}")
                    for t in range(T):
                        o = bank[b][:, t * D:(t + 1) * D]
                        for f in range(NF):
                            mm(o, l["big"][:, f, t * 128:(t + 1) * 128], w_2[:, f, :], start=(f == 0), stop=False)
                        last = mm(o, l["kT"][:, t * 128:(t + 1) * 128], ident[:, :], start=False, stop=True)
                    end(last, b)
                elif step == LN4:
                    transposed_hat(f"h2T{u}", b0, u, "ln4_hat")
                elif step == GATE:
                    b = b0 + 1
                    loaded(pe, "expert")
                    ready(f"h2T{u}")
                    begin(f"gate{u}", b)
                    for t in range(T):
                        last = mm(bank[b][:, t * GA:(t + 1) * GA], l["hT"][:, t * 128:(t + 1) * 128], w_ga[:, :], start=True, stop=True)
                    end(last, b)
                elif step == LORA:
                    b = b0
                    begin(f"umT{u}", b)
                    ready(f"gate{u}")
                    for t in range(T):
                        last = nc.tensor.transpose(bank[b][0:E * R, t * 128:(t + 1) * 128], l["um"][:, t, :], ident[:, :])
                    end(last, b)
                elif step == EXPERT1:
                    ready(f"umT{u}")
                    for f in range(NF):
                        b = b0 + (1 + f) % 4
                        begin(f"f2{u}{f}", b)
                        mm(bank[b], w_i[:, f * 128:(f + 1) * 128], l["hT"][:, :], start=True, stop=False)
                        end(mm(bank[b], lora_b[:, f * 128:(f + 1) * 128], l["umT"][:, :], start=False, stop=True), b)
                elif step == EXPERT2:
                    b = b0 + 1
                    begin(f"y3{u}", b)
                    for f in range(NF):
                        ready(f"f2{u}{f}")
                    for t in range(T):
                        for f in range(NF):
                            last = mm(bank[b][:, t * D:(t + 1) * D], l["big"][:, f, t * 128:(t + 1) * 128], w_of[:, f, :],
                                      start=(f == 0), stop=(f == NF - 1))
                    end(last, b)
                elif step == LN5:
                    transposed_hat(f"h3T{u}", b0, u, "ln5_hat")

            def chunk(j):
                return h3[:, j, :, :].rearrange("p b t -> p (b t)")

            ring = [0]

            def begin_ring(name):
                b = 6 + ring[0] % 2
                ring[0] += 1
                begin(name, b)
                return b

            def rows(name, w, j, f):
                b = begin_ring(f"{name}{j}{f}")
                end(mm(bank[b], chunk(j), w[:, f * HALF:(f + 1) * HALF], start=True, stop=True), b)

            def turned(name, src, f, wait):
                b = begin_ring(name)
                wait()
                for g in range(4 * f, 4 * f + 4):
                    last = nc.tensor.transpose(bank[b][:, (g % 4) * 128:(g % 4 + 1) * 128], src[:, g * 128:(g + 1) * 128], ident[:, :])
                end(last, b)

            def predict(name, src, f):
                b = 4 + f
                for h in range(HH * f, HH * (f + 1)):
                    for c in range(2):
                        last = mm(bank[b][64 * c:64 * c + 64, (h % HH) * HD:(h % HH + 1) * HD],
                                  src[:, h, 64 * c:64 * c + 64], w_sb[:, h, c, :], start=True, stop=True)
                end(last, b)

            def start_state(half):
                for n in (2 * half, 2 * half + 1):
                    begin(f"w{n}", n)
                    for part in range(3):
                        last = mm(bank[n][0:C, :], ident_bf[0:C, 0:C],
                                  w_parts[:, part, 4 * n:4 * n + 4, :].unsqueeze(2).broadcast_to([C, 4, 2, HD]),
                                  start=(part == 0), stop=(part == 2), skip_group_check=True)
                    end(last, n)

            def rest_of_start():
                rows("t1_", w_t1, 0, 0)
                turned("kT1_01", k_tok[:, 0, :], 1, lambda: ready("k1_01"))
                start_state(1)
                rows("t1_", w_t1, 0, 1)
                begin("gates1", 5)
                for k in range(2):
                    for b in range(2):
                        last = mm(bank[5][64 * b:64 * b + 64, k * D:(k + 1) * D], mod[:, 8 + 3 * k, b:b + 1].broadcast_to([128, 64]),
                                  ident, start=True, stop=True)
                end(last, 5)

            def slot(s):
                j, f = divmod(s, 2)
                jq, fq = divmod(s - 1, 2)
                jo, fo = divmod(s - 2, 2)
                if j < NJ:
                    begin(f"z{j}{f}", 4 + f)
                    pe.wait_ge(S["w_ready"], s + 1)
                    ready(f"kT1_{j}{f}")
                    predict("z", kT1, f)
                if s == 0:
                    rest_of_start()
                if 0 <= jq < NJ - 1:
                    turned(f"kT1_{jq + 1}{fq}", k_tok[:, (jq + 1) % 2, :], fq, lambda: ready(f"k1_{jq + 1}{fq}"))
                if 1 <= jq <= NJ:
                    begin(f"zq{jq - 1}{fq}", 4 + fq)
                    pe.wait_ge(S["w_ready"], s)
                    ready(f"qT1_{jq - 1}{fq}")
                    predict("zq", qT1, fq)
                if j + 1 < NJ:
                    rows("t1_", w_t1, j + 1, f)
                if 1 <= jo <= NJ:
                    turned(f"zT{jo - 1}{fo}", zq_hat, fo, lambda: pe.wait_ge(S["zq_ready"], s - 3))
                if 0 <= jq < NJ:
                    b = begin_ring(f"qT1_{jq}{fq}")
                    pe.wait_ge(S["k_scaled"], s)
                    pe.wait_ge(S["grad_top"], s)
                    pe.wait_ge(S["grad_bot"], s)
                    for h in range(HH * fq, HH * (fq + 1)):
                        last = mm(bank[h // 4][0:C, (h % 4) * 128:(h % 4 + 1) * 128], k_sc[:, h, :],
                                  grad[:, h, :, :].rearrange("p b d -> p (b d)"), start=False, stop=(h % 4 == 3),
                                  skip_group_check=True)
                    last.then_inc(S["dw_done"], 1)
                    for g in range(4 * fq, 4 * fq + 4):
                        last = mm(bank[b][:, (g % 4) * 128:(g % 4 + 1) * 128], w_q1[:, g * 128:(g + 1) * 128], chunk(jq), start=True, stop=True)
                    end(last, b)
                if j + 1 < NJ:
                    rows("k1_", w_k1, j + 1, f)
                if 1 <= jo <= NJ and fo == 1:
                    b = begin_ring(f"o{jo - 1}")
                    ready(f"zT{jo - 1}0")
                    ready(f"zT{jo - 1}1")
                    mm(bank[b][:, 0:D], chunk(jo - 1), w_qo[:, :], start=True, stop=False)
                    for g in range(HP):
                        last = mm(bank[b][:, 0:D], zT[:, g, :], g_wo[:, g, :], start=False, stop=(g == HP - 1))
                    end(last, b)

            def recurrence():
                ring[0] = 0

                begin("rate", 4)
                for j in range(NJ):
                    last = mm(bank[4][:, j * H:(j + 1) * H], chunk(j), w_theta[:, :], start=True, stop=True)
                end(last, 4)
                rows("k1_", w_k1, 0, 0)
                start_state(0)
                rows("k1_", w_k1, 0, 1)
                turned("kT1_00", k_tok[:, 0, :], 0, lambda: ready("k1_00"))
                for s in range(MAIN_SLOTS):
                    slot(s)

            def mixing(step):
                if step == MIX_NORM:
                    pe.wait_ge(S["ln6_hat"], 1)
                    for half in range(2):
                        b = 4 + half
                        begin(f"h4{half}", b)
                        for t in range(4):
                            last = nc.tensor.transpose(bank[b][:, t * 128:(t + 1) * 128], hat6[:, 4 * half + t, :], ident[:, :])
                        end(last, b)
                elif step == MIX_IN:
                    pe.wait_ge(S["mix_ready"], 2)
                    for half in range(2):
                        b = 6 + half
                        begin(f"key{half}", b)
                        end(mm(bank[b], w_kf[:, :], mix_k[:, half * 512:(half + 1) * 512], start=True, stop=True), b)
                    for half in range(2):
                        b = 4 + half
                        begin(f"r{half}", b)
                        for t in range(4):
                            j = 4 * half + t
                            last = mm(bank[b][:, t * D:(t + 1) * D], mix_r[:, j * 128:(j + 1) * 128], w_r[:, :], start=True, stop=True)
                        end(last, b)
                elif step == MIX_OUT:
                    for half in range(2):
                        b = 6 + half
                        begin(f"val{half}", b)
                        pe.wait_ge(S["key_ready"], half + 1)
                        for t in range(4):
                            j = 4 * half + t
                            last = mm(bank[b][:, t * D:(t + 1) * D], kact[:, j * 128:(j + 1) * 128], w_vf[:, :], start=True, stop=True)
                        end(last, b)

            def between_layers(who):
                if 0 in who:
                    gate_rows()
                for u, step in turns(who):
                    if u == 3:
                        slot(MAIN_SLOTS + step)
                    elif u == 2:
                        mixing(step)
                    else:
                        layer0(step, u)

            def round_ends():
                pe.drain().then_inc(S["engines_done"], 1)
                pe.wait_ge(go["pe"], 1)
                pe.sem_clear(go["pe"])

            between_layers((0, 1))
            loaded(pe, "ttt")
            pe.wait_ge(pool_set, N_POOL_SET)
            round_ends()
            now[0] = LOOP
            with pe.Fori(0, PAIRS - 1) as _i:
                count[:] = [0] * 8
                recurrence()
                between_layers((0, 1, 2, 3))
                round_ends()
            now[0] = LAST
            count[:] = [0] * 8
            recurrence()
            between_layers((2, 3))

        def filled(eng, name):
            b, n = rounds[now[0]][name]
            eng.wait_ge(S[f"filled_{b}"], n)
            return bank[b]

        def drained(name):
            return S[f"drained_{rounds[now[0]][name][0]}"]

        def ready(eng, name):
            b, n = rounds[now[0]][name]
            eng.wait_ge(S[f"drained_{b}"], n)

        @block.scalar
        def _(act):
            loaded(act, "mod")
            nc.scalar.activation(s_sig[:, :, :], cT, ACT.Sigmoid).then_inc(act_set, 1)
            act.wait_ge(pe_set, 2)
            nc.scalar.copy(w_qo[:, :], bank[0][:, 0:D])
            nc.scalar.copy(bc_out1[:, :], bank[1][:, 0:D]).then_inc(act_set, 1)
            loaded(act, "attn")
            act.wait_ge(dve_set, 3)
            act.wait_ge(pool_set, N_LAYER0_SET)

            def root(name, src, dst, u=None, scale=1.0, eps=LN_EPS):
                key = name if u is None else f"{name}_{u}"
                nc.scalar.activation(dst, src, ACT.Sqrt, bias=eps, scale=scale).then_inc(S[key], 1)

            def modulated(name, dst, shift, scl_):
                src = filled(act, name)
                nc.scalar.activation(dst, src, ACT.Identity, bias=shift, scale=scl_)\
                   .then_inc(drained(name), 1)

            def layer0(step, u):
                l = L[u]
                roots = {LN1_STATS: "ln1", PROJECT: "ln2", FF2: "ln3", LN3: "ln4", EXPERT2: "ln5"}
                if step == LN1:
                    modulated(f"hT{u}", l["hT"][:, :], mod[:, 0, u:u + 1], mod[:, 1, u:u + 1])
                elif step == QKV:
                    for name, dst, dst2, bias in (("qT", "qT", "q2", b_q0), ("kT", "kT", "k2", b_k0)):
                        src = filled(act, f"{name}{u}")
                        nc.scalar.activation(l[dst][:, :], src, ACT.Identity, bias=bias[:, :])
                        nc.scalar.activation(l[dst2][:, :], src, ACT.Square, bias=bias[:, :]).then_inc(drained(f"{name}{u}"), 1)
                elif step == K_MAX:
                    for t in range(T):
                        src = filled(act, f"xk{u}{t}")
                        nc.scalar.copy(l["ek"][:, t, :], src).then_inc(drained(f"xk{u}{t}"), 1)
                elif step == STABLE:
                    for t in range(T):
                        ready(act, f"xq{u}{t}")
                        nc.scalar.activation(l["big"][:, t, :], l["big"][:, t, :], ACT.Exp).then_inc(S[f"q_exp_{u}"], 1)
                elif step == K_FEATURES:
                    for t in range(T):
                        act.wait_ge(S[f"k_shifted_{u}"], t + 1)
                        nc.scalar.activation(l["ek"][:, t, :], l["ek"][:, t, :], ACT.Exp).then_inc(S[f"k_exp_{u}"], 1)
                elif step == ATTN_T:
                    src = filled(act, f"attnT{u}")
                    nc.scalar.copy(l["q2"][:, :], src).then_inc(drained(f"attnT{u}"), 1)
                elif step == LN2:
                    modulated(f"x1T{u}", l["kT"][:, :], be2[:, :], g2[:, :])
                elif step in (FF1, EXPERT1):
                    name, bias = ("f1", b_1) if step == FF1 else ("f2", b_i)
                    for f in range(NF):
                        src = filled(act, f"{name}{u}{f}")
                        nc.scalar.activation(l["big"][:, f, :], src, ACT.Relu, bias=bias[:, f:f + 1]).then_inc(drained(f"{name}{u}{f}"), 1)
                elif step == LN4:
                    modulated(f"h2T{u}", l["hT"][:, :], mod[:, 3, u:u + 1], mod[:, 4, u:u + 1])
                elif step == LORA:
                    src = filled(act, f"umT{u}")
                    nc.scalar.copy(l["umT"][0:E * R, :], src[0:E * R, :]).then_inc(drained(f"umT{u}"), 1)
                elif step == LN5:
                    act.wait_ge(pool_set, N_POOL_SET)
                    if now[0] == LOOP:
                        act.wait_ge(S["x_final"], 2)
                    src = filled(act, f"h3T{u}")
                    nc.scalar.activation(h3[:, :, u, :], src.rearrange("p (j t) -> p j t", j=NJ), ACT.Identity,
                                         bias=mod[:, 6, u:u + 1], scale=mod[:, 7, u:u + 1]).then_inc(drained(f"h3T{u}"), 1)
                if step in roots:
                    name = roots[step]
                    act.wait_ge(S[f"{name}_var_{u}"], 1)
                    root(f"{name}_std", l["mv"][:, :, 1], l["std"][:, :], u)

            def state(half):
                nc.scalar.copy(w_sb[:, HH * half:HH * (half + 1), :, :].rearrange("p h b d -> p (h b d)"),
                               ps[0:C, 2 * half:2 * half + 2, :].rearrange("p a c -> p (a c)")).then_inc(S["w_ready"], 1)

            def split_heads(key, dst, f, halves=(0, 1)):
                src = filled(act, key).rearrange("p (g t) -> p g t", g=4)
                d = dst[0:HD, HH * f:HH * (f + 1), :].rearrange("p (g e) t -> p g e t", e=2)
                if 0 in halves:
                    nc.scalar.copy(d[:, :, 0, :], src[0:HD])
                if 1 in halves:
                    nc.scalar.copy(d[:, :, 1, :], src[HD:128]).then_inc(drained(key), 1)

            def key_rows(j, f):
                src = filled(act, f"k1_{j}{f}")
                if j >= 2:
                    act.wait_ge(S["k_scaled"], 2 * (j - 2) + f + 1)
                nc.scalar.copy(k_tok[:, j % 2, f * HALF:(f + 1) * HALF], src).then_inc(drained(f"k1_{j}{f}"), 1)

            def target_rows(j, f):
                src = filled(act, f"t1_{j}{f}")
                if j >= 2:
                    act.wait_ge(S["grad_base"], 2 * (j - 2) + f + 1)
                nc.scalar.copy(t_tok[:, j % 2, f * HALF:(f + 1) * HALF], src).then_inc(drained(f"t1_{j}{f}"), 1)

            def spread(sem_in, n, dst, src, sem_out):
                act.wait_ge(S[sem_in], n)
                nc.scalar.activation(dst, src, ACT.Sqrt, bias=TTT_EPS, scale=1.0 / HD).then_inc(S[sem_out], 1)

            def start_state(half):
                for n in (2 * half, 2 * half + 1):
                    filled(act, f"w{n}")
                state(half)

            def rest_of_start():
                target_rows(0, 0)
                split_heads("kT1_01", kT1, 1)
                start_state(1)
                target_rows(0, 1)
                src = filled(act, "gates1")
                nc.scalar.copy(g_ab1[:, :, :].rearrange("p k d -> p (k d)"), src[:, 0:2 * D]).then_inc(drained("gates1"), 1)

            def slot(s):
                j, f = divmod(s, 2)
                jq, fq = divmod(s - 1, 2)
                jo, fo = divmod(s - 2, 2)
                if j < NJ:
                    src = filled(act, f"z{j}{f}")
                    nc.scalar.activation(sq[:, f * HALF:(f + 1) * HALF], src, ACT.Square).then_inc(S["z_squared"], 1)
                if 0 <= jq < NJ - 1:
                    split_heads(f"kT1_{jq + 1}{fq}", kT1, fq, (0,))
                if j < NJ:
                    spread("z_var", s + 1, zstd[:, HH * f:HH * (f + 1)], ssum[:, HH * f:HH * (f + 1)], "z_std")
                if s == 0:
                    rest_of_start()
                if 0 <= jq < NJ - 1:
                    split_heads(f"kT1_{jq + 1}{fq}", kT1, fq, (1,))
                if 1 <= jq <= NJ:
                    src = filled(act, f"zq{jq - 1}{fq}")
                    hq = slice(fq * HALF, (fq + 1) * HALF)
                    nc.scalar.activation(sqq[:, hq], src, ACT.Square).then_inc(S["zq_squared"], 1)
                    nc.scalar.copy(zq_hat[:, hq], src).then_inc(drained(f"zq{jq - 1}{fq}"), 1)
                if j + 1 < NJ:
                    target_rows(j + 1, f)
                if 1 <= jq <= NJ:
                    spread("zq_var", s - 2, qstd[:, HH * fq:HH * (fq + 1)], qsum[:, HH * fq:HH * (fq + 1)], "zq_std")
                if 1 <= jo <= NJ:
                    if jo >= 2:
                        filled(act, f"o{jo - 2}")
                    src = filled(act, f"zT{jo - 1}{fo}")
                    nc.scalar.copy(zT[:, 4 * fo:4 * fo + 4, :].rearrange("p g t -> p (g t)"), src).then_inc(drained(f"zT{jo - 1}{fo}"), 1)
                if 0 <= jq < NJ:
                    act.wait_ge(S["dw_done"], s)
                    state(fq)
                    split_heads(f"qT1_{jq}{fq}", qT1, fq)
                if j + 1 < NJ:
                    key_rows(j + 1, f)
                if 1 <= jo <= NJ and fo == 1:
                    src = filled(act, f"o{jo - 1}")
                    if jo >= 3:
                        act.wait_ge(S["x_ttt"], jo - 2)
                    nc.scalar.copy(att1[:, jo % 2, :], src[:, 0:D]).then_inc(drained(f"o{jo - 1}"), 1)

            def recurrence():
                ready(act, "rate")
                nc.scalar.activation(eta[:, :, :], eta[:, :, :], ACT.Sigmoid).then_inc(S["rate_sig"], 1)
                key_rows(0, 0)
                start_state(0)
                key_rows(0, 1)
                split_heads("kT1_00", kT1, 0)
                for s in range(MAIN_SLOTS):
                    slot(s)

            def mixing(step):
                if step == MIX_STATS:
                    act.wait_ge(S["ln6_var"], 1)
                    nc.scalar.activation(std6[:, :], mv6[:, :, 1], ACT.Sqrt, bias=LN_EPS).then_inc(S["ln6_std"], 1)
                elif step == MIX_NORM:
                    for half in range(2):
                        src = filled(act, f"h4{half}").rearrange("p (j b t) -> p j b t", j=4, b=2)
                        nc.scalar.activation(h4[:, 4 * half:4 * half + 4, 0, :], src[:, :, 0, :], ACT.Identity,
                                             bias=mod_mix[:, 0, 0:1], scale=mod_mix[:, 1, 0:1])
                        nc.scalar.activation(h4[:, 4 * half:4 * half + 4, 1, :], src[:, :, 1, :], ACT.Identity,
                                             bias=mod_mix[:, 0, 1:2], scale=mod_mix[:, 1, 1:2]).then_inc(drained(f"h4{half}"), 1)
                elif step == MIX_IN:
                    for half in range(2):
                        src = filled(act, f"key{half}")
                        d = kact[:, half * 512:(half + 1) * 512]
                        nc.scalar.activation(d, src, ACT.Relu).then_inc(drained(f"key{half}"), 1)
                        ready(act, f"key{half}")
                        nc.scalar.activation(d, d, ACT.Square).then_inc(S["key_ready"], 1)
                    for half in range(2):
                        src = filled(act, f"r{half}")
                        nc.scalar.activation(r_sb[:, half * 512:(half + 1) * 512], src, ACT.Sigmoid).then_inc(drained(f"r{half}"), 1)

            def between_layers(who):
                if now[0] == LOOP:
                    act.wait_ge(S["w_ready"], 2 * NJ + 2)
                    for n in range(4):
                        act.sem_inc(drained(f"w{n}"), 1)
                    for name in ("k_scaled", "grad_top", "grad_bot"):
                        act.wait_ge(S[name], 2 * NJ)
                if 0 in who:
                    act.wait_ge(S["mods_ready"], 1)
                    src = filled(act, "gates0")
                    nc.scalar.copy(g_ab0[:, :, :, :].rearrange("p b k d -> p (b k d)"), src).then_inc(drained("gates0"), 1)
                for u, step in turns(who):
                    if u == 3:
                        slot(MAIN_SLOTS + step)
                    elif u == 2:
                        mixing(step)
                    else:
                        layer0(step, u)

            def round_ends():
                act.drain().then_inc(S["engines_done"], 1)
                act.wait_ge(go["act"], 1)
                act.sem_clear(go["act"])

            now[0] = FIRST
            between_layers((0, 1))
            round_ends()
            now[0] = LOOP
            with act.Fori(0, PAIRS - 1) as _i:
                recurrence()
                between_layers((0, 1, 2, 3))
                round_ends()
            now[0] = LAST
            recurrence()
            between_layers((2, 3))

        @block.vector
        def _(dve):
            V = nc.vector
            steps = [0]

            def counted(ins, sem):
                steps[0] += 1
                ins.then_inc(sem, 1)
                return steps[0]

            def link0(ins):
                dve.wait_ge(set_step, counted(ins, set_step))

            loaded(dve, "mod")
            dve.wait_ge(act_set, 1)
            V.tensor_tensor(s_sig[:, :, :], cT, s_sig[:, :, :], ALU.mult).then_inc(dve_set, 1)
            link0(V.tensor_tensor(rate[:, :], token_rate, alpha, ALU.add))
            link0(V.tensor_scalar(rate[:, :], rate[:, :], 0.0, -1.0 / HD, ALU.max, ALU.mult))
            V.tensor_scalar(mu_r, mu_r, -1.0, None, ALU.add)
            V.tensor_scalar(mu_k, mu_k, -1.0, None, ALU.add)
            dve.wait_ge(pe_set, 1)
            link0(V.tensor_copy(mod_all[:, :, :].rearrange("p k b -> p (k b)"), bank[2][:, 0:12 * B]))
            of3 = mod_all[:, :, :].rearrange("p (g three) b -> p g three b", three=3)
            V.tensor_scalar(of3[:, :, 1, :], of3[:, :, 1, :], 1.0, None, ALU.add)
            gv, sign, size = of3[:, :, 2, :], s_gate[:, 0, :, :], s_gate[:, 1, :, :]
            V.tensor_scalar(sign, gv, 0.0, 2.0, ALU.is_ge, ALU.mult)
            link0(V.tensor_scalar(size, gv, -1.0, None, ALU.mult))
            link0(V.tensor_tensor(size, size, gv, ALU.max))
            link0(V.tensor_scalar(size, size, 0.25, None, ALU.max))
            link0(V.scalar_tensor_tensor(gv, sign, -1.0, size, ALU.add, ALU.mult))
            loaded(dve, "attn")
            V.tensor_tensor(proj_bd, proj_bd, s_mask, ALU.mult).then_inc(dve_set, 2)
            dve.wait_ge(dve_set, 3)
            dve.wait_ge(pool_set, N_LAYER0_SET)

            def go_on(ins):
                return counted(ins, S["dve_step"])

            def settled(n):
                dve.wait_ge(S["dve_step"], n)

            def link(ins):
                settled(go_on(ins))

            def over(ap, n):
                return ap.unsqueeze(1).broadcast_to([128, n, D])

            def norm_stats(name, u, src):
                l = L[u]
                for t in range(T):
                    n = go_on(V.bn_stats(l["stats"][:, t, :], src[:, t, :]))
                settled(n)
                for t in range(T):
                    last = V.bn_aggr(l["mv"][:, t, :], l["stats"][:, t, :])
                last.then_inc(S[f"{name}_var_{u}"], 1)

            def norm_apply(name, u, src):
                l = L[u]
                dve.wait_ge(S[f"{name}_std_{u}"], 1)
                link(V.reciprocal(l["inv"][:, :], l["std"][:, :]))
                for t in range(T):
                    last = V.tensor_scalar(l["hat"][:, t, :], src[:, t, :], l["mv"][:, t, 0:1], l["inv"][:, t:t + 1],
                                           ALU.subtract, ALU.mult)
                last.then_inc(S[f"{name}_hat_{u}"], 1)

            def add_row(name, u, row):
                src = filled(dve, f"{name}{u}").rearrange("p (t d) -> p t d", t=T)
                V.tensor_tensor(L[u]["y"][:, :, :], src, over(row[:, :], T), ALU.add).then_inc(drained(f"{name}{u}"), 1)
                ready(dve, f"{name}{u}")

            biased = [0, 0]

            def layer0(step, u):
                l = L[u]
                if step == LN1_STATS:
                    dve.wait_ge(x_loaded[u], 16)
                    dve.sem_clear(x_loaded[u])
                    norm_stats("ln1", u, x[:, u, :, :])
                elif step == LN1:
                    norm_apply("ln1", u, x[:, u, :, :])
                elif step == QKV:
                    src = filled(dve, f"v{u}").rearrange("p (t d) -> p t d", t=T)
                    V.tensor_tensor(l["v"][:, :, 0:D], src, over(bc_v0[:, :], T), ALU.add).then_inc(drained(f"v{u}"), 1)
                    ready(dve, "gates0")
                    V.tensor_tensor(gg3[:, u, 0, :], g_ab0[:, u, 0, :], bc_g3[:, :], ALU.mult)
                    link(V.tensor_tensor(gg3[:, u, 1, :], g_ab0[:, u, 0, :], bc_be3[:, :], ALU.mult))
                    go_on(V.tensor_tensor(g_ab0[:, u, 0, :], g_ab0[:, u, 1, :], bc_wo[:, :], ALU.mult))
                elif step == Q_SHIFT:
                    src = filled(dve, f"dq{u}")
                    V.tensor_copy(l["qd"][:, :, :].rearrange("p t h -> p (t h)"), src[:, 0:T * H0]).then_inc(drained(f"dq{u}"), 1)
                    for t in range(T):
                        src = filled(dve, f"xq{u}{t}").rearrange("p (h m) -> p h m", h=H0)
                        link(V.tensor_reduce(l["qmax"][:, t, :], src, AX, ALU.max))
                        if t == 0:
                            ready(dve, f"dq{u}")
                        link(V.tensor_tensor(l["qmax"][:, t, :], l["qmax"][:, t, :], l["qd"][:, t, :], ALU.add))
                        V.tensor_tensor(l["big"][:, t, :].rearrange("p (h m) -> p h m", h=H0), src,
                                        l["qmax"][:, t, :].unsqueeze(2).broadcast_to([128, H0, M]), ALU.subtract)\
                         .then_inc(drained(f"xq{u}{t}"), 1)
                elif step == K_MAX:
                    for t in range(T):
                        ready(dve, f"xk{u}{t}")
                        n = go_on(V.tensor_reduce(l["kmax"][:, t, :], l["ek"][:, t, :].rearrange("p (h m) -> p h m", h=H0), AX, ALU.max))
                    settled(n)
                    V.tensor_reduce(l["kmx"][:, :], l["kmax"][:, :, :].rearrange("p t h -> p h t"), AX, ALU.max).then_inc(S[f"k_max_ready_{u}"], 1)
                elif step == STABLE:
                    src = filled(dve, f"kmT{u}")
                    V.tensor_reduce(l["stab"][:, :], src[0:H0, 0:128], AX, ALU.max).then_inc(drained(f"kmT{u}"), 1)
                    ready(dve, f"kmT{u}")
                    V.tensor_scalar(l["sd"][:, :], ident[0:H0, 0:H0], l["stab"][:, :], None, ALU.mult).then_inc(S[f"k_stab_ready_{u}"], 1)
                elif step == K_SHIFT:
                    src = filled(dve, f"kb{u}")
                    V.tensor_copy(l["kmax"][:, :, :].rearrange("p t h -> p (t h)"), src[:, 0:T * H0]).then_inc(drained(f"kb{u}"), 1)
                    ready(dve, f"kb{u}")
                    for t in range(T):
                        e = l["ek"][:, t, :].rearrange("p (h m) -> p h m", h=H0)
                        V.tensor_tensor(e, e, l["kmax"][:, t, :].unsqueeze(2).broadcast_to([128, H0, M]), ALU.subtract)\
                         .then_inc(S[f"k_shifted_{u}"], 1)
                elif step == Q_FEATURES:
                    for g in range(G):
                        src = filled(dve, f"fq{u}{g}")
                        V.tensor_scalar(l["qf"][:, g, :], src, EPS_K, None, ALU.add).then_inc(drained(f"fq{u}{g}"), 1)
                elif step == K_FEATURES:
                    for t in range(T):
                        dve.wait_ge(S[f"k_exp_{u}"], t + 1)
                        V.tensor_scalar(l["ek"][:, t, :], l["ek"][:, t, :], EPS_K, None, ALU.add).then_inc(S[f"k_feat_ready_{u}"], 1)
                elif step == CONTEXT:
                    loaded(dve, "attn2")
                    for half in range(2):
                        src = filled(dve, f"ctx{u}{half}")
                        for g in (2 * half, 2 * half + 1):
                            o = (g % 2) * 256
                            V.tensor_tensor(l["ctx"][:, g, 0:D], src[:, o:o + D], ctx_mask[:, g, :], ALU.mult)
                            last = V.tensor_scalar(l["ctx"][:, g, D:D + H0], head_sel[:, g, :], src[:, o + D:o + D + 1], None, ALU.mult)
                        last.then_inc(drained(f"ctx{u}{half}"), 1)
                elif step == ATTEND:
                    for half in range(2):
                        src = filled(dve, f"num{u}{half}").rearrange("p (t c) -> p t c", t=2)
                        link(V.reciprocal(l["rden"][:, 2 * half:2 * half + 2, :], src[:, :, D:D + H0]))
                        for t in (2 * half, 2 * half + 1):
                            last = V.tensor_tensor(l["y"][:, t, :].rearrange("p (h d) -> p h d", h=H0),
                                                   src[:, t % 2, 0:D].rearrange("p (h d) -> p h d", h=H0),
                                                   l["rden"][:, t, :].unsqueeze(2).broadcast_to([128, H0, DH]), ALU.mult)
                        last.then_inc(drained(f"num{u}{half}"), 1)
                    biased[u] = go_on(V.tensor_tensor(x[:, u, :, :], x[:, u, :, :], over(gg3[:, u, 1, :], T), ALU.add))
                elif step == PROJECT:
                    add_row("y1", u, bc_o0)
                    norm_stats("ln2", u, l["y"])
                elif step == LN2:
                    norm_apply("ln2", u, l["y"])
                elif step == FF2:
                    add_row("y2", u, bc_b2)
                    norm_stats("ln3", u, l["y"])
                elif step == LN3:
                    dve.wait_ge(S[f"ln3_var_{u}"], 1)
                    for t in range(T):
                        V.scalar_tensor_tensor(l["y"][:, t, :], l["y"][:, t, :], l["mv"][:, t, 0:1], gg3[:, u, 0, :], ALU.subtract, ALU.mult)
                    dve.wait_ge(S[f"ln3_std_{u}"], 1)
                    link(V.reciprocal(l["inv"][:, :], l["std"][:, :]))
                    settled(biased[u])
                    for t in range(T):
                        n = go_on(V.scalar_tensor_tensor(x[:, u, t, :], l["y"][:, t, :], l["inv"][:, t:t + 1], x[:, u, t, :], ALU.mult, ALU.add))
                    settled(n)
                    norm_stats("ln4", u, x[:, u, :, :])
                elif step == LN4:
                    norm_apply("ln4", u, x[:, u, :, :])
                elif step == GATE:
                    loaded(dve, "expert")
                    src = filled(dve, f"gate{u}")[:, 0:T * GA].rearrange("p (t c) -> p t c", t=T)
                    lg, eq, lm = l["lg"][:, :, :], l["eq"][:, :, :], l["lm"]
                    link(V.tensor_tensor(lg, src[:, :, 0:E], bc_gate[:, :].unsqueeze(1).broadcast_to([128, T, E]), ALU.add))
                    link(V.tensor_reduce(lm[:, :], lg, AX, ALU.max))
                    link(V.tensor_tensor(eq, lg, lm[:, :].unsqueeze(2).broadcast_to([128, T, E]), ALU.is_ge))
                    link(V.tensor_tensor(eq, eq, first[:, :].unsqueeze(1).broadcast_to([128, T, E]), ALU.mult))
                    link(V.tensor_reduce(lm[:, :], eq, AX, ALU.max))
                    link(V.tensor_tensor(eq, eq, lm[:, :].unsqueeze(2).broadcast_to([128, T, E]), ALU.is_equal))
                    V.tensor_tensor(l["um"][:, :, :].rearrange("p t (e r) -> p t e r", e=E),
                                    src[:, :, E:E + E * R].rearrange("p t (e r) -> p t e r", e=E),
                                    eq.unsqueeze(3).broadcast_to([128, T, E, R]), ALU.mult).then_inc(drained(f"gate{u}"), 1)
                elif step == EXPERT1:
                    dve.wait_ge(S[f"ln4_hat_{u}"], 1)
                    biased[u] = go_on(V.tensor_tensor(x[:, u, :, :], x[:, u, :, :], over(g_ab0[:, u, 0, :], T), ALU.add))
                elif step == EXPERT2:
                    src = filled(dve, f"y3{u}").rearrange("p (t d) -> p t d", t=T)
                    V.tensor_tensor(l["y"][:, :, :], src, over(g_ab0[:, u, 1, :], T), ALU.mult).then_inc(drained(f"y3{u}"), 1)
                    ready(dve, f"y3{u}")
                    settled(biased[u])
                    V.tensor_tensor(x[:, u, :, :], x[:, u, :, :], l["y"][:, :, :], ALU.add).then_inc(S[f"x_layer0_{u}"], 1)
                    dve.wait_ge(S[f"x_layer0_{u}"], 1)
                    norm_stats("ln5", u, x[:, u, :, :])
                elif step == LN5:
                    norm_apply("ln5", u, x[:, u, :, :])

            kept = [0]

            def heads(ap, half):
                return ap[:, half * HALF:(half + 1) * HALF].rearrange("p (h d) -> p h d", h=HH)

            def per_head(ap):
                return ap.unsqueeze(2).broadcast_to([ap.shape[0], HH, HD])

            def slot(s):
                j, f = divmod(s, 2)
                jq, fq = divmod(s - 1, 2)
                hs = slice(HH * f, HH * (f + 1))
                hq = slice(HH * fq, HH * (fq + 1))
                if j < NJ:
                    dve.wait_ge(S["z_squared"], s + 1)
                    V.tensor_reduce(ssum[:, hs], heads(sq, f), AX, ALU.add).then_inc(S["z_var"], 1)
                if j < NJ:
                    dve.wait_ge(S["z_std"], s + 1)
                    link(V.reciprocal(zinv[:, hs], zstd[:, hs]))
                    V.tensor_tensor(heads(zhat, f), filled(dve, f"z{j}{f}").rearrange("p (h d) -> p h d", h=HH),
                                    per_head(zinv[:, hs]), ALU.mult).then_inc(drained(f"z{j}{f}"), 1)
                    V.tensor_tensor(scl[:, hs], zinv[:, hs], eta[:, j, hs], ALU.mult).then_inc(S["scale_ready"], 1)
                if 1 <= jq <= NJ:
                    dve.wait_ge(S["zq_squared"], s - 2)
                    V.tensor_reduce(qsum[:, hq], heads(sqq, fq), AX, ALU.add).then_inc(S["zq_var"], 1)
                if j < NJ:
                    dve.wait_ge(S["g_hat"], s + 1)
                    dve.wait_ge(S["target_ready"], s + 1)
                    link(V.tensor_tensor(heads(gbase, f), heads(gbase, f), heads(t_tok[:, j % 2, :], f), ALU.add))
                    ready(dve, f"z{j}{f}")
                    prod = go_on(V.tensor_tensor(heads(tmp, f), heads(gbase, f), heads(zhat, f), ALU.mult))
                    link(V.tensor_reduce(c12[:, f, 0, :], heads(gbase, f), AX, ALU.add))
                    mean = go_on(V.tensor_scalar(c12[:, f, 0, :], c12[:, f, 0, :], 1.0 / HD, None, ALU.mult))
                if 1 <= jq <= NJ:
                    dve.wait_ge(S["zq_std"], s - 2)
                    V.reciprocal(qinv[:, hq], qstd[:, hq]).then_inc(S["zq_inv"], 1)
                if j < NJ:
                    settled(prod)
                    link(V.tensor_reduce(c12[:, f, 1, :], heads(tmp, f), AX, ALU.add))
                    link(V.scalar_tensor_tensor(heads(tmp, f), heads(zhat, f), 1.0 / HD, per_head(c12[:, f, 1, :]), ALU.mult, ALU.mult))
                    V.tensor_tensor(heads(gbase, f), heads(gbase, f), heads(tmp, f), ALU.subtract).then_inc(S["grad_base"], 1)
                    settled(mean)
                    dve.wait_ge(S["grad_base"], s + 1)
                    V.tensor_tensor(grad[0:K, hs, 0, :], heads(gbase, f)[0:K], per_head(c12[0:K, f, 0, :]),
                                    ALU.subtract).then_inc(S["grad_top"], 1)

            def recurrence():
                steps[0] = 0
                kept[0] = go_on(V.tensor_copy(mod_mix[:, :, :], mod[:, 9:11, :]))
                dve.wait_ge(pool_set, N_POOL_SET)
                src = filled(dve, "rate")[:, 0:NJ * H].rearrange("p (j h) -> p j h", j=NJ)
                V.tensor_tensor(eta[:, :, :], src, bc_tb[:, :].unsqueeze(1).broadcast_to([128, NJ, H]), ALU.add).then_inc(drained("rate"), 1)
                dve.wait_ge(S["rate_sig"], 1)
                link(V.tensor_scalar(eta[:, :, :], eta[:, :, :], rate[:, :], None, ALU.mult))
                for s in range(MAIN_SLOTS):
                    slot(s)

            def mixing(step):
                if step == MIX_STATS:
                    dve.wait_ge(S["x_ttt"], NJ)
                    for j in range(NJ):
                        n = go_on(V.bn_stats(stats6[:, j, :], xc[:, j, :]))
                    settled(n)
                    for j in range(NJ):
                        last = V.bn_aggr(mv6[:, j, :], stats6[:, j, :])
                    last.then_inc(S["ln6_var"], 1)
                elif step == MIX_NORM:
                    dve.wait_ge(S["ln6_std"], 1)
                    link(V.reciprocal(inv6[:, :], std6[:, :]))
                    for j in range(NJ):
                        last = V.tensor_scalar(hat6[:, j, :], xc[:, j, :], mv6[:, j, 0:1], inv6[:, j:j + 1], ALU.subtract, ALU.mult)
                    last.then_inc(S["ln6_hat"], 1)
                elif step == MIX_SHIFT:
                    for half in range(2):
                        ready(dve, f"h4{half}")
                    V.tensor_tensor(diff[:, :, :, 1:K], h4[:, :, :, 1:K], h4[:, :, :, 0:K - 1], ALU.subtract)
                    V.tensor_tensor(diff[:, 1:NJ, :, 0], h4[:, 1:NJ, :, 0], h4[:, 0:NJ - 1, :, K - 1], ALU.subtract)
                    link(V.tensor_copy(diff[:, 0, :, 0], h4[:, 0, :, 0]))
                    V.scalar_tensor_tensor(mix_k, diff_flat, mu_k[:, :], h4_flat, ALU.mult, ALU.add).then_inc(S["mix_ready"], 1)
                    V.scalar_tensor_tensor(mix_r, diff_flat, mu_r[:, :], h4_flat, ALU.mult, ALU.add).then_inc(S["mix_ready"], 1)
                elif step == MIX_OUT:
                    dve.wait_ge(S["mix_ready"], 2)
                    for half in range(2):
                        ready(dve, f"r{half}")
                        o = diff_flat[:, half * 512:(half + 1) * 512]
                        V.tensor_tensor(o, filled(dve, f"val{half}"), r_sb[:, half * 512:(half + 1) * 512], ALU.mult).then_inc(drained(f"val{half}"), 1)
                        ready(dve, f"val{half}")
                        o3 = o.rearrange("p (j d) -> p j d", j=4)
                        link(V.tensor_tensor(o3, o3, over(g_ab1[:, 1, :], 4), ALU.mult))
                        V.tensor_tensor(xc[:, 4 * half:4 * half + 4, :], xc[:, 4 * half:4 * half + 4, :], o3, ALU.add).then_inc(S["x_final"], 1)

            def between_layers(who, pair=0):
                if 0 in who:
                    if now[0] == LOOP:
                        ready(dve, "gates1")
                        settled(kept[0])
                    V.tensor_copy(mod[:, :, :], mod_all[:, :, bass.ds(2 * pair, 2)]).then_inc(S["mods_ready"], 1)
                for u, step in turns(who):
                    if u == 3:
                        slot(MAIN_SLOTS + step)
                    elif u == 2:
                        mixing(step)
                    else:
                        layer0(step, u)

            def round_ends():
                dve.drain().then_inc(S["engines_done"], 1)
                dve.wait_ge(go["dve"], 1)
                dve.sem_clear(go["dve"])

            now[0] = FIRST
            steps[0] = 0
            between_layers((0, 1))
            round_ends()
            now[0] = LOOP
            with dve.Fori(0, PAIRS - 1) as i:
                recurrence()
                between_layers((0, 1, 2, 3), i + 1)
                round_ends()
            now[0] = LAST
            recurrence()
            between_layers((2, 3))

        @block.sync
        def _(sp):
            def load(name):
                for dst, src in loads[name]:
                    sp.dma_start(dst, src).then_inc(loaded_sem[name], 16)

            def load_x(pair):
                for u in range(2):
                    sp.dma_start(x[:, u, :, :], x_dram[bass.ds(2 * pair + u, 1), :, :, :].rearrange("b p t d -> (b p) t d")).then_inc(x_loaded[u], 16)

            load("mod")
            for u in range(2):
                sp.dma_start(x[:, u, :, :], x_dram[u, :, :, :]).then_inc(x_loaded[u], 16)
            for name in loads:
                if name != "mod":
                    load(name)
            sp.sem_inc(out_stored, 32)

            def round_ends():
                sp.drain().then_inc(S["engines_done"], 1)
                sp.wait_ge(go["sp"], 1)
                sp.sem_clear(go["sp"])

            def move_x():
                sp.wait_ge(out_stored, 32)
                sp.sem_clear(out_stored)
                for b in range(2):
                    for odd in range(2):
                        sp.dma_start(xc[64 * b:64 * b + 64, :, :].rearrange("p (t o) d -> p t o d", o=2)[:, :, odd, :],
                                     x[64 * odd:64 * odd + 64, b, :, :]).then_inc(S["x_moved"], 16)
                sp.wait_ge(S["x_moved"], 64)

            def store(pair):
                sp.wait_ge(S["x_final"], 2)
                for b in range(2):
                    sp.dma_start(out_dram[bass.ds(2 * pair + b, 1), :, :, :].rearrange("b t j d -> (b t) j d"),
                                 xc[64 * b:64 * b + 64, :, :]).then_inc(out_stored, 16)

            round_ends()
            with sp.Fori(0, PAIRS - 1) as i:
                move_x()
                load_x(i + 1)
                store(i)
                round_ends()
            move_x()
            store(PAIRS - 1)
            sp.wait_ge(out_stored, 32)

        @block.gpsimd
        def _(pool):
            P = nc.gpsimd
            done = [0]

            def then(ins):
                done[0] += 1
                ins.then_inc(pool_set, 1)
                pool.wait_ge(pool_set, done[0])

            for t in (ones[:, :], L[0]["v"][:, :, D:D + 1], L[1]["v"][:, :, D:D + 1]):
                then(P.memset(t, 1.0))
            for t in (L[0]["umT"][:, :], L[1]["umT"][:, :]):
                then(P.memset(t, 0.0))
            loaded(pool, "attn")
            then(P.tensor_copy(ident_bf[:, :], ident))
            loaded(pool, "compose")
            loaded(pool, "ttt")
            tt = P.tensor_tensor
            then(tt(w_t1[:, :], w_k1, s_wv, ALU.subtract))
            then(tt(w_t1[:, :], w_t1[:, :], s_gam, ALU.mult))
            then(tt(gamma2[:, :], s_gam, s_gam, ALU.mult))
            then(tt(gam_bet[:, :], s_gam, s_bet, ALU.mult))
            then(tt(s_the, s_the, w_k1, ALU.mult))
            th = s_the.rearrange("p (h d) -> p h d", h=H)
            w = HD // 2
            while w > 1:
                then(tt(th[:, :, 0:w], th[:, :, 0:w], th[:, :, w:2 * w], ALU.add))
                w //= 2
            then(tt(w_theta[:, 0:H].unsqueeze(2), th[:, :, 0:1], th[:, :, 1:2], ALU.add))
            w = HD // 2
            then(tt(s_sum, s_w0[:, :, 0:w], s_w0[:, :, w:2 * w], ALU.add))
            while w > 2:
                w //= 2
                then(tt(s_sum[:, :, 0:w], s_sum[:, :, 0:w], s_sum[:, :, w:2 * w], ALU.add))
            then(tt(s_mean[:, :].unsqueeze(2), s_sum[:, :, 0:1], s_sum[:, :, 1:2], ALU.add))
            then(P.tensor_scalar(s_mean[:, :], s_mean[:, :], 1.0 / HD, None, ALU.mult))
            then(tt(s_w0, s_w0, s_mean[:, :].unsqueeze(2).broadcast_to([C, H, HD]), ALU.subtract))
            for part in range(3):
                then(P.tensor_copy(w_parts[:, part, :, :], s_w0))
                if part < 2:
                    then(tt(s_w0, s_w0, w_parts[:, part, :, :], ALU.subtract))
            then(tt(g_wo[:, :, :], s_wo, gammaT.unsqueeze(2).broadcast_to([128, HP, D]), ALU.mult))
            then(P.memset(kT1[HD:C, :, :], 1.0))
            then(P.memset(qT1[HD:C, :, :], 1.0))
            pool.wait_ge(pe_set, 1)
            then(P.memset(grad[:, :, :, :], 0.0))
            assert done[0] == N_POOL_SET, done
            def heads(ap, f):
                return ap[:, f * HALF:(f + 1) * HALF].rearrange("p (h d) -> p h d", h=HH)

            def target(j, f):
                ready(pool, f"t1_{j}{f}")
                t = t_tok[:, j % 2, f * HALF:(f + 1) * HALF]
                P.tensor_tensor(t, t, gam_bet[:, f * HALF:(f + 1) * HALF], ALU.add).then_inc(S["target_ready"], 1)

            def recurrence():
                for s in range(MAIN_SLOTS + TAIL_SLOTS):
                    j, f = divmod(s, 2)
                    jq, fq = divmod(s - 1, 2)
                    jx, fx = divmod(s - 3, 2)
                    hs = slice(HH * f, HH * (f + 1))
                    if j < NJ:
                        if s:
                            pool.wait_ge(S["grad_bot"], s)
                        ready(pool, f"z{j}{f}")
                        P.tensor_tensor(heads(gbase, f), heads(zhat, f), heads(gamma2, f), ALU.mult).then_inc(S["g_hat"], 1)
                        if s == 0:
                            target(0, 0)
                        ready(pool, f"k1_{j}{f}")
                        pool.wait_ge(S["scale_ready"], s + 1)
                        P.tensor_tensor(k_sc[:, hs, 0:HD], heads(k_tok[:, j % 2, :], f), scl[:, hs].unsqueeze(2).broadcast_to([128, HH, HD]), ALU.mult)
                        P.tensor_copy(k_sc[:, hs, HD:C], scl[:, hs].unsqueeze(2)).then_inc(S["k_scaled"], 1)
                        pool.wait_ge(S["k_scaled"], s + 1)
                        if s == 0:
                            target(0, 1)
                        if j + 1 < NJ:
                            target(j + 1, f)
                    if 1 <= jq <= NJ:
                        if j >= NJ and s <= 2 * NJ:
                            pool.wait_ge(S["grad_bot"], s)
                        ready(pool, f"zq{jq - 1}{fq}")
                        pool.wait_ge(S["zq_inv"], s - 2)
                        P.tensor_tensor(heads(zq_hat, fq), heads(zq_hat, fq),
                                        qinv[:, HH * fq:HH * (fq + 1)].unsqueeze(2).broadcast_to([128, HH, HD]), ALU.mult).then_inc(S["zq_ready"], 1)
                    if 1 <= jx <= NJ and fx == 1:
                        if s <= 2 * NJ:
                            pool.wait_ge(S["grad_bot"], s)
                        ready(pool, f"o{jx - 1}")
                        at = att1[:, jx % 2, :]
                        P.tensor_tensor(at, at, bc_out1[:, :], ALU.add).then_inc(S["att_step"], 1)
                        pool.wait_ge(S["att_step"], 2 * jx - 1)
                        P.tensor_tensor(at, at, g_ab1[:, 0, :], ALU.mult).then_inc(S["att_step"], 1)
                        pool.wait_ge(S["att_step"], 2 * jx)
                        if jx == 1:
                            pool.wait_ge(S["x_moved"], 64)
                        P.tensor_tensor(xc[:, jx - 1, :], xc[:, jx - 1, :], at, ALU.add).then_inc(S["x_ttt"], 1)
                        pool.wait_ge(S["x_ttt"], jx)
                    if j < NJ:
                        if j + 1 < NJ:
                            pool.wait_ge(S["target_ready"], s + 3)
                        if jq >= 1:
                            pool.wait_ge(S["zq_ready"], s - 2)
                        pool.wait_ge(S["grad_base"], s + 1)
                        P.tensor_tensor(grad[K:128, hs, 1, :], heads(gbase, f)[K:128],
                                        c12[K:128, f, 0, :].unsqueeze(2).broadcast_to([K, HH, HD]), ALU.subtract).then_inc(S["grad_bot"], 1)

            def round_ends():
                pool.drain().then_inc(S["engines_done"], 1)
                pool.wait_ge(S["engines_done"], 5)
                pool.sem_clear(range(numbers[0], numbers[-1] + 1))
                for sem in go.values():
                    pool.sem_inc(sem, 1)

            now[0] = FIRST
            round_ends()
            now[0] = LOOP
            with pool.Fori(0, PAIRS - 1) as _i:
                recurrence()
                round_ends()
            now[0] = LAST
            recurrence()


def laid_out(i):
    v = {n: np.asarray(x) for n, x in i.items()}
    col = lambda n: v[n].reshape(-1, 128).T
    row = lambda n: v[n].reshape(1, -1)
    by_group = lambda m: m.reshape(-1, 128, D).transpose(1, 0, 2).reshape(128, -1)
    lora_b = np.zeros((128, FF), np.float32)
    lora_b[:E * R] = v["L0_ffn_lora_B"].transpose(0, 2, 1).reshape(E * R, FF)
    gate_a = np.concatenate([v["L0_ffn_gate_W"], v["L0_ffn_lora_A"].reshape(E * R, D)]).T
    const = shape_constants()
    parts = {
        "cols": dict(c0=v["L0_c"].T, c1=v["L1_c"].T, bq=col("L0_attn_bq"), bk=col("L0_attn_bk"), g2=col("L0_attn_g2"), be2=col("L0_attn_be2"),
                     mu_r=col("L1_ffn_mu_r"), mu_k=col("L1_ffn_mu_k"), alpha=np.tile(v["L1_attn_alpha"], 2)[:, None],
                     token_rate=const["token_rate"], b1=col("L0_attn_b1"), bi=col("L0_ffn_wi_b"), beta=col("L1_attn_beta"), gamma=col("L1_attn_gamma")),
        "wmod": dict(wmod0=v["L0_wmod"], wmod1=v["L1_wmod"]),
        "compose": dict(wqT=by_group(v["L1_attn_wq"].T), wo=by_group(v["L1_attn_wo"])),
        "attn": dict(ident=const["ident"], wq=v["L0_attn_Wq"].T, wk=v["L0_attn_Wk"].T, wv=v["L0_attn_Wv"].T, half_square=const["half_square"],
                     proj=np.tile(v["L0_attn_proj"].T, (H0, H0))),
        "attn2": dict(ctx_mask=const["ctx_mask"], head_sel=const["head_sel"], wo0=v["L0_attn_Wo"].T,
                      w1=v["L0_attn_W1"].T, w2=by_group(v["L0_attn_W2"].T)),
        "expert": dict(gate_a=gate_a, wi=v["L0_ffn_wi_W"].T, wof=by_group(v["L0_ffn_wo_W"].T), lora_b=lora_b, first=const["first"]),
        "ttt": dict(wk1=v["L1_attn_wk"], wq1=v["L1_attn_wq"], w_r=v["L1_ffn_W_r"].T, w_kf=v["L1_ffn_W_k"].T, w_vf=v["L1_ffn_W_v"].T),
        "rows": dict(bv=row("L0_attn_bv"), bo=row("L0_attn_bo"), b2=row("L0_attn_b2"), g3=row("L0_attn_g3"), be3=row("L0_attn_be3"),
                     wo_b=row("L0_ffn_wo_b"), gate_b=row("L0_ffn_gate_b"), theta_bias=row("L1_attn_theta_bias")),
        "gam_bet_rows": dict(gamma=row("L1_attn_gamma"), beta=row("L1_attn_beta")),
    }
    arrays = {n: np.ascontiguousarray(np.concatenate([parts[n][k] for k, _ in spec], axis=1)) for n, spec in PACKS.items()}
    x = np.ascontiguousarray(v["L0_attn_video"].reshape(B, T, 128, D))
    w0 = np.concatenate([v["L1_attn_W1"].transpose(1, 0, 2).reshape(HD, HW), row("L1_attn_b1")])
    return {**arrays, "x": x, "c_proj_mask": const["proj_mask"], "wv1": np.ascontiguousarray(v["L1_attn_wv"]), "theta": row("L1_attn_theta"), "w0": w0}


def kernel(**inputs):
    import concourse.bacc as bacc
    from concourse.bass_utils import run_bass_kernel_spmd

    arrays = laid_out(inputs)
    nc = bacc.Bacc("TRN2", target_bir_lowering=False, num_devices=1)
    aps = {n: nc.dram_tensor(f"in_{n}", v.shape, mybir.dt.from_np(v.dtype), kind="ExternalInput").ap() for n, v in arrays.items()}
    out = nc.dram_tensor("out_x", (B, N, D), F32, kind="ExternalOutput").ap()
    build(nc, aps, out)
    r = run_bass_kernel_spmd(nc, [{f"in_{n}": v for n, v in arrays.items()}], core_ids=[0])
    return r.results[0]["out_x"]
```
